# Optimizing a Trainium2 kernel written in Bass

```python
import numpy as np
import jax
import jax.numpy as jnp

def _softmax(x, axis=-1):
    return jax.nn.softmax(x, axis=axis)

def _gelu(x):
    return jax.nn.gelu(x, approximate=True)

def _silu(x):
    return jax.nn.silu(x)

def _sigmoid(x):
    return jax.nn.sigmoid(x)

def _layernorm(x, axis=-1, eps=1e-05):
    m = jnp.mean(x, axis=axis, keepdims=True)
    v = jnp.var(x, axis=axis, keepdims=True)
    return (x - m) / jnp.sqrt(v + eps)

def _scatter_add(tgt, idx, src, axis=0):
    return tgt.at[idx].add(src)

def _segment_sum(src, seg, n):
    return jax.ops.segment_sum(src, seg, n)
kernel_name = 'mk_flamingo_gated_d4_seqx_r8_9e8736'

def setup_inputs(seed: int=0):
    np.random.seed(seed)
    _w = jnp.asarray

    def _rec_inputs():
        import jax
        import jax.numpy as jnp
        _rk = jax.random.key(seed)
        x = -0.0003929 + 0.9999 * jax.random.normal(jax.random.fold_in(_rk, 1), (16, 64, 128), jnp.float32)
        _lenS = 64 - jax.random.randint(jax.random.fold_in(_rk, 7), (16,), 0, max(1, 64 // 4) + 1, jnp.int32)
        _lenS2 = 64 - jax.random.randint(jax.random.fold_in(_rk, 8), (16,), 0, max(1, 64 // 4) + 1, jnp.int32)
        _ctx_1024P = jax.random.normal(jax.random.fold_in(_rk, 11), (16, 16, 128), jnp.float32)
        _ctx_1024c = jax.random.dirichlet(jax.random.fold_in(_rk, 511), 0.3 * jnp.ones((16,), jnp.float32), (16, 64))
        _ctx_1024t = jnp.einsum('bsk,bkd->bsd', _ctx_1024c, _ctx_1024P)
        _ctx_1024t = _ctx_1024t * jax.lax.rsqrt(jnp.mean(jnp.square(_ctx_1024t)) + 1e-12) * 0.953939
        ctx_1024 = 2.81802e-05 + 1.00001 * (_ctx_1024t + 0.3 * jax.random.normal(jax.random.fold_in(_rk, 611), (16, 64, 128), jnp.float32))
        itok_BxS_8_8191 = jax.random.randint(jax.random.fold_in(_rk, 12), (16, 64), 8, 1024, jnp.int32)
        itok_BxS2_1_8191 = jax.random.randint(jax.random.fold_in(_rk, 13), (16, 64), 1, 1024, jnp.int32)
        _validS = jnp.arange(64)[None, :] < _lenS[:, None]
        _validS2 = jnp.arange(64)[None, :] < _lenS2[:, None]
        _causal = jnp.tril(jnp.ones((64, 64), dtype=bool))
        mask_BxSxS2_if1 = jnp.where(jnp.ones((16, 64, 64), dtype=bool), 1, 0).astype(jnp.int32)
        mask_BxS2_bk0 = jnp.logical_not(jnp.broadcast_to(_validS2[:, :], (16, 64)))
        _g = jax.random.normal(jax.random.fold_in(_rk, 9001), (2, 4), jnp.float32)
        _g = jnp.sign(_g) * jnp.maximum(jnp.abs(_g), 1.0) + (_g == 0) * 1.0
        g_xattn = _g[0]
        g_ffn = _g[1]
        return (x, ctx_1024, itok_BxS_8_8191, itok_BxS2_1_8191, mask_BxSxS2_if1, mask_BxS2_bk0, g_xattn, g_ffn)
    x, ctx_1024, itok_BxS_8_8191, itok_BxS2_1_8191, mask_BxSxS2_if1, mask_BxS2_bk0, g_xattn, g_ffn = _rec_inputs()

    def _L0_xattn_setup():
        import jax, jax.numpy as jnp
        import numpy as np
        D1, D2, D3 = (128, 128, 128)
        key = jax.random.key(seed)
        k1, k2, kw, kb = jax.random.split(key, 4)
        x1 = jax.random.normal(k1, (8, 256, D1), dtype=jnp.float32)
        x2 = jax.random.normal(k2, (8, 256, D2), dtype=jnp.float32)
        bound = 1.0 / np.sqrt(D1 + D2)
        W = jax.random.uniform(kw, (D3, D1 + D2), minval=-bound, maxval=bound, dtype=jnp.float32)
        b = jax.random.uniform(kb, (D3,), minval=-bound, maxval=bound, dtype=jnp.float32)
        return {'x1': x1, 'x2': x2, 'W': W, 'b': b}
    _L0_xattn_all = _L0_xattn_setup()
    _L0_xattn_in = {k: v for k, v in _L0_xattn_all.items() if k in ('W', 'b')}
    del _L0_xattn_all

    def _L0_ffn_setup():
        import jax, jax.numpy as jnp
        import numpy as np
        H = 8
        QD = 32
        HALF = QD // 2
        DIMS = (32, 32)
        TOPK = 16
        DTK = 4
        EPS_BN = 1e-05
        EPS_NORM = 1e-12

        def _l2norm(x):
            n = jnp.linalg.norm(x, axis=-1, keepdims=True)
            return x / jnp.maximum(n, EPS_NORM)
        key = jax.random.key(seed)
        ks = jax.random.split(key, 6)
        B, S, D, O, E = (2, 64, 128, 128, 128)
        hidden_states = jax.random.normal(ks[0], (B, S, D), jnp.float32)
        Wq = jax.random.normal(ks[1], (D, H * QD), jnp.float32) * 0.02
        bq = jnp.zeros((H * QD,), jnp.float32)
        bn_gamma = jnp.ones((QD,), jnp.float32)
        bn_beta = jnp.zeros((QD,), jnp.float32)
        sub_key0 = jax.random.normal(ks[2], (DIMS[0], HALF), jnp.float32) * 0.02
        sub_key1 = jax.random.normal(ks[3], (DIMS[1], HALF), jnp.float32) * 0.02
        expert_down = jax.random.normal(ks[4], (E, D), jnp.float32) * 0.02
        expert_up = jax.random.normal(ks[5], (E, O), jnp.float32) * 0.02
        return {'hidden_states': hidden_states, 'Wq': Wq, 'bq': bq, 'bn_gamma': bn_gamma, 'bn_beta': bn_beta, 'sub_key0': sub_key0, 'sub_key1': sub_key1, 'expert_down': expert_down, 'expert_up': expert_up}
    _L0_ffn_all = _L0_ffn_setup()
    _L0_ffn_in = {k: v for k, v in _L0_ffn_all.items() if k in ('Wq', 'bq', 'bn_gamma', 'bn_beta', 'sub_key0', 'sub_key1', 'expert_down', 'expert_up')}
    del _L0_ffn_all

    def _L1_xattn_setup():
        import jax, jax.numpy as jnp
        import numpy as np
        DIM = 128
        NUM_HEADS = 16
        HEAD_DIM = DIM // NUM_HEADS

        def _slopes(num_heads):
            ratio = 2.0 ** (-8.0 / num_heads)
            return jnp.asarray([ratio ** i for i in range(1, num_heads + 1)], dtype=jnp.float32)
        key = jax.random.key(seed)
        ks = jax.random.split(key, 10)
        b, q_len, k_len = (2, 256, 512)
        query = jax.random.normal(ks[0], (b, q_len, DIM), dtype=jnp.float32)
        keys = jax.random.normal(ks[1], (b, k_len, DIM), dtype=jnp.float32)
        values = jax.random.normal(ks[2], (b, k_len, DIM), dtype=jnp.float32)
        query_pos = jnp.sort(jax.random.randint(ks[3], (b, q_len), 0, 1024), axis=-1)
        key_pos = jnp.sort(jax.random.randint(ks[4], (b, k_len), 0, 1024), axis=-1)
        mask = jnp.ones((b, q_len, k_len), dtype=jnp.int32)
        lim = float(np.sqrt(6.0 / (DIM + DIM)))
        W_q = jax.random.uniform(ks[5], (DIM, DIM), minval=-lim, maxval=lim, dtype=jnp.float32)
        W_k = jax.random.uniform(ks[6], (DIM, DIM), minval=-lim, maxval=lim, dtype=jnp.float32)
        W_v = jax.random.uniform(ks[7], (DIM, DIM), minval=-lim, maxval=lim, dtype=jnp.float32)
        W_o = jax.random.uniform(ks[8], (DIM, DIM), minval=-lim, maxval=lim, dtype=jnp.float32)
        return {'query': query, 'keys': keys, 'values': values, 'W_q': W_q, 'W_k': W_k, 'W_v': W_v, 'W_o': W_o, 'query_pos': query_pos, 'key_pos': key_pos, 'mask': mask}
    _L1_xattn_all = _L1_xattn_setup()
    _L1_xattn_in = {k: v for k, v in _L1_xattn_all.items() if k in ('W_q', 'W_k', 'W_v', 'W_o')}
    del _L1_xattn_all

    def _L1_ffn_setup():
        import jax, jax.numpy as jnp
        import numpy as np
        H = 16
        TOP_K = 2
        LN_EPS = 1e-05
        key = jax.random.key(seed)
        ks = jax.random.split(key, 8)
        B, S, E, NE = (2, 128, 128, 8)
        w = lambda k, shp: jax.random.normal(k, shp, dtype=jnp.float32) * 0.02
        return {'x': jax.random.normal(ks[0], (B, S, E), dtype=jnp.float32), 'rW1': w(ks[1], (E // 2, E)), 'rb1': jnp.zeros((E // 2,), jnp.float32), 'ln_g': jnp.ones((E // 2,), jnp.float32), 'ln_b': jnp.zeros((E // 2,), jnp.float32), 'rW2': w(ks[2], (NE, E // 2)), 'rb2': jnp.zeros((NE,), jnp.float32), 'qW': w(ks[3], (NE, E, E)), 'qb': jnp.zeros((NE, E), jnp.float32), 'kW': w(ks[4], (NE, E, E)), 'kb': jnp.zeros((NE, E), jnp.float32), 'vW': w(ks[5], (NE, E, E)), 'vb': jnp.zeros((NE, E), jnp.float32), 'oW': w(ks[6], (NE, E, E)), 'ob': jnp.zeros((NE, E), jnp.float32)}
    _L1_ffn_all = _L1_ffn_setup()
    _L1_ffn_in = {k: v for k, v in _L1_ffn_all.items() if k in ('rW1', 'rb1', 'ln_g', 'ln_b', 'rW2', 'rb2', 'qW', 'qb', 'kW', 'kb', 'vW', 'vb', 'oW', 'ob')}
    del _L1_ffn_all

    def _L2_xattn_setup():
        import jax, jax.numpy as jnp
        import numpy as np
        DIM = 128
        NUM_HEADS = 16
        HEAD_DIM = DIM // NUM_HEADS
        ROPE_BASE = 10000.0
        SCALE = 1.0 / np.sqrt(HEAD_DIM)

        def _rotate_half(x):
            x1, x2 = jnp.split(x, 2, axis=-1)
            return jnp.concatenate([-x2, x1], axis=-1)

        def _rope(x, seq_len):
            inv_freq = 1.0 / ROPE_BASE ** (jnp.arange(0, HEAD_DIM, 2, dtype=jnp.float32) / HEAD_DIM)
            t = jnp.arange(seq_len, dtype=jnp.float32)
            freqs = jnp.outer(t, inv_freq)
            emb = jnp.concatenate([freqs, freqs], -1)
            cos = jnp.cos(emb)[None, None]
            sin = jnp.sin(emb)[None, None]
            return x * cos + _rotate_half(x) * sin
        key = jax.random.key(seed)
        ks = jax.random.split(key, 6)
        B, T_q, T_k = (4, 128, 512)
        s = 1.0 / np.sqrt(DIM)
        return {'x_query': jax.random.normal(ks[0], (B, T_q, DIM), jnp.float32), 'x_kv': jax.random.normal(ks[1], (B, T_k, DIM), jnp.float32), 'Wq': jax.random.normal(ks[2], (DIM, DIM), jnp.float32) * s, 'Wk': jax.random.normal(ks[3], (DIM, DIM), jnp.float32) * s, 'Wv': jax.random.normal(ks[4], (DIM, DIM), jnp.float32) * s, 'Wo': jax.random.normal(ks[5], (DIM, DIM), jnp.float32) * s}
    _L2_xattn_all = _L2_xattn_setup()
    _L2_xattn_in = {k: v for k, v in _L2_xattn_all.items() if k in ('Wq', 'Wk', 'Wv', 'Wo')}
    del _L2_xattn_all

    def _L2_ffn_setup():
        import jax, jax.numpy as jnp
        import numpy as np
        DIM = 128
        HID = 64
        N_EXPERTS = 16
        TOP_K = 4
        key = jax.random.key(seed)
        ks = jax.random.split(key, 8)
        s = 0.02
        x = jax.random.normal(ks[0], (2, 128, DIM), dtype=jnp.float32)
        gate_w = jax.random.normal(ks[1], (N_EXPERTS, DIM), dtype=jnp.float32) * s
        w1 = jax.random.normal(ks[2], (N_EXPERTS, HID, DIM), dtype=jnp.float32) * s
        w3 = jax.random.normal(ks[3], (N_EXPERTS, HID, DIM), dtype=jnp.float32) * s
        w2 = jax.random.normal(ks[4], (N_EXPERTS, DIM, HID), dtype=jnp.float32) * s
        sw1 = jax.random.normal(ks[5], (HID, DIM), dtype=jnp.float32) * s
        sw3 = jax.random.normal(ks[6], (HID, DIM), dtype=jnp.float32) * s
        sw2 = jax.random.normal(ks[7], (DIM, HID), dtype=jnp.float32) * s
        return {'x': x, 'gate_w': gate_w, 'w1': w1, 'w3': w3, 'w2': w2, 'sw1': sw1, 'sw3': sw3, 'sw2': sw2}
    _L2_ffn_all = _L2_ffn_setup()
    _L2_ffn_in = {k: v for k, v in _L2_ffn_all.items() if k in ('gate_w', 'w1', 'w3', 'w2', 'sw1', 'sw3', 'sw2')}
    del _L2_ffn_all

    def _L3_xattn_setup():
        import jax, jax.numpy as jnp
        import numpy as np
        DIM = 128
        DIM_LATENT = 128
        DIM_HEAD = 64
        INNER = max(DIM, DIM_LATENT)
        HEADS = INNER // DIM_HEAD
        SCALE = DIM_HEAD ** (-0.5)
        LN_EPS = 1e-05
        RMS_EPS = 1e-08

        def layernorm(x, g, b):
            mu = jnp.mean(x, axis=-1, keepdims=True)
            var = jnp.mean(jnp.square(x - mu), axis=-1, keepdims=True)
            return (x - mu) * jax.lax.rsqrt(var + LN_EPS) * g + b

        def rmsnorm(x, gamma):
            n = jnp.linalg.norm(x, axis=-1, keepdims=True) * x.shape[-1] ** (-0.5)
            return x / jnp.maximum(n, RMS_EPS) * gamma
        key = jax.random.key(seed)
        ks = jax.random.split(key, 8)
        b, n, nl = (8, 256, 64)
        x = jax.random.normal(ks[0], (b, n, DIM), dtype=jnp.float32)
        latents = jax.random.normal(ks[1], (b, nl, DIM_LATENT), dtype=jnp.float32)
        mask = jax.random.randint(ks[2], (b, n), 0, 2).astype(bool)
        init = lambda k, shape, fan_in: jax.random.normal(k, shape, jnp.float32) * fan_in ** (-0.5)
        return {'x': x, 'latents': latents, 'mask': mask, 'ln_x_g': jnp.ones((DIM,), jnp.float32), 'ln_x_b': jnp.zeros((DIM,), jnp.float32), 'ln_l_g': jnp.ones((DIM_LATENT,), jnp.float32), 'ln_l_b': jnp.zeros((DIM_LATENT,), jnp.float32), 'q_gamma': jnp.ones((DIM_HEAD,), jnp.float32), 'k_gamma': jnp.ones((DIM_HEAD,), jnp.float32), 'W_q': init(ks[3], (DIM_LATENT, INNER), DIM_LATENT), 'W_kv': init(ks[4], (DIM, 2 * INNER), DIM), 'W_out': init(ks[5], (INNER, DIM_LATENT), INNER), 'b_out': jnp.zeros((DIM_LATENT,), jnp.float32)}
    _L3_xattn_all = _L3_xattn_setup()
    _L3_xattn_in = {k: v for k, v in _L3_xattn_all.items() if k in ('ln_x_g', 'ln_x_b', 'ln_l_g', 'ln_l_b', 'q_gamma', 'k_gamma', 'W_q', 'W_kv', 'W_out', 'b_out')}
    del _L3_xattn_all

    def _L3_ffn_setup():
        import jax, jax.numpy as jnp
        import numpy as np

        def _bitlinear(x, w_latent):
            scale = jax.lax.stop_gradient(jnp.clip(jnp.mean(jnp.abs(w_latent), axis=1, keepdims=True), 1e-05, None))
            tern = jnp.clip(jnp.round(w_latent / scale), -1.0, 1.0)
            w = w_latent + jax.lax.stop_gradient(tern - w_latent)
            return x @ (w * scale).T
        key = jax.random.key(seed)
        ks = jax.random.split(key, 6)
        dim, hidden, rank = (128, 512, 16)
        B, S = (4, 512)
        x = jax.random.normal(ks[0], (B, S, dim), dtype=jnp.float32)
        w_fc = 0.02 * jax.random.normal(ks[1], (hidden, dim), dtype=jnp.float32)
        w_proj = 0.02 * jax.random.normal(ks[2], (dim, hidden), dtype=jnp.float32)
        u = 0.02 * jax.random.normal(ks[3], (hidden, rank), dtype=jnp.float32)
        v = 0.02 * jax.random.normal(ks[4], (rank, dim), dtype=jnp.float32)
        fast_b = jax.random.normal(ks[5], (rank, rank), dtype=jnp.float32)
        gate = jnp.float32(0.05)
        return {'x': x, 'fast_b': fast_b, 'w_fc': w_fc, 'w_proj': w_proj, 'u': u, 'v': v, 'gate': gate}
    _L3_ffn_all = _L3_ffn_setup()
    _L3_ffn_in = {k: v for k, v in _L3_ffn_all.items() if k in ('fast_b', 'w_fc', 'w_proj', 'u', 'v', 'gate')}
    del _L3_ffn_all
    return {'x': x, 'ctx_1024': ctx_1024, 'itok_BxS_8_8191': itok_BxS_8_8191, 'itok_BxS2_1_8191': itok_BxS2_1_8191, 'mask_BxSxS2_if1': mask_BxSxS2_if1, 'mask_BxS2_bk0': mask_BxS2_bk0, 'g_xattn': g_xattn, 'g_ffn': g_ffn, 'L0_xattn_W': _L0_xattn_in['W'], 'L0_xattn_b': _L0_xattn_in['b'], 'L0_ffn_Wq': _L0_ffn_in['Wq'], 'L0_ffn_bq': _L0_ffn_in['bq'], 'L0_ffn_bn_gamma': _L0_ffn_in['bn_gamma'], 'L0_ffn_bn_beta': _L0_ffn_in['bn_beta'], 'L0_ffn_sub_key0': _L0_ffn_in['sub_key0'], 'L0_ffn_sub_key1': _L0_ffn_in['sub_key1'], 'L0_ffn_expert_down': _L0_ffn_in['expert_down'], 'L0_ffn_expert_up': _L0_ffn_in['expert_up'], 'L1_xattn_W_q': _L1_xattn_in['W_q'], 'L1_xattn_W_k': _L1_xattn_in['W_k'], 'L1_xattn_W_v': _L1_xattn_in['W_v'], 'L1_xattn_W_o': _L1_xattn_in['W_o'], 'L1_ffn_rW1': _L1_ffn_in['rW1'], 'L1_ffn_rb1': _L1_ffn_in['rb1'], 'L1_ffn_ln_g': _L1_ffn_in['ln_g'], 'L1_ffn_ln_b': _L1_ffn_in['ln_b'], 'L1_ffn_rW2': _L1_ffn_in['rW2'], 'L1_ffn_rb2': _L1_ffn_in['rb2'], 'L1_ffn_qW': _L1_ffn_in['qW'], 'L1_ffn_qb': _L1_ffn_in['qb'], 'L1_ffn_kW': _L1_ffn_in['kW'], 'L1_ffn_kb': _L1_ffn_in['kb'], 'L1_ffn_vW': _L1_ffn_in['vW'], 'L1_ffn_vb': _L1_ffn_in['vb'], 'L1_ffn_oW': _L1_ffn_in['oW'], 'L1_ffn_ob': _L1_ffn_in['ob'], 'L2_xattn_Wq': _L2_xattn_in['Wq'], 'L2_xattn_Wk': _L2_xattn_in['Wk'], 'L2_xattn_Wv': _L2_xattn_in['Wv'], 'L2_xattn_Wo': _L2_xattn_in['Wo'], 'L2_ffn_gate_w': _L2_ffn_in['gate_w'], 'L2_ffn_w1': _L2_ffn_in['w1'], 'L2_ffn_w3': _L2_ffn_in['w3'], 'L2_ffn_w2': _L2_ffn_in['w2'], 'L2_ffn_sw1': _L2_ffn_in['sw1'], 'L2_ffn_sw3': _L2_ffn_in['sw3'], 'L2_ffn_sw2': _L2_ffn_in['sw2'], 'L3_xattn_ln_x_g': _L3_xattn_in['ln_x_g'], 'L3_xattn_ln_x_b': _L3_xattn_in['ln_x_b'], 'L3_xattn_ln_l_g': _L3_xattn_in['ln_l_g'], 'L3_xattn_ln_l_b': _L3_xattn_in['ln_l_b'], 'L3_xattn_q_gamma': _L3_xattn_in['q_gamma'], 'L3_xattn_k_gamma': _L3_xattn_in['k_gamma'], 'L3_xattn_W_q': _L3_xattn_in['W_q'], 'L3_xattn_W_kv': _L3_xattn_in['W_kv'], 'L3_xattn_W_out': _L3_xattn_in['W_out'], 'L3_xattn_b_out': _L3_xattn_in['b_out'], 'L3_ffn_fast_b': _L3_ffn_in['fast_b'], 'L3_ffn_w_fc': _L3_ffn_in['w_fc'], 'L3_ffn_w_proj': _L3_ffn_in['w_proj'], 'L3_ffn_u': _L3_ffn_in['u'], 'L3_ffn_v': _L3_ffn_in['v'], 'L3_ffn_gate': _L3_ffn_in['gate']}

def reference(x, ctx_1024, itok_BxS_8_8191, itok_BxS2_1_8191, mask_BxSxS2_if1, mask_BxS2_bk0, g_xattn, g_ffn, L0_xattn_W, L0_xattn_b, L0_ffn_Wq, L0_ffn_bq, L0_ffn_bn_gamma, L0_ffn_bn_beta, L0_ffn_sub_key0, L0_ffn_sub_key1, L0_ffn_expert_down, L0_ffn_expert_up, L1_xattn_W_q, L1_xattn_W_k, L1_xattn_W_v, L1_xattn_W_o, L1_ffn_rW1, L1_ffn_rb1, L1_ffn_ln_g, L1_ffn_ln_b, L1_ffn_rW2, L1_ffn_rb2, L1_ffn_qW, L1_ffn_qb, L1_ffn_kW, L1_ffn_kb, L1_ffn_vW, L1_ffn_vb, L1_ffn_oW, L1_ffn_ob, L2_xattn_Wq, L2_xattn_Wk, L2_xattn_Wv, L2_xattn_Wo, L2_ffn_gate_w, L2_ffn_w1, L2_ffn_w3, L2_ffn_w2, L2_ffn_sw1, L2_ffn_sw3, L2_ffn_sw2, L3_xattn_ln_x_g, L3_xattn_ln_x_b, L3_xattn_ln_l_g, L3_xattn_ln_l_b, L3_xattn_q_gamma, L3_xattn_k_gamma, L3_xattn_W_q, L3_xattn_W_kv, L3_xattn_W_out, L3_xattn_b_out, L3_ffn_fast_b, L3_ffn_w_fc, L3_ffn_w_proj, L3_ffn_u, L3_ffn_v, L3_ffn_gate):
    import jax
    import jax.numpy as jnp

    def _L0_xattn_ref(x1, x2, W, b):
        import jax, jax.numpy as jnp
        import numpy as np
        D1, D2, D3 = (128, 128, 128)
        d1 = x1.shape[-1]
        W1 = W[:, :d1]
        W2 = W[:, d1:]
        part1 = jnp.einsum('bld,ed->ble', x1, W1)
        part2 = jnp.einsum('bld,ed->be', x2, W2) / x2.shape[1]
        return part1 + part2[:, None, :] + b

    def _L0_ffn_ref(hidden_states, Wq, bq, bn_gamma, bn_beta, sub_key0, sub_key1, expert_down, expert_up):
        import jax, jax.numpy as jnp
        import numpy as np
        H = 8
        QD = 32
        HALF = QD // 2
        DIMS = (32, 32)
        TOPK = 16
        DTK = 4
        EPS_BN = 1e-05
        EPS_NORM = 1e-12

        def _l2norm(x):
            n = jnp.linalg.norm(x, axis=-1, keepdims=True)
            return x / jnp.maximum(n, EPS_NORM)
        B, S, D = hidden_states.shape
        q = (hidden_states @ Wq + bq).reshape(B, S, H, QD)
        mean = q.mean(axis=(0, 1, 2))
        var = q.var(axis=(0, 1, 2))
        q = (q - mean) / jnp.sqrt(var + EPS_BN) * bn_gamma + bn_beta
        q0 = _l2norm(q[..., :HALF])
        q1 = _l2norm(q[..., HALF:])
        k0 = _l2norm(sub_key0)
        k1 = _l2norm(sub_key1)
        s0 = jnp.einsum('bshq,kq->bshk', q0, k0)
        s1 = jnp.einsum('bshq,kq->bshk', q1, k1)
        ts0, ti0 = jax.lax.top_k(s0, DTK)
        ts1, ti1 = jax.lax.top_k(s1, DTK)
        comb_s = (ts0[..., :, None] + ts1[..., None, :]).reshape(B, S, H, DTK * DTK)
        comb_i = (ti0[..., :, None] * DIMS[1] + ti1[..., None, :]).reshape(B, S, H, DTK * DTK)
        top_s, pos = jax.lax.top_k(comb_s, TOPK)
        idx = jnp.take_along_axis(comb_i, pos, axis=-1)
        w = jax.nn.softmax(top_s, axis=-1)
        down = expert_down[idx]
        up = expert_up[idx]
        eh = jnp.einsum('bshkd,bsd->bshk', down, hidden_states)
        eh = jax.nn.gelu(eh, approximate=False)
        out = jnp.einsum('bshko,bshk->bso', up, eh * w)
        return out

    def _L1_xattn_ref(query, keys, values, W_q, W_k, W_v, W_o, query_pos, key_pos, mask):
        import jax, jax.numpy as jnp
        import numpy as np
        DIM = 128
        NUM_HEADS = 16
        HEAD_DIM = DIM // NUM_HEADS

        def _slopes(num_heads):
            ratio = 2.0 ** (-8.0 / num_heads)
            return jnp.asarray([ratio ** i for i in range(1, num_heads + 1)], dtype=jnp.float32)
        b, q_len, _ = query.shape
        k_len = keys.shape[1]
        scale = 1.0 / np.sqrt(HEAD_DIM)
        Q = (query @ W_q.T).reshape(b, q_len, NUM_HEADS, HEAD_DIM).transpose(0, 2, 1, 3)
        K = (keys @ W_k.T).reshape(b, k_len, NUM_HEADS, HEAD_DIM).transpose(0, 2, 1, 3)
        V = (values @ W_v.T).reshape(b, k_len, NUM_HEADS, HEAD_DIM).transpose(0, 2, 1, 3)
        scores = jnp.einsum('bhqd,bhkd->bhqk', Q, K) * scale
        dist = (query_pos[:, :, None] - key_pos[:, None, :]).astype(scores.dtype)
        bias = -_slopes(NUM_HEADS)[None, :, None, None] * dist[:, None, :, :]
        scores = scores + bias
        scores = jnp.where(mask[:, None, :, :] == 0, -jnp.inf, scores)
        m = jnp.max(scores, axis=-1, keepdims=True)
        e = jnp.exp(scores - m)
        attn = e / (1.0 + jnp.sum(e, axis=-1, keepdims=True))
        out = jnp.einsum('bhqk,bhkd->bhqd', attn, V)
        out = out.transpose(0, 2, 1, 3).reshape(b, q_len, DIM)
        return out @ W_o.T

    def _L1_ffn_ref(x, rW1, rb1, ln_g, ln_b, rW2, rb2, qW, qb, kW, kb, vW, vb, oW, ob):
        import jax, jax.numpy as jnp
        import numpy as np
        H = 16
        TOP_K = 2
        LN_EPS = 1e-05
        B, S, E = x.shape
        NE = qW.shape[0]
        Dh = E // H
        scale = 1.0 / jnp.sqrt(jnp.asarray(Dh, x.dtype))
        h = x @ rW1.T + rb1
        mu = h.mean(-1, keepdims=True)
        var = ((h - mu) ** 2).mean(-1, keepdims=True)
        h = (h - mu) * jax.lax.rsqrt(var + LN_EPS) * ln_g + ln_b
        h = jax.nn.relu(h)
        logits = h @ rW2.T + rb2
        probs = jax.nn.softmax(logits, axis=-1)
        tp, ti = jax.lax.top_k(probs, TOP_K)
        tp = tp / tp.sum(-1, keepdims=True)
        expert_mask = (jax.nn.one_hot(ti, NE, dtype=probs.dtype) * tp[..., None]).sum(-2)
        gates = jnp.moveaxis(expert_mask, -1, 0)

        def expert_step(acc, params):
            qw, qb_, kw, kb_, vw, vb_, ow, ob_, g = params
            q = (x @ qw.T + qb_).reshape(B, S, H, Dh).transpose(0, 2, 1, 3)
            k = (x @ kw.T + kb_).reshape(B, S, H, Dh).transpose(0, 2, 1, 3)
            v = (x @ vw.T + vb_).reshape(B, S, H, Dh).transpose(0, 2, 1, 3)
            scores = jnp.einsum('bhqd,bhkd->bhqk', q, k) * scale
            p = jax.nn.softmax(scores, axis=-1)
            o = jnp.einsum('bhqk,bhkd->bhqd', p, v)
            o = o.transpose(0, 2, 1, 3).reshape(B, S, E) @ ow.T + ob_
            return (acc + o * g[..., None], None)
        out, _ = jax.lax.scan(expert_step, jnp.zeros_like(x), (qW, qb, kW, kb, vW, vb, oW, ob, gates))
        return out

    def _L2_xattn_ref(x_query, x_kv, Wq, Wk, Wv, Wo):
        import jax, jax.numpy as jnp
        import numpy as np
        DIM = 128
        NUM_HEADS = 16
        HEAD_DIM = DIM // NUM_HEADS
        ROPE_BASE = 10000.0
        SCALE = 1.0 / np.sqrt(HEAD_DIM)

        def _rotate_half(x):
            x1, x2 = jnp.split(x, 2, axis=-1)
            return jnp.concatenate([-x2, x1], axis=-1)

        def _rope(x, seq_len):
            inv_freq = 1.0 / ROPE_BASE ** (jnp.arange(0, HEAD_DIM, 2, dtype=jnp.float32) / HEAD_DIM)
            t = jnp.arange(seq_len, dtype=jnp.float32)
            freqs = jnp.outer(t, inv_freq)
            emb = jnp.concatenate([freqs, freqs], -1)
            cos = jnp.cos(emb)[None, None]
            sin = jnp.sin(emb)[None, None]
            return x * cos + _rotate_half(x) * sin
        B, T_q, _ = x_query.shape
        T_k = x_kv.shape[1]
        h, d = (NUM_HEADS, HEAD_DIM)
        q = (x_query @ Wq.T).reshape(B, T_q, h, d).transpose(0, 2, 1, 3)
        k = (x_kv @ Wk.T).reshape(B, T_k, h, d).transpose(0, 2, 1, 3)
        v = (x_kv @ Wv.T).reshape(B, T_k, h, d).transpose(0, 2, 1, 3)
        q = _rope(q, T_q)
        k = _rope(k, T_k)
        attn = jnp.einsum('bhqd,bhkd->bhqk', q, k) * SCALE
        attn = jax.nn.softmax(attn, axis=-1)
        out = jnp.einsum('bhqk,bhkd->bhqd', attn, v)
        out = out.transpose(0, 2, 1, 3).reshape(B, T_q, DIM)
        return out @ Wo.T

    def _L2_ffn_ref(x, gate_w, w1, w3, w2, sw1, sw3, sw2):
        import jax, jax.numpy as jnp
        import numpy as np
        DIM = 128
        HID = 64
        N_EXPERTS = 16
        TOP_K = 4
        bsz, seq_len, dim = x.shape
        xf = x.reshape(-1, dim)
        T = xf.shape[0]
        probs = jax.nn.softmax(xf @ gate_w.T, axis=-1)
        top_w, top_idx = jax.lax.top_k(probs, TOP_K)
        top_w = top_w / jnp.sum(top_w, axis=-1, keepdims=True)
        rows = jnp.arange(T)[:, None]
        combine = jnp.zeros((T, N_EXPERTS), dtype=xf.dtype).at[rows, top_idx].set(top_w)
        h1 = jnp.einsum('td,ehd->teh', xf, w1)
        h3 = jnp.einsum('td,ehd->teh', xf, w3)
        act = jax.nn.silu(h1) * h3
        eout = jnp.einsum('teh,edh->ted', act, w2)
        moe_out = jnp.einsum('ted,te->td', eout, combine)
        shared = jax.nn.silu(xf @ sw1.T) * (xf @ sw3.T) @ sw2.T
        return (moe_out + shared).reshape(bsz, seq_len, dim)

    def _L3_xattn_ref(x, latents, mask, ln_x_g, ln_x_b, ln_l_g, ln_l_b, q_gamma, k_gamma, W_q, W_kv, W_out, b_out):
        import jax, jax.numpy as jnp
        import numpy as np
        DIM = 128
        DIM_LATENT = 128
        DIM_HEAD = 64
        INNER = max(DIM, DIM_LATENT)
        HEADS = INNER // DIM_HEAD
        SCALE = DIM_HEAD ** (-0.5)
        LN_EPS = 1e-05
        RMS_EPS = 1e-08

        def layernorm(x, g, b):
            mu = jnp.mean(x, axis=-1, keepdims=True)
            var = jnp.mean(jnp.square(x - mu), axis=-1, keepdims=True)
            return (x - mu) * jax.lax.rsqrt(var + LN_EPS) * g + b

        def rmsnorm(x, gamma):
            n = jnp.linalg.norm(x, axis=-1, keepdims=True) * x.shape[-1] ** (-0.5)
            return x / jnp.maximum(n, RMS_EPS) * gamma
        b, n, _ = x.shape
        nl = latents.shape[1]
        xn = layernorm(x, ln_x_g, ln_x_b)
        ln = layernorm(latents, ln_l_g, ln_l_b)
        q = ln @ W_q
        kv = jnp.concatenate([xn @ W_kv, ln @ W_kv], axis=1)
        k, v = (kv[..., :INNER], kv[..., INNER:])
        to_heads = lambda t: t.reshape(t.shape[0], t.shape[1], HEADS, DIM_HEAD).transpose(0, 2, 1, 3)
        q, k, v = (to_heads(q), to_heads(k), to_heads(v))
        qn = rmsnorm(q, q_gamma) * SCALE
        kn = rmsnorm(k, k_gamma)
        sim = jnp.einsum('bhid,bhjd->bhij', qn, kn)
        full_mask = jnp.pad(mask, ((0, 0), (0, nl)), constant_values=True)
        neg = -jnp.finfo(sim.dtype).max
        sim = jnp.where(full_mask[:, None, None, :], sim, neg)
        attn = jax.nn.softmax(sim.astype(jnp.float32), axis=-1).astype(sim.dtype)
        out = jnp.einsum('bhij,bhjd->bhid', attn, v)
        out = out.transpose(0, 2, 1, 3).reshape(b, nl, INNER)
        return out @ W_out + b_out

    def _L3_ffn_ref(x, fast_b, w_fc, w_proj, u, v, gate):
        import jax, jax.numpy as jnp
        import numpy as np

        def _bitlinear(x, w_latent):
            scale = jax.lax.stop_gradient(jnp.clip(jnp.mean(jnp.abs(w_latent), axis=1, keepdims=True), 1e-05, None))
            tern = jnp.clip(jnp.round(w_latent / scale), -1.0, 1.0)
            w = w_latent + jax.lax.stop_gradient(tern - w_latent)
            return x @ (w * scale).T
        h = _bitlinear(x, w_fc) + gate * (x @ v.T @ fast_b.T @ u.T)
        r = jnp.maximum(h, 0.0)
        return _bitlinear(r * r, w_proj)
    x = x + jnp.tanh(g_xattn[0]) * _L0_xattn_ref(_layernorm(x, axis=-1), ctx_1024, L0_xattn_W, L0_xattn_b)
    x = x + jnp.tanh(g_ffn[0]) * _L0_ffn_ref(_layernorm(x, axis=-1), L0_ffn_Wq, L0_ffn_bq, L0_ffn_bn_gamma, L0_ffn_bn_beta, L0_ffn_sub_key0, L0_ffn_sub_key1, L0_ffn_expert_down, L0_ffn_expert_up)
    x = x + jnp.tanh(g_xattn[1]) * _L1_xattn_ref(_layernorm(x, axis=-1), ctx_1024, ctx_1024, L1_xattn_W_q, L1_xattn_W_k, L1_xattn_W_v, L1_xattn_W_o, itok_BxS_8_8191, itok_BxS2_1_8191, mask_BxSxS2_if1)
    x = x + jnp.tanh(g_ffn[1]) * _L1_ffn_ref(_layernorm(x, axis=-1), L1_ffn_rW1, L1_ffn_rb1, L1_ffn_ln_g, L1_ffn_ln_b, L1_ffn_rW2, L1_ffn_rb2, L1_ffn_qW, L1_ffn_qb, L1_ffn_kW, L1_ffn_kb, L1_ffn_vW, L1_ffn_vb, L1_ffn_oW, L1_ffn_ob)
    x = x + jnp.tanh(g_xattn[2]) * _L2_xattn_ref(_layernorm(x, axis=-1), ctx_1024, L2_xattn_Wq, L2_xattn_Wk, L2_xattn_Wv, L2_xattn_Wo)
    x = x + jnp.tanh(g_ffn[2]) * _L2_ffn_ref(_layernorm(x, axis=-1), L2_ffn_gate_w, L2_ffn_w1, L2_ffn_w3, L2_ffn_w2, L2_ffn_sw1, L2_ffn_sw3, L2_ffn_sw2)
    x = x + jnp.tanh(g_xattn[3]) * _L3_xattn_ref(ctx_1024, _layernorm(x, axis=-1), mask_BxS2_bk0, L3_xattn_ln_x_g, L3_xattn_ln_x_b, L3_xattn_ln_l_g, L3_xattn_ln_l_b, L3_xattn_q_gamma, L3_xattn_k_gamma, L3_xattn_W_q, L3_xattn_W_kv, L3_xattn_W_out, L3_xattn_b_out)
    x = x + jnp.tanh(g_ffn[3]) * _L3_ffn_ref(_layernorm(x, axis=-1), L3_ffn_fast_b, L3_ffn_w_fc, L3_ffn_w_proj, L3_ffn_u, L3_ffn_v, L3_ffn_gate)
    return x

_drawn_inputs = setup_inputs


def setup_inputs(seed=0):
    import zlib

    import numpy as np

    out = dict(_drawn_inputs(seed))
    spreads = {'L0_ffn_bq': (0.0, 0.8),
     'L0_ffn_bn_gamma': (1.0, 0.6),
     'L0_ffn_bn_beta': (0.0, 0.8),
     'L1_ffn_rb1': (0.0, 0.372),
     'L1_ffn_ln_g': (1.0, 0.6),
     'L1_ffn_ln_b': (0.0, 0.583),
     'L1_ffn_rb2': (0.0, 0.1),
     'L1_ffn_qb': (0.0, 0.8),
     'L1_ffn_kb': (0.0, 2.0),
     'L1_ffn_vb': (0.0, 0.653),
     'L1_ffn_ob': (0.0, 0.1),
     'L3_xattn_ln_x_g': (1.0, 0.6),
     'L3_xattn_ln_x_b': (0.0, 0.731),
     'L3_xattn_ln_l_g': (1.0, 0.2),
     'L3_xattn_ln_l_b': (0.0, 0.351),
     'L3_xattn_q_gamma': (1.0, 0.6),
     'L3_xattn_k_gamma': (1.0, 0.6),
     'L3_xattn_b_out': (0.0, 0.1)}
    factors = {'g_ffn': 8.0,
     'L0_ffn_Wq': 8.0,
     'L0_ffn_sub_key0': 8.0,
     'L0_ffn_sub_key1': 8.0,
     'L0_ffn_expert_down': 4.765,
     'L0_ffn_expert_up': 5.162,
     'L1_ffn_qW': 8.0,
     'L1_ffn_kW': 8.0,
     'L1_ffn_vW': 4.868,
     'L1_ffn_oW': 3.307,
     'L2_ffn_gate_w': 8.0,
     'L2_ffn_w1': 8.0,
     'L2_ffn_w3': 8.0,
     'L2_ffn_w2': 8.0,
     'L2_ffn_sw1': 8.0,
     'L2_ffn_sw3': 8.0,
     'L2_ffn_sw2': 8.0,
     'L3_ffn_fast_b': 8.0,
     'L3_ffn_w_fc': 7.189,
     'L3_ffn_w_proj': 5.52,
     'L3_ffn_u': 8.0,
     'L3_ffn_v': 8.0}
    for name, (base, spread) in spreads.items():
        noise = np.random.default_rng([zlib.crc32(name.encode()), seed]).standard_normal(out[name].shape)
        drawn = base * np.exp(spread * noise) if base else spread * noise
        out[name] = jnp.asarray(drawn.astype(out[name].dtype))
    for name, factor in factors.items():
        out[name] = (out[name] * factor).astype(out[name].dtype)
    return out
```

```python
from contextlib import ExitStack

import numpy as np

import concourse.bass as bass
from concourse import mybir

F32 = mybir.dt.float32
I32 = mybir.dt.int32
ACT = mybir.ActivationFunctionType
ALU = mybir.AluOpType
AX = mybir.AxisListType

P = 128
BATCH, SEQ, DIM = 16, 64, 128
TOKENS = BATCH * SEQ
TILES = TOKENS // P
HEADS, HEAD_DIM = 16, 8
HALF = 512
PK_HEADS, PK_KEYS, PK_TOP = 8, 32, 4
PK_EXPERTS = 128
PK_GROUPS = 2 * PK_HEADS
PK_FAR = PK_EXPERTS // PK_KEYS
AE, AE_HID = 8, 64
FE, FE_HID, FE_TOP = 16, 64, 4
PAIRS = FE // 2 + 1
L_HEADS, L_DIM = 2, 64
KEYS = 2 * SEQ
HIDDEN, RANK = 512, 16
CHUNKS = HIDDEN // P
EPS = 1e-5
MASKED = -1e30
SCALE8 = float(HEAD_DIM ** -0.5)
V_COLS = 18
RING_K, RING_Q, RING_V = 4, 8, 6
PAIRS_H = HEADS // 2

PACK = [
    ("ident", P), ("w1t", P), ("w2t", P), ("ones", P),
    ("rows", 5 * P),
    ("pk_wq", 2 * P), ("pk_bq", 2), ("pk_gamma", 1), ("pk_beta", 1), ("pk_keys", 2 * P),
    ("pk_group", 8), ("pk_mean", P), ("pk_down", P), ("pk_up", P),
    ("a1_q", P), ("a1_k", P), ("a1_v", P), ("a1_o", P), ("slopes", HEADS),
    ("r_w1", AE_HID), ("r_g", 1), ("r_b", 1), ("r_w2", AE),
    ("e_qb", AE), ("e_kb", AE), ("e_vb", AE * AE), ("e_ob", P),
    ("e_q", AE * P), ("e_k", AE * P), ("e_v", AE * P), ("e_o", AE * P),
    ("a2_q", P), ("a2_qp", P), ("a2_k", P), ("a2_kp", P), ("a2_v", P), ("a2_o", P),
    ("cosq", SEQ), ("sinq", SEQ), ("cosk", SEQ), ("sink", SEQ),
    ("f_gate", FE), ("f_w1", PAIRS * P), ("f_w3", PAIRS * P), ("f_w2", PAIRS * P),
    ("x_g", 1), ("x_b", 1), ("l_g", 1), ("l_b", 1), ("q_gamma", 1), ("k_gamma", 1),
    ("l3_q", P), ("l3_kv", 2 * P), ("l3_o", P),
    ("b_fc", HIDDEN), ("b_proj", CHUNKS * P), ("b_v", P), ("b_ut", HIDDEN), ("b_fb", RANK), ("b_gate", 1),
]
OFFSET, _at = {}, 0
for _name, _width in PACK:
    OFFSET[_name] = (_at, _width)
    _at += _width
PACK_COLS = _at
GROUPS = ["rows", "pk_up", "slopes", "e_ob", "e_o", "sink", "f_w2", "b_gate"]


def group_ends():
    return [OFFSET[name][0] + OFFSET[name][1] for name in GROUPS]


def build(nc, d_x, d_ctx, d_ctxt, d_pack, d_gates, d_qpos, d_kpos, d_mask, d_keep, d_out, layers=8):
    ctx = ExitStack()
    with ctx:
        def sb(name, cols, dt=F32):
            return ctx.enter_context(nc.sbuf_tensor(name, [P, cols], dt))

        def sem(name):
            return ctx.enter_context(nc.semaphore(name))

        bank = [ctx.enter_context(nc.psum_tensor(f"bank{i}", [P, HALF], F32)) for i in range(8)]

        pack = sb("pack", PACK_COLS)

        def W(name, a=0, n=None, rows=P):
            at, width = OFFSET[name]
            return pack[0:rows, at + a:at + a + (width if n is None else n)]

        X = sb("X", TOKENS)
        H = sb("H", TOKENS)
        HT = sb("HT", TOKENS)
        CT = sb("ctxT", TOKENS)
        KBD = sb("KBD", RING_K * 2 * HEADS * SEQ)
        SCR = sb("scratch", 16384)
        VM = sb("VM", RING_V * 2 * PAIRS_H * V_COLS)
        QT = sb("QT", RING_Q * P)
        KT = sb("KT", RING_Q * P)
        PB = sb("probs", 2 * HEADS * SEQ)
        PTB = sb("probsT", 2 * HEADS * SEQ)
        ON = sb("heads_out", 2 * P)
        OTB = sb("heads_outT", 2 * P)
        gates_in = sb("gates_in", 8)
        gate = sb("gate", 8)
        stats = sb("stats", TILES * 6)
        mv = sb("mean_var", TILES * 2)
        var_eps = sb("var_eps", TILES)
        rstd = sb("rstd", TILES)
        neghalf = sb("neghalf", 2 * P)
        rowmax = sb("rowmax", HEADS)
        rsum = sb("rsum", 2 * HEADS)
        qpos = sb("qpos", TILES, I32)
        qposf = sb("qposf", TILES)
        kpos = PB[:, 0:TILES * SEQ].bitcast(I32)
        mask = PB[:, TILES * SEQ:2 * TILES * SEQ].bitcast(I32)
        keep = sb("keep", SEQ, I32)
        ND = sb("minus_distance", TILES * SEQ)
        MADD = sb("mask_add", TILES * SEQ)
        small = sb("small", 512)
        GATES = sb("expert_gates", TILES * AE)
        GT = H[0:AE, :]
        OB = sb("out_bias", P)

        Xt = X[:, :].rearrange("p (t d) -> p t d", t=TILES)
        Ht = H[:, :].rearrange("p (t d) -> p t d", t=TILES)
        Ct = QT[:, :].rearrange("p (t d) -> p t d", t=TILES)
        KBDu = KBD[:, :].rearrange("p (u b h k) -> p u b h k", u=RING_K, b=2, h=HEADS)
        VMu = VM[:, :].rearrange("p (u b j c) -> p u b j c", u=RING_V, b=2, j=PAIRS_H)
        MV = mv[:, :].rearrange("p (t c) -> p t c", c=2)
        STATS = stats[:, :].rearrange("p (t c) -> p t c", c=6)
        ident = W("ident")
        row_at = {"b0": 0, "b3": P, "rb1": 2 * P, "rb2": 3 * P}

        in_x = sem("in_x")
        in_ctx = sem("in_ctx")
        in_small = sem("in_small")
        in_pack = [sem(f"in_pack_{g}") for g in GROUPS]
        layer_end = sem("layer_end")
        own = {e: sem(f"own_{e}") for e in ("vector", "pool", "scalar")}
        zeroed = sem("zeroed")
        consts = sem("consts")
        gate_ready = sem("gate_ready")
        var_ready = sem("var_ready")
        rstd_ready = sem("rstd_ready")
        normed = sem("normed")
        turned = sem("turned")
        ht_ready = sem("ht_ready")
        l0_out = sem("l0_out")
        ctx_mean = sem("ctx_mean")
        out_stored = sem("out_stored")

        class Order:

            def __init__(self, eng, name):
                self.eng, self.sem, self.n = eng, own[name], 0

            def mark(self, ins):
                ins.then_inc(self.sem, 1)
                self.n += 1

            def settle(self):
                self.eng.wait_ge(self.sem, self.n)

            def link(self, ins):
                self.mark(ins)
                self.settle()

        def end_layer(eng, k):
            eng.drain().then_inc(layer_end, 1)
            eng.wait_ge(layer_end, 5 * (k + 1))

        first_use = {0: (0,), 1: (1,), 2: (2,), 3: (3, 4), 4: (5,), 5: (6,), 6: (7,)}

        def norm_vector(v, order, src, dst, n):
            for t in range(TILES):
                order.mark(v.bn_stats(STATS[:, t, :], src(t)))
            order.settle()
            for t in range(TILES):
                last = v.bn_aggr(MV[:, t, :], STATS[:, t, :])
            last.then_inc(var_ready, 1)
            v.wait_ge(rstd_ready, n + 1)
            for t in range(TILES):
                v.tensor_scalar(dst(t), src(t), MV[:, t, 0:1], rstd[:, t:t + 1], ALU.subtract, ALU.mult)\
                    .then_inc(normed, 1)

        def norm_pool(g, order, n):
            g.wait_ge(var_ready, n + 1)
            order.link(g.tensor_scalar(var_eps[:, :], MV[:, :, 1], EPS, None, ALU.add))
            g.tensor_tensor(rstd[:, :], var_eps[:, :], neghalf[:, 0:TILES], ALU.pow).then_inc(rstd_ready, 1)

        def turn_tensor(pe, src, norm_n, banks=(0, 1)):
            for t in range(TILES):
                pe.wait_ge(normed, TILES * norm_n + t + 1)
                ins = pe.transpose(bank[banks[t // 4]][:, P * (t % 4):P * (t % 4) + P], src(t), ident)
                if t % 4 == 3:
                    ins.then_inc(turned, 1)

        def turn_scalar(a, n, banks=(0, 1)):
            for j in range(2):
                a.wait_ge(turned, 2 * n + j + 1)
                a.copy(HT[:, HALF * j:HALF * j + HALF], bank[banks[j]][:, :]).then_inc(ht_ready, 1)

        def x_tile(t):
            return Xt[:, t, :]

        def h_tile(t):
            return Ht[:, t, :]

        def ht(t, n=1):
            return HT[:, P * t:P * (t + n)]

        def add_to_x(v, k, half, src):
            xs = X[:, HALF * half:HALF * half + HALF]
            return v.scalar_tensor_tensor(xs, src, gate[:, k:k + 1], xs, ALU.mult, ALU.add)

        CS = small[:, 0:BATCH]
        CSB = SCR[:, 0:TOKENS]

        def l0x_vector(v, o):
            v.wait_ge(in_ctx, 16)
            o.link(v.tensor_reduce(CS, CT[:, :].rearrange("p (b s) -> p b s", b=BATCH), AX.X, ALU.add))
            v.tensor_scalar(CSB.rearrange("p (b s) -> p b s", b=BATCH),
                            CS[:, :, None].to_broadcast([P, BATCH, SEQ]), 1.0 / SEQ, None, ALU.mult)\
                .then_inc(ctx_mean, 1)
            v.wait_ge(in_x, 16)
            norm_vector(v, o, x_tile, h_tile, 0)
            v.wait_ge(gate_ready, 1)
            for j in range(2):
                v.wait_ge(l0_out, j + 1)
                add_to_x(v, 0, j, bank[2 + j][:, :])

        def l0x_tensor(pe):
            pe.wait_ge(in_pack[0], 16)
            turn_tensor(pe, h_tile, 0)
            pe.wait_ge(ctx_mean, 1)
            for t in range(TILES):
                pe.wait_ge(ht_ready, t // 4 + 1)
                out = bank[2 + t // 4][:, P * (t % 4):P * (t % 4) + P]
                pe.matmul(out, ht(t), W("w1t"), start=True, stop=False)
                pe.matmul(out, CSB[:, P * t:P * t + P], W("w2t"), start=False, stop=False)
                ins = pe.matmul(out, W("ones", rows=1), W("rows", row_at["b0"], P, rows=1), start=False, stop=True)
                if t % 4 == 3:
                    ins.then_inc(l0_out, 1)

        qa = SCR[:, 0:2048].rearrange("p (a t) -> p a t", a=2)
        qn = SCR[:, 2048:4096].rearrange("p (a t) -> p a t", a=2)
        sq = SCR[:, 4096:6144].rearrange("p (a t) -> p a t", a=2)
        sc = SCR[:, 6144:10240].rearrange("p (t g k) -> p t g k", t=TILES, g=PK_GROUPS)
        mk = SCR[:, 10240:14336].rearrange("p (t g k) -> p t g k", t=TILES, g=PK_GROUPS)
        pw = SCR[:, 14336:16384].rearrange("p (b h i k) -> p b h i k", b=2, h=PK_HEADS, i=PK_FAR)
        gelu_t = SCR[:, 0:1024]
        wg = SCR[:, 2048:3072]
        wexp = SCR[:, 3072:4096].rearrange("p (t e) -> p t e", t=TILES)
        keybd = SCR[:, 14336:14592]
        keysq = SCR[:, 14592:14848]
        pkst = small[:, 0:64]
        n2 = small[:, 64:192]
        rn = small[:, 192:320]
        top8 = small[:, 320:448]
        totals = small[:, 448:464]
        rtot = small[:, 464:480]
        rem = small[:, 480:488]
        near = small[:, 488:496]
        farw = small[:, 496:497]
        p0n = PTB[:, 0:TILES * PK_HEADS * PK_FAR]
        p0nt = p0n[:, :].rearrange("p (t h i) -> p t h i", t=TILES, h=PK_HEADS)
        knorm = PTB[:, 512:512 + 2 * P]
        pk_q, pk_qa = sem("pk_q"), sem("pk_qa")
        pk_keysq, pk_keysum, pk_keyn2, pk_keyr = sem("pk_keysq"), sem("pk_keysum"), sem("pk_keyn2"), sem("pk_keyr")
        pk_keyready = sem("pk_keyready")
        pk_rowstat, pk_stat, pk_qvar, pk_qrstd = sem("pk_rowstat"), sem("pk_stat"), sem("pk_qvar"), sem("pk_qrstd")
        pk_qn, pk_sq, pk_score, pk_norm2 = sem("pk_qn"), sem("pk_sq"), sem("pk_score"), sem("pk_norm2")
        pk_n2, pk_rn, pk_sc, pk_exp = sem("pk_n2"), sem("pk_rn"), sem("pk_sc"), sem("pk_exp")
        pk_p0, pk_pw, pk_w, pk_wt, pk_wg = sem("pk_p0"), sem("pk_pw"), sem("pk_w"), sem("pk_wt"), sem("pk_wg")
        pk_eh, pk_gelu, pk_out, pk_pwread = sem("pk_eh"), sem("pk_gelu"), sem("pk_out"), sem("pk_pwread")
        pk_scread = sem("pk_scread")

        def l0f_keys_vector(v, o):
            v.tensor_tensor(keysq, W("pk_keys"), W("pk_keys"), ALU.mult).then_inc(pk_keysq, 1)
            v.wait_ge(pk_keysum, 1)
            v.tensor_scalar(knorm[:, :], bank[2][:, 0:2 * P], 1e-24, None, ALU.max).then_inc(pk_keyn2, 1)
            v.wait_ge(pk_keyr, 1)
            v.tensor_tensor(keybd, W("pk_keys"), knorm[:, :], ALU.mult).then_inc(pk_keyready, 1)

        def l0f_vector(v, o):
            norm_vector(v, o, x_tile, h_tile, 1)
            l0f_keys_vector(v, o)
            st = pkst[:, 0:24].rearrange("p (a c) -> p a c", a=4)
            agg = pkst[:, 24:28].rearrange("p (a c) -> p a c", a=2)
            for a_ in range(2):
                for j in range(2):
                    v.wait_ge(pk_qa, 2 * a_ + j + 1)
                    o.mark(v.bn_stats(st[:, 2 * a_ + j, :], qa[:, a_, HALF * j:HALF * j + HALF]))
            o.settle()
            for a_ in range(2):
                o.mark(v.bn_aggr(agg[:, a_, :], st[:, 2 * a_:2 * a_ + 2, :].rearrange("p a c -> p (a c)")))
            o.settle()
            msq = pkst[:, 28:30]
            o.link(v.tensor_tensor(msq, agg[:, :, 0], agg[:, :, 0], ALU.mult))
            v.tensor_tensor(agg[:, :, 1], agg[:, :, 1], msq, ALU.add).then_inc(pk_rowstat, 1)
            v.wait_ge(pk_stat, 1)
            stat = pkst[:, 30:32]
            o.link(v.tensor_copy(stat, bank[2][:, 0:2]))
            mean2, qvar = pkst[:, 32:33], pkst[:, 33:34]
            o.link(v.tensor_tensor(mean2, stat[:, 0:1], stat[:, 0:1], ALU.mult))
            o.link(v.tensor_tensor(qvar, stat[:, 1:2], mean2, ALU.subtract))
            v.tensor_scalar(pkst[:, 34:35], qvar, EPS, None, ALU.add).then_inc(pk_qvar, 1)
            v.wait_ge(pk_qrstd, 1)
            scale, shift = pkst[:, 36:37], pkst[:, 37:38]
            o.link(v.tensor_tensor(scale, pkst[:, 35:36], W("pk_gamma"), ALU.mult))
            o.link(v.tensor_tensor(pkst[:, 38:39], stat[:, 0:1], scale, ALU.mult))
            o.link(v.tensor_tensor(shift, W("pk_beta"), pkst[:, 38:39], ALU.subtract))
            for a_ in range(2):
                v.tensor_scalar(qn[:, a_, :], qa[:, a_, :], scale, shift, ALU.mult, ALU.add).then_inc(pk_qn, 1)
            v.wait_ge(pk_norm2, 1)
            v.tensor_scalar(n2, bank[3][:, 0:P], 1e-24, None, ALU.max).then_inc(pk_n2, 1)
            v.wait_ge(pk_rn, 1)
            rng = rn.rearrange("p (t g) -> p t g", t=TILES)
            for t in range(TILES):
                v.wait_ge(pk_score, t + 1)
                v.tensor_tensor(sc[:, t], bank[4 + t % 4][:, :].rearrange("p (g k) -> p g k", g=PK_GROUPS),
                                rng[:, t, :, None].to_broadcast([P, PK_GROUPS, PK_KEYS]), ALU.mult)\
                    .then_inc(pk_sc, 1)
                v.wait_ge(pk_sc, 2 * t + 1)
                for g_ in range(PK_GROUPS):
                    o.mark(v.max(top8[:, 8 * g_:8 * g_ + 8], sc[:, t, g_, :]))
                o.settle()
                fourth = top8.rearrange("p (g k) -> p g k", g=PK_GROUPS)[:, :, PK_TOP - 1:PK_TOP]
                v.tensor_tensor(mk[:, t], sc[:, t], fourth.to_broadcast([P, PK_GROUPS, PK_KEYS]), ALU.is_ge)\
                    .then_inc(pk_sc, 1)
            hh = "p (h c) k -> p h c k"
            for t in range(TILES):
                v.wait_ge(pk_exp, t + 1)
                o.link(v.tensor_tensor(mk[:, t], mk[:, t], sc[:, t], ALU.mult))
                first = mk[:, t].rearrange(hh, c=2)[:, :, 0, :]
                o.mark(v.tensor_reduce(totals, mk[:, t], AX.X, ALU.add))
                o.mark(v.tensor_reduce(rem, first[:, :, PK_FAR:PK_KEYS], AX.X, ALU.add))
                o.settle()
                o.link(v.reciprocal(rtot, totals))
                rt = rtot.rearrange("p (h c) -> p h c", c=2)
                o.mark(v.tensor_tensor(near, rt[:, :, 0], rt[:, :, 1], ALU.mult))
                o.mark(v.tensor_tensor(rem, rem, rt[:, :, 0], ALU.mult))
                o.settle()
                v.tensor_tensor(p0nt[:, t], first[:, :, 0:PK_FAR],
                                near[:, :, None].to_broadcast([P, PK_HEADS, PK_FAR]), ALU.mult).then_inc(pk_p0, 1)
                o.link(v.tensor_reduce(farw, rem, AX.X, ALU.add))
                v.wait_ge(pk_pw, t + 1)
                v.tensor_reduce(wexp[:, t, :], pw[:, t % 2].rearrange("p h i k -> p (i k) h"), AX.X, ALU.add)\
                    .then_inc(pk_pwread, 1)
                v.wait_ge(pk_pwread, t + 1)
                last = wexp[:, t, PK_EXPERTS - 1:PK_EXPERTS]
                v.tensor_tensor(last, last, farw, ALU.add).then_inc(pk_w, 1)
            for j in range(2):
                v.wait_ge(pk_wt, j + 1)
                v.wait_ge(pk_gelu, j + 1)
                v.tensor_tensor(wg[:, HALF * j:HALF * j + HALF], bank[j][:, :],
                                gelu_t[:, HALF * j:HALF * j + HALF], ALU.mult).then_inc(pk_wg, 1)
            for j in range(2):
                v.wait_ge(pk_out, j + 1)
                add_to_x(v, 1, j, bank[4 + j][:, :])

        def l0f_tensor(pe):
            pe.wait_ge(pk_keysq, 1)
            pe.matmul(bank[2][:, 0:2 * P], W("ones"), keysq, start=True, stop=True).then_inc(pk_keysum, 1)
            for j in range(2):
                for a_ in range(2):
                    pass
            for a_ in range(2):
                for j in range(2):
                    pe.wait_ge(ht_ready, 2 * 1 + j + 1)
                    pe.matmul(bank[4 + 2 * a_ + j][:, :], W("pk_wq", P * a_, P), HT[:, HALF * j:HALF * j + HALF],
                              start=True, stop=True).then_inc(pk_q, 1)
            pe.wait_ge(pk_keyn2, 1)
            pe.wait_ge(pk_rowstat, 1)
            agg = pkst[:, 24:28].rearrange("p (a c) -> p a c", a=2)
            for a_ in range(2):
                ins = pe.matmul(bank[2][:, 0:2], W("pk_mean"), agg[:, a_, :], start=(a_ == 0), stop=(a_ == 1))
            ins.then_inc(pk_stat, 1)
            for a_ in range(2):
                pe.wait_ge(pk_sq, a_ + 1)
            for t in range(TILES):
                for a_ in range(2):
                    ins = pe.matmul(bank[3][:, 16 * t + 8 * a_:16 * t + 8 * a_ + 8], sq[:, a_, P * t:P * t + P],
                                    W("pk_group"), start=True, stop=True)
            ins.then_inc(pk_norm2, 1)
            pe.wait_ge(pk_qa, 4)
            pe.wait_ge(pk_keyready, 1)
            for t in range(TILES):
                if t >= 4:
                    pe.wait_ge(pk_sc, 2 * (t - 4) + 1)
                for a_ in range(2):
                    ins = pe.matmul(bank[4 + t % 4][:, 2 * P * a_:2 * P * a_ + 2 * P], qn[:, a_, P * t:P * t + P],
                                    keybd, start=True, stop=True)
                ins.then_inc(pk_score, 1)
            pe.wait_ge(pk_stat, 1)
            for j in range(2):
                if j == 0:
                    pe.wait_ge(pk_qvar, 1)
                if j == 1:
                    pe.wait_ge(pk_n2, 1)
                pe.matmul(bank[2 + j][:, :], W("pk_down"), HT[:, HALF * j:HALF * j + HALF],
                          start=True, stop=True).then_inc(pk_eh, 1)
            for t in range(TILES):
                pe.wait_ge(pk_w, t + 1)
                ins = pe.transpose(bank[t // 4][:, P * (t % 4):P * (t % 4) + P], wexp[:, t, :], ident)
                if t % 4 == 3:
                    ins.then_inc(pk_wt, 1)
            pe.wait_ge(pk_sc, 2 * TILES)
            for t in range(TILES):
                pe.wait_ge(pk_wg, t // 4 + 1)
                ins = pe.matmul(bank[4 + t // 4][:, P * (t % 4):P * (t % 4) + P], wg[:, P * t:P * t + P], W("pk_up"),
                                start=True, stop=True)
                if t % 4 == 3:
                    ins.then_inc(pk_out, 1)

        def l0f_scalar(a):
            for a_ in range(2):
                for j in range(2):
                    a.wait_ge(pk_q, 2 * a_ + j + 1)
                    a.activation(qa[:, a_, HALF * j:HALF * j + HALF], bank[4 + 2 * a_ + j][:, :], ACT.Identity,
                                 bias=W("pk_bq", a_, 1)).then_inc(pk_qa, 1)
            for a_ in range(2):
                a.wait_ge(pk_qn, a_ + 1)
                a.activation(sq[:, a_, :], qn[:, a_, :], ACT.Square).then_inc(pk_sq, 1)
            for t in range(TILES):
                a.wait_ge(pk_sc, 2 * t + 2)
                a.activation(sc[:, t], sc[:, t], ACT.Exp).then_inc(pk_exp, 1)
            for j in range(2):
                a.wait_ge(pk_eh, j + 1)
                a.activation(gelu_t[:, HALF * j:HALF * j + HALF], bank[2 + j][:, :], ACT.Gelu).then_inc(pk_gelu, 1)

        def l0f_pool(g, o):
            norm_pool(g, o, 1)
            g.wait_ge(pk_keyn2, 1)
            g.tensor_tensor(knorm[:, :], knorm[:, :], neghalf[:, :], ALU.pow).then_inc(pk_keyr, 1)
            g.wait_ge(pk_qvar, 1)
            g.tensor_tensor(pkst[:, 35:36], pkst[:, 34:35], neghalf[:, 0:1], ALU.pow).then_inc(pk_qrstd, 1)
            g.wait_ge(pk_n2, 1)
            g.tensor_tensor(rn, n2, neghalf[:, 0:P], ALU.pow).then_inc(pk_rn, 1)
            for t in range(TILES):
                g.wait_ge(pk_p0, t + 1)
                if t == 0:
                    g.wait_ge(pk_score, TILES)
                if t >= 2:
                    g.wait_ge(pk_pwread, t - 1)
                second = mk[:, t].rearrange("p (h c) k -> p h c k", c=2)[:, :, 1, :]
                shape = [P, PK_HEADS, PK_FAR, PK_KEYS]
                g.tensor_tensor(pw[:, t % 2], p0nt[:, t][:, :, :, None].to_broadcast(shape),
                                second[:, :, None, :].to_broadcast(shape), ALU.mult).then_inc(pk_pw, 1)

        a_proj, a_q, a_k, a_v = sem("a_proj"), sem("a_q"), sem("a_k"), sem("a_v")
        a_kbd = [sem(f"a_kbd{i}") for i in range(RING_K)]
        a_s, a_sub, a_exp = sem("a_s"), sem("a_sub"), sem("a_exp")
        a_t = [sem("a_t0"), sem("a_t1")]
        a_pt = [sem("a_pt0"), sem("a_pt1")]
        a_pv, a_on, a_ot, a_ots, a_out, a_x = (sem("a_pv"), sem("a_on"), sem("a_ot"), sem("a_ots"), sem("a_out"),
                                               sem("a_x"))
        a_biased, a_bias = sem("a_biased"), sem("a_bias")
        rope_q, rope_k = sem("rope_q"), sem("rope_k")
        lead_s, lead_t, lead_pv, lead_ot, lead_out = 3, 4, 5, 6, 7

        class Attention:

            def __init__(self, first, experts, tiles_before, gate_k, wq, wk, wv, wo, self_kv, rope=False, biased=False):
                self.first, self.experts, self.n = first, experts, experts * TILES
                self.tiles_before, self.gate_k = tiles_before, gate_k
                self.wq, self.wk, self.wv, self.wo = wq, wk, wv, wo
                self.self_kv, self.rope, self.biased = self_kv, rope, biased

        cross1 = Attention(0, 1, 0, 2, "a1_q", "a1_k", "a1_v", "a1_o", False, biased=True)
        moe = Attention(8, AE, 8, 3, "e_q", "e_k", "e_v", "e_o", True)
        cross2 = Attention(8 + 8 * AE, 1, 16, 4, None, None, "a2_v", "a2_o", False, rope=True)
        bias1 = SCR[:, 0:8192].rearrange("p (t h k) -> p t h k", t=TILES, h=HEADS)
        S_BANK, PT_BANK, O_BANK, PJ_BANK, OT_BANK, Y_BANK = (0, 1), (2, 3), 4, 5, 6, 7
        PROJECTED = cross1.n + moe.n
        qb_scaled = sb("qb_scaled", AE)

        def attend_tensor(pe, A):
            for s in range(A.n + lead_out):
                i = s
                if i < A.n:
                    g, t, e = A.first + i, i // A.experts, i % A.experts
                    if g > 0:
                        pe.wait_ge(a_v, g)
                    pe.wait_ge(ht_ready, A.ht_need + 2)
                    kv = HT if A.self_kv else CT
                    pj = bank[PJ_BANK]
                    if not A.rope:
                        pe.matmul(pj[:, 0:P], W(A.wk, P * e, P), kv[:, P * t:P * t + P], start=True, stop=True)
                        pe.matmul(pj[:, P:2 * P], W(A.wq, P * e, P), ht(t), start=True, stop=True)
                    for b in range(2):
                        src = kv[:, P * t + SEQ * b:P * t + SEQ * b + SEQ]
                        for half in range(2):
                            ins = pe.matmul(pj[SEQ * half:SEQ * half + SEQ, P * (2 + b):P * (3 + b)], src,
                                            W(A.wv, P * e, P), start=True, stop=True)
                    ins.then_inc(a_proj, 1)
                i = s - lead_s
                if 0 <= i < A.n:
                    g = A.first + i
                    if A.rope:
                        pe.wait_ge(rope_q, 2)
                    else:
                        pe.wait_ge(a_q, g + 1)
                    pe.wait_ge(a_kbd[g % RING_K], 16 * HEADS * (g // RING_K + 1))
                    q0 = P * (g % RING_Q)
                    for half in range(2):
                        if g > 0:
                            pe.wait_ge(a_sub, 2 * (g - 1) + half + 1)
                        for b in range(2):
                            ins = pe.matmul(bank[S_BANK[half]][SEQ * b:SEQ * b + SEQ, :],
                                            QT[:, q0 + SEQ * b:q0 + SEQ * b + SEQ],
                                            KBDu[:, g % RING_K, b, 8 * half:8 * half + 8, :]
                                            .rearrange("p h k -> p (h k)"), start=True, stop=True)
                        ins.then_inc(a_s, 1)
                i = s - lead_t
                if 0 <= i < A.n:
                    g = A.first + i
                    for half in range(2):
                        pe.wait_ge(a_exp, 2 * g + half + 1)
                        if g > 0:
                            pe.wait_ge(a_pt[half], g)
                        for j in range(4):
                            at = 1024 * (g % 2) + HALF * half + P * j
                            ins = pe.transpose(bank[PT_BANK[half]][:, P * j:P * j + P], PB[:, at:at + P], ident)
                        ins.then_inc(a_t[half], 1)
                i = s - lead_pv
                if 0 <= i < A.n:
                    g = A.first + i
                    pe.wait_ge(a_v, g + 1)
                    if g > 0:
                        pe.wait_ge(a_on, g)
                    for j in range(PAIRS_H):
                        if j % 4 == 0:
                            pe.wait_ge(a_pt[j // 4], g + 1)
                        for b in range(2):
                            at = 1024 * (g % 2) + P * j + SEQ * b
                            ins = pe.matmul(bank[O_BANK][SEQ * b:SEQ * b + SEQ, V_COLS * j:V_COLS * (j + 1)],
                                            PTB[:, at:at + SEQ], VMu[:, g % RING_V, b, j, :], start=True, stop=True)
                    ins.then_inc(a_pv, 1)
                i = s - lead_ot
                if 0 <= i < A.n:
                    g = A.first + i
                    pe.wait_ge(a_on, g + 1)
                    if g > 0:
                        pe.wait_ge(a_ots, g)
                    pe.transpose(bank[OT_BANK][:, 0:P], ON[:, P * (g % 2):P * (g % 2) + P], ident).then_inc(a_ot, 1)
                i = s - lead_out
                if 0 <= i < A.n:
                    g, t, e = A.first + i, i // A.experts, i % A.experts
                    pe.wait_ge(a_ots, g + 1)
                    y = bank[Y_BANK][:, 0:P]
                    if e == 0:
                        if A.tiles_before + t > 0:
                            pe.wait_ge(a_x, A.tiles_before + t)
                        if A.experts > 1:
                            pe.wait_ge(r_ready, 2)
                            pe.matmul(y, GT[0:AE, P * t:P * t + P], OB[0:AE, :], start=True, stop=False)
                    pe.matmul(y, OTB[:, P * (g % 2):P * (g % 2) + P], W(A.wo, P * e, P),
                              start=(A.experts == 1), stop=(e == A.experts - 1)).then_inc(a_out, 1)

        def attend_scalar(a, A):
            for s in range(A.n + lead_out):
                i = s
                if i < A.n:
                    g, e = A.first + i, i % A.experts
                    a.wait_ge(a_proj, g + 1)
                    pj, q0 = bank[PJ_BANK], P * (g % RING_Q)
                    if g >= RING_Q:
                        a.wait_ge(a_s, 2 * (g - RING_Q + 1))
                    if not A.rope:
                        if A.experts > 1:
                            a.activation(KT[:, q0:q0 + P], pj[:, 0:P], ACT.Identity, bias=W("e_kb", e, 1))\
                                .then_inc(a_k, 1)
                            a.activation(QT[:, q0:q0 + P], pj[:, P:2 * P], ACT.Identity,
                                         bias=qb_scaled[:, e:e + 1], scale=SCALE8).then_inc(a_q, 1)
                        else:
                            a.copy(KT[:, q0:q0 + P], pj[:, 0:P]).then_inc(a_k, 1)
                            a.mul(QT[:, q0:q0 + P], pj[:, P:2 * P], SCALE8).then_inc(a_q, 1)
                    if g >= RING_V:
                        a.wait_ge(a_pv, g - RING_V + 1)
                    for half in range(2):
                        rows = slice(SEQ * half, SEQ * half + SEQ)
                        src = pj[rows, 2 * P:4 * P].rearrange("p (b j c d) -> p b j c d", b=2, j=PAIRS_H, c=2)
                        ins = a.copy(VMu[rows, g % RING_V, :, :, HEAD_DIM * half:HEAD_DIM * half + HEAD_DIM],
                                     src[:, :, :, half, :])
                    ins.then_inc(a_v, 1)
                i = s - lead_t
                if 0 <= i < A.n:
                    g = A.first + i
                    a.wait_ge(a_t[0], g + 1)
                    if g >= 2:
                        a.wait_ge(a_pv, g - 1)
                    a.copy(PTB[:, 1024 * (g % 2):1024 * (g % 2) + HALF], bank[PT_BANK[0]][:, :]).then_inc(a_pt[0], 1)
                i = s - lead_s
                if 0 <= i < A.n:
                    g = A.first + i
                    for half in range(2):
                        a.wait_ge(a_sub, 2 * g + half + 1)
                        at = 1024 * (g % 2) + HALF * half
                        a.activation(PB[:, at:at + HALF], PB[:, at:at + HALF], ACT.Exp).then_inc(a_exp, 1)
                i = s - lead_ot
                if 0 <= i < A.n:
                    g = A.first + i
                    a.wait_ge(a_ot, g + 1)
                    if g >= 2:
                        a.wait_ge(a_out, g - 1)
                    a.copy(OTB[:, P * (g % 2):P * (g % 2) + P], bank[OT_BANK][:, 0:P]).then_inc(a_ots, 1)

        def attend_vector(v, o, A):
            for s in range(lead_s, A.n + lead_out + 1):
                i = s - lead_s
                if 0 <= i < A.n:
                    g = A.first + i
                    if g >= 2:
                        v.wait_ge(a_t[1], g - 1)
                    for half in range(2):
                        v.wait_ge(a_s, 2 * g + half + 1)
                        at = 1024 * (g % 2) + HALF * half
                        probs = PB[:, at:at + HALF].rearrange("p (h k) -> p h k", h=8)
                        scores = bank[S_BANK[half]][:, :].rearrange("p (h k) -> p h k", h=8)
                        if A.biased:
                            v.wait_ge(a_bias, i + 1)
                            v.tensor_tensor(probs, scores, bias1[:, i, 8 * half:8 * half + 8, :], ALU.add)\
                                .then_inc(a_biased, 1)
                            v.wait_ge(a_biased, 2 * i + half + 1)
                            scores = probs
                        m = rowmax[:, 8 * half:8 * half + 8]
                        o.link(v.tensor_reduce(m, scores, AX.X, ALU.max))
                        v.tensor_tensor(probs, scores, m[:, :, None].to_broadcast([P, 8, SEQ]), ALU.subtract)\
                            .then_inc(a_sub, 1)
                i = s - lead_t
                if 0 <= i < A.n:
                    g = A.first + i
                    v.wait_ge(a_t[1], g + 1)
                    if g >= 2:
                        v.wait_ge(a_pv, g - 1)
                    v.tensor_copy(PTB[:, 1024 * (g % 2) + HALF:1024 * (g % 2) + 1024], bank[PT_BANK[1]][:, :])\
                        .then_inc(a_pt[1], 1)
                i = s - lead_pv
                if 0 <= i < A.n:
                    g, t, e = A.first + i, i // A.experts, i % A.experts
                    v.wait_ge(a_pv, g + 1)
                    if g >= 2:
                        v.wait_ge(a_ot, g - 1)
                    heads = bank[O_BANK][:, 0:PAIRS_H * V_COLS].rearrange("p (j c) -> p j c", j=PAIRS_H)
                    r = rsum[:, 0:HEADS].rearrange("p (j c) -> p j c", c=2)
                    r2 = rsum[:, HEADS:2 * HEADS].rearrange("p (j c) -> p j c", c=2)
                    if A.biased:
                        o.link(v.tensor_scalar(r2, heads[:, :, 16:18], 1.0, None, ALU.add))
                        o.link(v.reciprocal(r, r2))
                    elif A.experts > 1:
                        o.link(v.reciprocal(r2, heads[:, :, 16:18]))
                        o.link(v.tensor_scalar(r, r2, GATES[:, AE * t + e:AE * t + e + 1], None, ALU.mult))
                    else:
                        o.link(v.reciprocal(r, heads[:, :, 16:18]))
                    shape = [P, PAIRS_H, 2, HEAD_DIM]
                    v.tensor_tensor(ON[:, P * (g % 2):P * (g % 2) + P].rearrange("p (j c d) -> p j c d", j=PAIRS_H, c=2),
                                    heads[:, :, 0:16].rearrange("p j (c d) -> p j c d", c=2),
                                    r[:, :, :, None].to_broadcast(shape), ALU.mult).then_inc(a_on, 1)
                i = s - lead_out - 1
                if 0 <= i < A.n and i % A.experts == A.experts - 1:
                    g, t = A.first + i, i // A.experts
                    v.wait_ge(a_out, g + 1)
                    v.scalar_tensor_tensor(Xt[:, t, :], bank[Y_BANK][:, 0:P], gate[:, A.gate_k:A.gate_k + 1],
                                           Xt[:, t, :], ALU.mult, ALU.add).then_inc(a_x, 1)

        def attend_sync(sp, A):
            for i in range(A.n):
                g = A.first + i
                if A.rope:
                    sp.wait_ge(rope_k, 2)
                else:
                    sp.wait_ge(a_k, g + 1)
                if g >= RING_K:
                    sp.wait_ge(a_s, 2 * (g - RING_K + 1))
                src = KT[:, P * (g % RING_Q):P * (g % RING_Q) + P].rearrange("p (b k) -> p b k", b=2)
                for h in range(HEADS):
                    rows = slice(HEAD_DIM * h, HEAD_DIM * h + HEAD_DIM)
                    sp.dma_start(KBDu[rows, g % RING_K, :, h, :], src[rows]).then_inc(a_kbd[g % RING_K], 16)

        def l1x_vector(v, o):
            norm_vector(v, o, x_tile, h_tile, 2)
            attend_vector(v, o, cross1)

        def l1x_pool(g, o):
            norm_pool(g, o, 2)
            for t in range(TILES):
                shape = [P, HEADS, SEQ]
                o.link(g.tensor_tensor(bias1[:, t], ND[:, SEQ * t:SEQ * t + SEQ][:, None, :].to_broadcast(shape),
                                       W("slopes")[:, :, None].to_broadcast(shape), ALU.mult))
                g.tensor_tensor(bias1[:, t], bias1[:, t],
                                MADD[:, SEQ * t:SEQ * t + SEQ][:, None, :].to_broadcast(shape), ALU.add)\
                    .then_inc(a_bias, 1)

        r_h, r_turned, r_relu, r_logits, r_sub, r_exp = (sem("r_h"), sem("r_turned"), sem("r_relu"), sem("r_logits"),
                                                         sem("r_sub"), sem("r_exp"))
        r_gates, r_gt, r_ob, r_ready = sem("r_gates"), sem("r_gt"), sem("r_ob"), sem("r_ready")
        r1 = SCR[:, 0:512]
        r1t = SCR[0:AE_HID, 512:1536]
        lg = SCR[:, 1536:1600]
        lge = SCR[:, 1600:1664]
        msk = SCR[:, 1664:1728]
        m8 = SCR[:, 1728:1792]

        def pick(v, o, logits, n, top, sub_sem, exp_sem, out, buf):
            lt, et, mt = (x.rearrange("p (t e) -> p t e", t=TILES) for x in buf[0:3])
            m8t = buf[3].rearrange("p (t e) -> p t e", t=TILES)
            o.link(v.tensor_copy(lt, logits))
            for t in range(TILES):
                o.mark(v.max(m8t[:, t, :], lt[:, t, :]))
            o.settle()
            o.mark(v.tensor_tensor(mt, lt, m8t[:, :, top - 1:top].to_broadcast([P, TILES, n]), ALU.is_ge))
            v.tensor_tensor(et, lt, m8t[:, :, 0:1].to_broadcast([P, TILES, n]), ALU.subtract).then_inc(sub_sem, 1)
            v.wait_ge(exp_sem, 1)
            o.settle()
            o.link(v.tensor_tensor(mt, mt, et, ALU.mult))
            o.link(v.tensor_reduce(rsum[:, 0:TILES], mt, AX.X, ALU.add))
            o.link(v.reciprocal(rsum[:, TILES:2 * TILES], rsum[:, 0:TILES]))
            return v.tensor_tensor(out, mt, rsum[:, TILES:2 * TILES, None].to_broadcast([P, TILES, n]), ALU.mult)

        def l1f_vector(v, o):
            norm_vector(v, o, x_tile, h_tile, 3)
            v.tensor_scalar(qb_scaled[:, :], W("e_qb"), SCALE8, None, ALU.mult).then_inc(r_ob, 1)
            v.wait_ge(r_h, 1)
            norm_vector(v, o, lambda t: bank[2][:, AE_HID * t:AE_HID * (t + 1)],
                        lambda t: r1[:, AE_HID * t:AE_HID * (t + 1)], 4)
            v.wait_ge(r_logits, 1)
            gt = GATES[:, :].rearrange("p (t e) -> p t e", t=TILES)
            pick(v, o, bank[3][:, 0:TILES * AE].rearrange("p (t e) -> p t e", t=TILES), AE, 2, r_sub, r_exp, gt,
                 (lg, lge, msk, m8)).then_inc(r_gates, 1)
            v.wait_ge(r_gates, 1)
            attend_vector(v, o, moe)

        def l1f_tensor(pe):
            turn_tensor(pe, h_tile, 3)
            pe.wait_ge(ht_ready, 8)
            for t in range(TILES):
                out = bank[2][:, AE_HID * t:AE_HID * (t + 1)]
                pe.matmul(out, ht(t), W("r_w1"), start=True, stop=False)
                ins = pe.matmul(out, W("ones", rows=1), W("rows", row_at["rb1"], AE_HID, rows=1), start=False, stop=True)
            ins.then_inc(r_h, 1)
            for e in range(AE):
                pe.matmul(bank[6][0:AE, 0:P], W("e_vb", AE * e, AE), W("e_o", P * e, P), start=(e == 0), stop=False)
            pe.matmul(bank[6][0:AE, 0:P], W("ident", 0, AE, rows=AE), W("e_ob", rows=AE), start=False, stop=True)\
                .then_inc(r_turned, 1)
            for t in range(TILES):
                pe.wait_ge(normed, TILES * 4 + t + 1)
                ins = pe.transpose(bank[4 + t // 4][0:AE_HID, P * (t % 4):P * (t % 4) + P],
                                   r1[:, AE_HID * t:AE_HID * (t + 1)], ident)
                if t % 4 == 3:
                    ins.then_inc(r_turned, 1)
            for t in range(TILES):
                pe.wait_ge(r_relu, t // 4 + 1)
                out = bank[3][:, AE * t:AE * (t + 1)]
                pe.matmul(out, r1t[:, P * t:P * t + P], W("r_w2", rows=AE_HID), start=True, stop=False)
                ins = pe.matmul(out, W("ones", rows=1), W("rows", row_at["rb2"], AE, rows=1), start=False, stop=True)
            ins.then_inc(r_logits, 1)
            pe.wait_ge(r_gates, 1)
            for t in range(TILES):
                ins = pe.transpose(bank[4 + t // 4][0:AE, P * (t % 4):P * (t % 4) + P],
                                   GATES[:, AE * t:AE * (t + 1)], ident)
                if t % 4 == 3:
                    ins.then_inc(r_gt, 1)
            pe.wait_ge(r_ready, 3)
            attend_tensor(pe, moe)

        def l1f_scalar(a):
            turn_scalar(a, 3)
            a.wait_ge(r_turned, 1)
            a.copy(OB[0:AE, :], bank[6][0:AE, 0:P]).then_inc(r_ready, 1)
            for j in range(2):
                a.wait_ge(r_turned, j + 2)
                a.activation(r1t[:, HALF * j:HALF * j + HALF], bank[4 + j][0:AE_HID, :], ACT.Relu,
                             bias=W("r_b", rows=AE_HID), scale=W("r_g", rows=AE_HID)).then_inc(r_relu, 1)
            a.wait_ge(r_sub, 1)
            a.activation(lge, lge, ACT.Exp).then_inc(r_exp, 1)
            for j in range(2):
                a.wait_ge(r_gt, j + 1)
                a.copy(GT[0:AE, HALF * j:HALF * j + HALF], bank[4 + j][0:AE, :]).then_inc(r_ready, 1)
            a.wait_ge(r_ob, 1)
            attend_scalar(a, moe)

        rp, rp_a, rp_b = sem("rp"), sem("rp_a"), sem("rp_b")
        t_cos = SCR[:, 0:1024]
        t_sin = SCR[:, 1024:2048]

        def l2x_tensor(pe):
            for r in range(4):
                src, half = ("k", r) if r < 2 else ("q", r - 2)
                if r == 2:
                    turn_tensor(pe, h_tile, 5)
                    pe.wait_ge(ht_ready, 10)
                if r >= 2:
                    pe.wait_ge(rp_b, r - 1)
                rhs = (CT if src == "k" else HT)[:, HALF * half:HALF * half + HALF]
                pe.matmul(bank[2 + 2 * (r % 2)][:, :], W(f"a2_{src}"), rhs, start=True, stop=True)
                pe.matmul(bank[3 + 2 * (r % 2)][:, :], W(f"a2_{src}p"), rhs, start=True, stop=True).then_inc(rp, 1)
            pe.wait_ge(rp_b, 4)
            attend_tensor(pe, cross2)

        def l2x_vector(v, o):
            norm_vector(v, o, x_tile, h_tile, 5)
            for r in range(4):
                src = "k" if r < 2 else "q"
                v.wait_ge(rp, r + 1)
                if r >= 2:
                    v.wait_ge(rope_k, r - 1)
                at = HALF * (r % 2)
                shape = [P, 8, SEQ]

                def by_batch(x):
                    return x.rearrange("p (b s) -> p b s", b=8)

                o.mark(v.tensor_tensor(by_batch(t_cos[:, at:at + HALF]), by_batch(bank[2 + 2 * (r % 2)][:, :]),
                                       W(f"cos{src}")[:, None, :].to_broadcast(shape), ALU.mult))
                o.settle()
                v.tensor_tensor(by_batch(t_sin[:, at:at + HALF]), by_batch(bank[3 + 2 * (r % 2)][:, :]),
                                W(f"sin{src}")[:, None, :].to_broadcast(shape), ALU.mult).then_inc(rp_b, 1)
            attend_vector(v, o, cross2)

        def l2x_pool(g, o):
            norm_pool(g, o, 5)
            for r in range(4):
                g.wait_ge(rp_b, r + 1)
                at = HALF * (r % 2)
                dst, ready = (KT, rope_k) if r < 2 else (QT, rope_q)
                g.tensor_tensor(dst[:, at:at + HALF], t_cos[:, at:at + HALF], t_sin[:, at:at + HALF], ALU.add)\
                    .then_inc(ready, 1)

        f_logits, f_sub, f_exp, f_comb, f_ct, f_ctr = (sem("f_logits"), sem("f_sub"), sem("f_exp"), sem("f_comb"),
                                                       sem("f_ct"), sem("f_ctr"))
        f_h, f_silu, f_gated, f_act, f_out = sem("f_h"), sem("f_silu"), sem("f_gated"), sem("f_act"), sem("f_out")
        act_t = SCR[:, 0:PAIRS * 1024].rearrange("p (e t) -> p e t", e=PAIRS)
        silu = SCR[:, 9216:10240]
        gated = SCR[:, 10240:11264]
        comb_t = SCR[:, 11264:12288]
        comb = SCR[:, 12288:13312].rearrange("p (t e) -> p t e", t=TILES)
        flg, fle, fmk, fm8 = SCR[:, 13312:13440], SCR[:, 13440:13568], SCR[:, 13568:13696], SCR[:, 13696:13760]

        pick_row = KT

        def l2f_vector(v, o):
            o.mark(v.memset(SCR[:, 12288:13312], 0.0))
            o.mark(v.tensor_copy(KT[:, :].rearrange("p (r c) -> p r c", c=SEQ),
                                 ident[:, 0:BATCH, None].to_broadcast([P, BATCH, SEQ])))
            o.settle()
            norm_vector(v, o, x_tile, h_tile, 6)
            v.wait_ge(f_logits, 1)
            pick(v, o, bank[2][:, 0:TILES * FE].rearrange("p (t e) -> p t e", t=TILES), FE, FE_TOP, f_sub, f_exp,
                 comb[:, :, 0:FE], (flg, fle, fmk, fm8)).then_inc(f_comb, 1)
            for r in range(2 * PAIRS):
                e, half = r // 2, r % 2
                at = HALF * (r % 2)
                dst = act_t[:, e, HALF * half:HALF * half + HALF]
                shared = e == PAIRS - 1
                v.wait_ge(f_silu, r + 1)
                g_ = dst if shared else gated[:, at:at + HALF]
                ins = v.tensor_tensor(g_, bank[2 + r % 2][:, :], silu[:, at:at + HALF], ALU.mult)
                ins.then_inc(f_gated, 1)
                if not shared:
                    v.wait_ge(f_gated, r + 1)
                    v.tensor_tensor(dst, bank[4 + r % 2][:, :], g_, ALU.mult).then_inc(f_act, 1)
            for j in range(2):
                v.wait_ge(f_out, j + 1)
                add_to_x(v, 5, j, bank[6 + j][:, :])

        def l2f_tensor(pe):
            turn_tensor(pe, h_tile, 6)
            pe.wait_ge(ht_ready, 12)
            for t in range(TILES):
                ins = pe.matmul(bank[2][:, FE * t:FE * (t + 1)], ht(t), W("f_gate"), start=True, stop=True)
            ins.then_inc(f_logits, 1)
            pe.wait_ge(f_comb, 1)
            for t in range(TILES):
                ins = pe.transpose(bank[6 + t // 4][:, P * (t % 4):P * (t % 4) + P], comb[:, t, :], ident)
                if t % 4 == 3:
                    ins.then_inc(f_ct, 1)
            pe.wait_ge(f_ctr, 2)
            for r in range(2 * PAIRS):
                e, half = r // 2, r % 2
                rhs = HT[:, HALF * half:HALF * half + HALF]
                if r >= 2:
                    pe.wait_ge(f_gated, r - 1)
                pe.matmul(bank[r % 2][:, :], W("f_w1", P * e, P), rhs, start=True, stop=True)
                pe.matmul(bank[2 + r % 2][:, :], W("f_w3", P * e, P), rhs, start=True, stop=True).then_inc(f_h, 1)
                if e < PAIRS - 1:
                    if r >= 2:
                        pe.wait_ge(f_act, r - 1)
                    pe.matmul(bank[4 + r % 2][:, :], pick_row[:, P * e:P * e + P], comb_t[:, HALF * half:HALF * half + HALF],
                              start=True, stop=True).then_inc(f_crep, 1)
            pe.wait_ge(f_gated, 2 * PAIRS)
            pe.wait_ge(f_act, 2 * (PAIRS - 1))
            for t in range(TILES):
                for e in range(PAIRS):
                    ins = pe.matmul(bank[6 + t // 4][:, P * (t % 4):P * (t % 4) + P], act_t[:, e, P * t:P * t + P],
                                    W("f_w2", P * e, P), start=(e == 0), stop=(e == PAIRS - 1))
                if t % 4 == 3:
                    ins.then_inc(f_out, 1)

        f_crep = sem("f_crep")

        def l2f_scalar(a):
            turn_scalar(a, 5)
            a.wait_ge(f_sub, 1)
            a.activation(fle, fle, ACT.Exp).then_inc(f_exp, 1)
            for j in range(2):
                a.wait_ge(f_ct, j + 1)
                a.copy(comb_t[:, HALF * j:HALF * j + HALF], bank[6 + j][:, :]).then_inc(f_ctr, 1)
            for r in range(2 * PAIRS):
                at = HALF * (r % 2)
                a.wait_ge(f_h, r + 1)
                if r < 2 * (PAIRS - 1):
                    a.wait_ge(f_crep, r + 1)
                if r >= 2:
                    a.wait_ge(f_gated, r - 1)
                a.activation(silu[:, at:at + HALF], bank[r % 2][:, :], ACT.Silu).then_inc(f_silu, 1)

        cat_t = SCR[:, 0:2048].rearrange("p (b j) -> p b j", b=BATCH)
        qq = SCR[:, 2048:3072]
        kk = SCR[:, 3072:5120]
        vv = SCR[:, 5120:7200].rearrange("p (b h c) -> p b h c", b=BATCH, h=L_HEADS)
        kt3 = SCR[:, 7200:9248].rearrange("p (b j) -> p b j", b=BATCH)
        pp = SCR[:, 9248:11296]
        ptt = SCR[:, 11296:13344].rearrange("p (h t q) -> p h t q", h=L_HEADS, t=TILES)
        h2 = SCR[:, 13344:14368].rearrange("p (t d) -> p t d", t=TILES)
        h3 = SCR[:, 14368:15392].rearrange("p (t d) -> p t d", t=TILES)
        sq3 = KBD[:, 0:3072]
        ss = KBD[:, 3072:3120]
        ssc = KBD[:, 3120:3168]
        rr = KBD[:, 3168:3216]
        madd3 = KBD[:, 3216:3472]
        qt3 = KBD[:, 3584:4608]
        on3 = KBD[:, 4608:5632]
        ot3 = KBD[:, 5632:6656]
        max3 = KBD[:, 6656:6672]
        inv3 = KBD[:, 6672:6688]
        l_cat, l_q, l_kv, l_qq, l_kk, l_sq, l_rn = (sem("l_cat"), sem("l_q"), sem("l_kv"), sem("l_qq"), sem("l_kk"),
                                                     sem("l_sq"), sem("l_rn"))
        l_qkn, l_turn, l_qkt, l_s, l_sub, l_exp = (sem("l_qkn"), sem("l_turn"), sem("l_qkt"), sem("l_s"), sem("l_sub"),
                                                   sem("l_exp"))
        l_pt, l_ptt, l_o, l_on, l_ot, l_ots, l_y, l_mask = (sem("l_pt"), sem("l_ptt"), sem("l_o"), sem("l_on"),
                                                            sem("l_ot"), sem("l_ots"), sem("l_y"), sem("l_mask"))

        def l3x_vector(v, o):
            norm_vector(v, o, x_tile, h_tile, 7)
            v.wait_ge(normed, 8 * TILES)
            norm_vector(v, o, h_tile, lambda t: h2[:, t, :], 8)
            v.wait_ge(in_ctx, 32)
            norm_vector(v, o, lambda t: Ct[:, t, :], lambda t: h3[:, t, :], 9)
            m3 = madd3.rearrange("p (h j) -> p h j", h=L_HEADS)
            o.link(v.memset(madd3, 0.0))
            for h in range(L_HEADS):
                ins = v.tensor_scalar(m3[0:BATCH, h, 0:SEQ], keep[0:BATCH, :], 0.0, MASKED, ALU.is_equal, ALU.mult)
            ins.then_inc(l_mask, 1)
            o.mark(v.memset(vv[:, :, :, L_DIM:L_DIM + 1], 1.0))
            v.wait_ge(l_qq, 2)
            o.mark(v.tensor_tensor(sq3[:, 0:1024], qq, qq, ALU.mult))
            v.wait_ge(l_kk, 8)
            o.mark(v.tensor_tensor(sq3[:, 1024:3072], kk, kk, ALU.mult))
            o.settle()
            o.link(v.tensor_reduce(ss, sq3.rearrange("p (g d) -> p g d", d=L_DIM), AX.X, ALU.add))
            v.tensor_scalar(ssc, ss, 1.0 / L_DIM, 1e-16, ALU.mult, ALU.max).then_inc(l_sq, 1)
            v.wait_ge(l_rn, 1)
            o.link(v.tensor_scalar(rr[:, 0:16], rr[:, 0:16], float(L_DIM ** -0.5), None, ALU.mult))
            for src, at, n in ((qq, 0, 16), (kk, 16, 32)):
                x = src.rearrange("p (g d) -> p g d", d=L_DIM)
                v.tensor_tensor(x, x, rr[:, at:at + n, None].to_broadcast([P, n, L_DIM]), ALU.mult).then_inc(l_qkn, 1)
            p3 = pp.rearrange("p (h t j) -> p h t j", h=L_HEADS, t=TILES)
            for r in range(4):
                h, part = r % 2, r // 2
                v.wait_ge(l_s, part + 1)
                s3 = bank[r][:, :].rearrange("p (t j) -> p t j", t=4)
                m = max3[:, 4 * r:4 * r + 4]
                o.link(v.tensor_reduce(m, s3, AX.X, ALU.max))
                v.tensor_tensor(p3[:, h, 4 * part:4 * part + 4, :], s3, m[:, :, None].to_broadcast([P, 4, KEYS]),
                                ALU.subtract).then_inc(l_sub, 1)
            for t in range(TILES):
                v.wait_ge(l_o, t // 2 + 1)
                o3 = bank[t // 2][:, 130 * (t % 2):130 * (t % 2) + 130].rearrange("p (h c) -> p h c", h=L_HEADS)
                r_ = inv3[:, 2 * t:2 * t + 2]
                o.link(v.reciprocal(r_, o3[:, :, L_DIM]))
                v.tensor_tensor(on3[:, P * t:P * t + P].rearrange("p (h d) -> p h d", h=L_HEADS), o3[:, :, 0:L_DIM],
                                r_[:, :, None].to_broadcast([P, L_HEADS, L_DIM]), ALU.mult).then_inc(l_on, 1)
            for j in range(2):
                v.wait_ge(l_y, j + 1)
                add_to_x(v, 6, j, bank[6 + j][:, :])

        def l3x_pool(g, o):
            norm_pool(g, o, 7)
            norm_pool(g, o, 8)
            norm_pool(g, o, 9)
            g.wait_ge(l_sq, 1)
            g.tensor_tensor(rr, ssc, neghalf[:, 0:48], ALU.pow).then_inc(l_rn, 1)

        def l3x_tensor(pe):
            for n, src in ((8, h2), (9, h3)):
                turn_tensor(pe, lambda t, s_=src: s_[:, t, :], n, banks=(0, 1) if n == 8 else (2, 3))
            pe.wait_ge(l_cat, 4)
            for t in range(TILES):
                for b in range(2):
                    ins = pe.matmul(bank[t // 4][SEQ * b:SEQ * b + SEQ, P * (t % 4):P * (t % 4) + P],
                                    cat_t[:, 2 * t + b, SEQ:KEYS], W("l3_q"), start=True, stop=True)
                if t % 4 == 3:
                    ins.then_inc(l_q, 1)
            for b in range(BATCH):
                r = b // 2
                if b % 2 == 0 and r >= 4:
                    pe.wait_ge(l_kk, r - 3)
                ins = pe.matmul(bank[4 + r % 4][:, 2 * P * (b % 2):2 * P * (b % 2) + 2 * P], cat_t[:, b, :],
                                W("l3_kv"), start=True, stop=True)
                if b % 2 == 1:
                    ins.then_inc(l_kv, 1)
            for r in range(6):
                if r == 0:
                    pe.wait_ge(l_qkn, 1)
                if r == 2:
                    pe.wait_ge(l_qkn, 2)
                src = qq if r < 2 else kk
                for j in range(4):
                    at = P * (4 * (r if r < 2 else r - 2) + j)
                    ins = pe.transpose(bank[r][:, P * j:P * j + P], src[:, at:at + P], ident)
                ins.then_inc(l_turn, 1)
            pe.wait_ge(l_qkt, 6)
            pe.wait_ge(l_mask, 1)
            for part in range(2):
                for t in range(4 * part, 4 * part + 4):
                    for h in range(L_HEADS):
                        out = bank[2 * part + h][:, KEYS * (t % 4):KEYS * (t % 4) + KEYS]
                        pe.matmul(out, pick_row[0:BATCH, P * t:P * t + P], madd3[0:BATCH, KEYS * h:KEYS * h + KEYS],
                                  start=True, stop=False)
                        for b in range(2):
                            rows = slice(L_DIM * h, L_DIM * h + L_DIM)
                            ins = pe.matmul(out[SEQ * b:SEQ * b + SEQ, :],
                                            qt3[rows, P * t + SEQ * b:P * t + SEQ * b + SEQ],
                                            kt3[rows, 2 * t + b, :], start=False, stop=True)
                ins.then_inc(l_s, 1)
            for r in range(4):
                h, part = r % 2, r // 2
                pe.wait_ge(l_exp, r + 1)
                for j in range(4):
                    at = 1024 * h + HALF * part + P * j
                    ins = pe.transpose(bank[4 + r][:, P * j:P * j + P], pp[:, at:at + P], ident)
                ins.then_inc(l_pt, 1)
            pe.wait_ge(l_ptt, 4)
            for t in range(TILES):
                for h in range(L_HEADS):
                    for b in range(2):
                        at = 130 * (t % 2) + 65 * h
                        ins = pe.matmul(bank[t // 2][SEQ * b:SEQ * b + SEQ, at:at + 65],
                                        ptt[:, h, t, SEQ * b:SEQ * b + SEQ], vv[:, 2 * t + b, h, :],
                                        start=True, stop=True)
                if t % 2 == 1:
                    ins.then_inc(l_o, 1)
            for t in range(TILES):
                pe.wait_ge(l_on, t + 1)
                ins = pe.transpose(bank[4 + t // 4][:, P * (t % 4):P * (t % 4) + P], on3[:, P * t:P * t + P], ident)
                if t % 4 == 3:
                    ins.then_inc(l_ot, 1)
            for t in range(TILES):
                pe.wait_ge(l_ots, t // 4 + 1)
                out = bank[6 + t // 4][:, P * (t % 4):P * (t % 4) + P]
                pe.matmul(out, ot3[:, P * t:P * t + P], W("l3_o"), start=True, stop=False)
                ins = pe.matmul(out, W("ones", rows=1), W("rows", row_at["b3"], P, rows=1), start=False, stop=True)
                if t % 4 == 3:
                    ins.then_inc(l_y, 1)

        def l3x_scalar(a):
            for n in range(2):
                for j in range(2):
                    a.wait_ge(turned, 2 * (6 + n) + j + 1)
                    g_, b_ = (W("l_g"), W("l_b")) if n == 0 else (W("x_g"), W("x_b"))
                    dst = cat_t[:, 8 * j:8 * j + 8, SEQ * (1 - n):SEQ * (2 - n)]
                    a.activation(dst, bank[2 * n + j][:, :].rearrange("p (b s) -> p b s", b=8), ACT.Identity,
                                 bias=b_, scale=g_).then_inc(l_cat, 1)
            for j in range(2):
                a.wait_ge(l_q, j + 1)
                a.copy(qq[:, HALF * j:HALF * j + HALF], bank[j][:, :]).then_inc(l_qq, 1)
            for r in range(8):
                a.wait_ge(l_kv, r + 1)
                src = bank[4 + r % 4][:, :].rearrange("p (b c) -> p b c", b=2)
                a.copy(vv[:, 2 * r:2 * r + 2, :, 0:L_DIM],
                       src[:, :, P:2 * P].rearrange("p b (h d) -> p b h d", h=L_HEADS))
                a.copy(kk[:, 2 * P * r:2 * P * r + 2 * P].rearrange("p (b c) -> p b c", b=2), src[:, :, 0:P])\
                    .then_inc(l_kk, 1)
            for r in range(6):
                a.wait_ge(l_turn, r + 1)
                dst = qt3[:, HALF * r:HALF * r + HALF] if r < 2 else \
                    SCR[:, 7200 + HALF * (r - 2):7200 + HALF * (r - 1)]
                a.mul(dst, bank[r][:, :], W("q_gamma") if r < 2 else W("k_gamma")).then_inc(l_qkt, 1)
            for r in range(4):
                h, part = r % 2, r // 2
                at = 1024 * h + HALF * part
                a.wait_ge(l_sub, r + 1)
                a.activation(pp[:, at:at + HALF], pp[:, at:at + HALF], ACT.Exp).then_inc(l_exp, 1)
            for r in range(4):
                h, part = r % 2, r // 2
                a.wait_ge(l_pt, r + 1)
                a.copy(ptt[:, h, 4 * part:4 * part + 4, :].rearrange("p t q -> p (t q)"), bank[4 + r][:, :])\
                    .then_inc(l_ptt, 1)
            for j in range(2):
                a.wait_ge(l_ot, j + 1)
                a.copy(ot3[:, HALF * j:HALF * j + HALF], bank[4 + j][:, :]).then_inc(l_ots, 1)

        b_abs, b_sum, b_scale, b_tern = sem("b_abs"), sem("b_sum"), sem("b_scale"), sem("b_tern")
        b_t1, b_t1s, b_m, b_w, b_h, b_relu, b_r2, b_y = (sem("b_t1"), sem("b_t1s"), sem("b_m"), sem("b_w"), sem("b_h"),
                                                         sem("b_relu"), sem("b_r2"), sem("b_y"))
        b_abs2, b_sum2, b_wp = sem("b_abs2"), sem("b_sum2"), sem("b_wp")
        wabs = SCR[:, 0:512]
        wscale = SCR[:, 512:1024]
        whalf = SCR[:, 1024:1536]
        wneg = SCR[:, 1536:2048]
        weff = SCR[:, 2048:2560]
        pabs = SCR[:, 2560:3072]
        pscale = SCR[:, 3072:3200]
        phalf = SCR[:, 3200:3328]
        pneg = SCR[:, 3328:3840]
        peff = SCR[:, 3840:4352]
        t1 = SCR[0:RANK, 4352:4864]
        rl = SCR[:, 5120:6144]
        r2 = SCR[:, 6144:10240].rearrange("p (c t) -> p c t", c=CHUNKS)

        def l3f_vector(v, o):
            norm_vector(v, o, x_tile, h_tile, 10)

            def ternary(w, total, n, scale, half, neg, out, shape=None):
                def s(x):
                    return x if shape is None else x[:, None, :].to_broadcast(shape)
                o.link(v.tensor_scalar(scale, total, 1.0 / n, 1e-5, ALU.mult, ALU.max))
                o.link(v.tensor_scalar(half, scale, -0.5, None, ALU.mult))
                o.link(v.tensor_tensor(neg, w, s(half), ALU.is_lt))
                o.link(v.tensor_scalar(half, scale, 0.5, None, ALU.mult))
                o.link(v.tensor_tensor(out, w, s(half), ALU.is_gt))
                o.link(v.tensor_tensor(out, out, neg, ALU.subtract))
                return v.tensor_tensor(out, out, s(scale), ALU.mult)

            v.wait_ge(b_sum, 1)
            o.link(ternary(W("b_fc"), bank[2][:, :], P, wscale, whalf, wneg, weff))
            v.wait_ge(b_m, 1)
            v.scalar_tensor_tensor(weff, bank[3][:, :], W("b_gate"), weff, ALU.mult, ALU.add).then_inc(b_w, 1)
            v.wait_ge(b_sum2, 1)
            shape = [P, CHUNKS, P]

            def by_chunk(x):
                return x.rearrange("p (c d) -> p c d", c=CHUNKS)

            ternary(by_chunk(W("b_proj")), bank[4][:, 0:P], HIDDEN, pscale, phalf, by_chunk(pneg), by_chunk(peff), shape)\
                .then_inc(b_wp, 1)
            for r in range(2 * CHUNKS):
                c, half = r // 2, r % 2
                at = HALF * (r % 2)
                v.wait_ge(b_relu, r + 1)
                v.tensor_tensor(r2[:, c, HALF * half:HALF * half + HALF], rl[:, at:at + HALF], rl[:, at:at + HALF],
                                ALU.mult).then_inc(b_r2, 1)
            for j in range(2):
                v.wait_ge(b_y, j + 1)
                add_to_x(v, 7, j, bank[6 + j][:, :]).then_inc(final_x, 1)

        final_x = sem("final_x")

        def l3f_tensor(pe):
            pe.wait_ge(b_abs, 1)
            pe.matmul(bank[2][:, :], W("ones"), wabs, start=True, stop=True).then_inc(b_sum, 1)
            pe.matmul(bank[3][0:RANK, :], W("b_fb", rows=RANK), W("b_ut", rows=RANK), start=True, stop=True)\
                .then_inc(b_t1, 1)
            pe.wait_ge(b_abs, 2)
            for c in range(CHUNKS):
                ins = pe.matmul(bank[4][:, 0:P], W("ones"), pabs[:, P * c:P * c + P], start=(c == 0), stop=(c == 3))
            ins.then_inc(b_sum2, 1)
            pe.wait_ge(b_t1s, 1)
            pe.matmul(bank[3][:, :], W("b_v", rows=RANK), t1, start=True, stop=True).then_inc(b_m, 1)
            turn_tensor(pe, h_tile, 10)
            pe.wait_ge(b_w, 1)
            for r in range(2 * CHUNKS):
                c, half = r // 2, r % 2
                pe.wait_ge(ht_ready, 12 + half + 1)
                if r >= 2:
                    pe.wait_ge(b_relu, r - 1)
                out = bank[(2, 3)[r % 2]]
                pe.matmul(out[:, :], weff[:, P * c:P * c + P], HT[:, HALF * half:HALF * half + HALF],
                          start=True, stop=True).then_inc(b_h, 1)
            pe.wait_ge(b_wp, 1)
            pe.wait_ge(b_r2, 2 * CHUNKS)
            for t in range(TILES):
                for c in range(CHUNKS):
                    ins = pe.matmul(bank[6 + t // 4][:, P * (t % 4):P * (t % 4) + P], r2[:, c, P * t:P * t + P],
                                    peff[:, P * c:P * c + P], start=(c == 0), stop=(c == CHUNKS - 1))
                if t % 4 == 3:
                    ins.then_inc(b_y, 1)

        def l3f_scalar(a):
            a.activation(wabs, W("b_fc"), ACT.Abs).then_inc(b_abs, 1)
            a.activation(pabs, W("b_proj"), ACT.Abs).then_inc(b_abs, 1)
            a.wait_ge(b_t1, 1)
            a.copy(t1, bank[3][0:RANK, :]).then_inc(b_t1s, 1)
            turn_scalar(a, 8)
            for r in range(2 * CHUNKS):
                at = HALF * (r % 2)
                a.wait_ge(b_h, r + 1)
                if r >= 2:
                    a.wait_ge(b_r2, r - 1)
                a.activation(rl[:, at:at + HALF], bank[(2, 3)[r % 2]][:, :], ACT.Relu).then_inc(b_relu, 1)

        cross1.ht_need, moe.ht_need, cross2.ht_need = 4, 6, 8

        block = ctx.enter_context(nc.Block())

        @block.sync
        def _(sp):
            ends = [0] + group_ends()

            def load_pack(g):
                sp.dma_start(pack[:, ends[g]:ends[g + 1]], d_pack[:, ends[g]:ends[g + 1]]).then_inc(in_pack[g], 16)

            sp.dma_start(Xt, d_x.rearrange("(t p) d -> p t d", p=P)).then_inc(in_x, 16)
            load_pack(0)
            sp.dma_start(CT[:, :], d_ctxt).then_inc(in_ctx, 16)
            sp.dma_start(gates_in[:, :], d_gates).then_inc(in_small, 16)
            load_pack(1)
            sp.dma_start(qpos[:, :], d_qpos).then_inc(in_small, 16)
            sp.dma_start(kpos[:, :], d_kpos).then_inc(in_small, 16)
            sp.dma_start(mask[:, :], d_mask).then_inc(in_small, 16)
            sp.dma_start(keep[0:BATCH, :], d_keep).then_inc(in_small, 16)
            for g in range(2, len(GROUPS)):
                load_pack(g)
            for k in range(8):
                if k < layers:
                    if k == 2:
                        attend_sync(sp, cross1)
                    if k == 3:
                        attend_sync(sp, moe)
                    if k == 4:
                        attend_sync(sp, cross2)
                    if k == 6:
                        sp.dma_start(Ct, d_ctx.rearrange("(t p) d -> p t d", p=P)).then_inc(in_ctx, 16)
                for g in first_use.get(k + 1, ()):
                    sp.wait_ge(in_pack[g], 16)
                end_layer(sp, k)
            sp.dma_start(d_out.rearrange("(t p) d -> p t d", p=P), Xt).then_inc(out_stored, 16)
            sp.wait_ge(out_stored, 16)

        @block.gpsimd
        def _(g):
            o = Order(g, "pool")
            g.memset(neghalf[:, :], -0.5).then_inc(consts, 1)
            g.wait_ge(consts, 1)
            for k in range(8):
                if k < layers:
                    if k == 0:
                        norm_pool(g, o, 0)
                        g.memset(KBD[:, 0:4096], 0.0).then_inc(zeroed, 1)
                        g.memset(KBD[:, 4096:8192], 0.0).then_inc(zeroed, 1)
                        g.memset(VM[:, :], 0.0).then_inc(zeroed, 1)
                        g.wait_ge(zeroed, 3)
                        vb = VM[:, :].rearrange("p (x c) -> p x c", c=V_COLS)
                        g.memset(vb[0:SEQ, :, 16:17], 1.0).then_inc(zeroed, 1)
                        g.memset(vb[SEQ:P, :, 17:18], 1.0).then_inc(zeroed, 1)
                    elif k == 1:
                        l0f_pool(g, o)
                    elif k == 2:
                        l1x_pool(g, o)
                    elif k == 3:
                        norm_pool(g, o, 3)
                        norm_pool(g, o, 4)
                    elif k == 4:
                        l2x_pool(g, o)
                    elif k == 5:
                        norm_pool(g, o, 6)
                    elif k == 6:
                        l3x_pool(g, o)
                    elif k == 7:
                        norm_pool(g, o, 10)
                end_layer(g, k)

        @block.scalar
        def _(a):
            a.wait_ge(in_small, 16 * 5)
            a.activation(gate[:, :], gates_in[:, :], ACT.Tanh).then_inc(gate_ready, 1)
            for k in range(8):
                if k < layers:
                    if k == 0:
                        turn_scalar(a, 0)
                    elif k == 1:
                        turn_scalar(a, 1)
                        l0f_scalar(a)
                    elif k == 2:
                        turn_scalar(a, 2)
                        attend_scalar(a, cross1)
                    elif k == 3:
                        l1f_scalar(a)
                    elif k == 4:
                        turn_scalar(a, 4)
                        attend_scalar(a, cross2)
                    elif k == 5:
                        l2f_scalar(a)
                    elif k == 6:
                        l3x_scalar(a)
                    elif k == 7:
                        l3f_scalar(a)
                end_layer(a, k)

        @block.tensor
        def _(pe):
            for k in range(8):
                if k < layers:
                    if k == 0:
                        l0x_tensor(pe)
                    elif k == 1:
                        turn_tensor(pe, h_tile, 1)
                        l0f_tensor(pe)
                    elif k == 2:
                        turn_tensor(pe, h_tile, 2)
                        attend_tensor(pe, cross1)
                    elif k == 3:
                        l1f_tensor(pe)
                    elif k == 4:
                        l2x_tensor(pe)
                    elif k == 5:
                        l2f_tensor(pe)
                    elif k == 6:
                        l3x_tensor(pe)
                    elif k == 7:
                        l3f_tensor(pe)
                end_layer(pe, k)

        @block.vector
        def _(v):
            o = Order(v, "vector")
            for k in range(8):
                if k < layers:
                    if k == 0:
                        l0x_vector(v, o)
                        v.wait_ge(in_small, 16 * 5)
                        o.link(v.tensor_copy(qposf[:, :], qpos[:, :]))
                        for t in range(TILES):
                            o.mark(v.tensor_scalar(ND[:, SEQ * t:SEQ * t + SEQ], kpos[:, SEQ * t:SEQ * t + SEQ],
                                                   qposf[:, t:t + 1], None, ALU.subtract))
                        o.mark(v.tensor_scalar(MADD[:, :], mask, 0.0, MASKED, ALU.is_equal, ALU.mult))
                    elif k == 1:
                        l0f_vector(v, o)
                    elif k == 2:
                        l1x_vector(v, o)
                    elif k == 3:
                        l1f_vector(v, o)
                    elif k == 4:
                        l2x_vector(v, o)
                    elif k == 5:
                        l2f_vector(v, o)
                    elif k == 6:
                        l3x_vector(v, o)
                    elif k == 7:
                        l3f_vector(v, o)
                end_layer(v, k)


def lay_out(i):
    f = {k: np.asarray(v) for k, v in i.items()}
    blocks = {}

    def put(name, a, rows=P):
        a = np.asarray(a, np.float32) if a.dtype == np.float32 else a
        full = np.zeros((P, OFFSET[name][1]), np.float32)
        full[0:a.shape[0], 0:a.shape[1]] = a
        blocks[name] = full

    def col(a):
        return a.reshape(-1, 1)

    put("ident", np.eye(P, dtype=np.float32))
    put("w1t", f["L0_xattn_W"][:, :DIM].T)
    put("w2t", f["L0_xattn_W"][:, DIM:].T)
    put("ones", np.ones((P, P), np.float32))
    rows = np.zeros((1, 5 * P), np.float32)
    rows[0, 0:P] = f["L0_xattn_b"]
    rows[0, P:2 * P] = f["L3_xattn_b_out"]
    rows[0, 2 * P:2 * P + AE_HID] = f["L1_ffn_rb1"]
    rows[0, 3 * P:3 * P + AE] = f["L1_ffn_rb2"]
    put("rows", rows)
    put("pk_wq", f["L0_ffn_Wq"])
    put("pk_bq", f["L0_ffn_bq"].reshape(2, P).T)
    put("pk_gamma", col(np.concatenate([f["L0_ffn_bn_gamma"]] * 4)))
    put("pk_beta", col(np.concatenate([f["L0_ffn_bn_beta"]] * 4)))
    keys = np.zeros((4, 2, 16, 4, 2, PK_KEYS), np.float32)
    group = np.zeros((4, 2, 16, 4, 2), np.float32)
    for h in range(4):
        for c, k in enumerate((f["L0_ffn_sub_key0"], f["L0_ffn_sub_key1"])):
            keys[h, c, :, h, c, :] = k.T
            group[h, c, :, h, c] = 1.0
    put("pk_keys", keys.reshape(P, 2 * P))
    put("pk_group", group.reshape(P, 8))
    same = np.equal.outer(np.arange(P) % 32, np.arange(P) % 32)
    put("pk_mean", np.where(same, np.float32(1.0 / PK_HEADS), np.float32(0.0)))
    put("pk_down", f["L0_ffn_expert_down"].T)
    put("pk_up", f["L0_ffn_expert_up"])
    for n, k in (("a1_q", "W_q"), ("a1_k", "W_k"), ("a1_v", "W_v"), ("a1_o", "W_o")):
        put(n, f["L1_xattn_" + k].T)
    ratio = 2.0 ** (-8.0 / HEADS)
    put("slopes", np.tile(np.array([[ratio ** h for h in range(1, HEADS + 1)]], np.float32), (P, 1)))
    put("r_w1", f["L1_ffn_rW1"].T)
    put("r_g", col(f["L1_ffn_ln_g"]))
    put("r_b", col(f["L1_ffn_ln_b"]))
    put("r_w2", f["L1_ffn_rW2"].T)
    put("e_qb", f["L1_ffn_qb"].T)
    put("e_kb", f["L1_ffn_kb"].T)
    vb = np.zeros((P, AE, AE), np.float32)
    for e in range(AE):
        vb[:, e, e] = f["L1_ffn_vb"][e]
    put("e_vb", vb.reshape(P, AE * AE))
    put("e_ob", f["L1_ffn_ob"])
    for n, k in (("e_q", "qW"), ("e_k", "kW"), ("e_v", "vW"), ("e_o", "oW")):
        put(n, f["L1_ffn_" + k].transpose(2, 0, 1).reshape(P, AE * P))
    turn = np.arange(P).reshape(HEADS, 2, HEAD_DIM // 2)[:, ::-1].reshape(P)
    for n, k in (("q", "Wq"), ("k", "Wk")):
        w = f["L2_xattn_" + k]
        put("a2_" + n, w.T)
        put("a2_" + n + "p", w[turn].T)
    put("a2_v", f["L2_xattn_Wv"].T)
    put("a2_o", f["L2_xattn_Wo"].T)
    freq = 1.0 / 10000.0 ** (np.arange(0, HEAD_DIM, 2, dtype=np.float32) / np.float32(HEAD_DIM))
    angle = np.outer(np.arange(SEQ, dtype=np.float32), freq.astype(np.float32)).astype(np.float32)
    cos = np.tile(np.cos(angle).T, (2 * HEADS, 1))
    sin = np.sin(angle).T
    sin = np.tile(np.concatenate([-sin, sin]), (HEADS, 1))
    put("cosq", (cos * SCALE8).astype(np.float32))
    put("sinq", (sin * SCALE8).astype(np.float32))
    put("cosk", cos.astype(np.float32))
    put("sink", sin.astype(np.float32))
    put("f_gate", f["L2_ffn_gate_w"].T)
    for n, k in (("f_w1", "w1"), ("f_w3", "w3")):
        full = np.zeros((P, 2 * PAIRS, FE_HID), np.float32)
        full[:, 0:FE] = f["L2_ffn_" + k].transpose(2, 0, 1)
        full[:, FE] = f["L2_ffn_s" + k].T
        put(n, full.reshape(P, PAIRS * P))
    full = np.zeros((2, FE_HID, PAIRS, P), np.float32)
    full[:, :, 0:FE // 2] = f["L2_ffn_w2"].transpose(0, 2, 1).reshape(FE // 2, 2, FE_HID, P).transpose(1, 2, 0, 3)
    full[0, :, FE // 2] = f["L2_ffn_sw2"].T
    put("f_w2", full.reshape(P, PAIRS * P))
    for n, k in (("x_g", "ln_x_g"), ("x_b", "ln_x_b"), ("l_g", "ln_l_g"), ("l_b", "ln_l_b")):
        put(n, col(f["L3_xattn_" + k]))
    for n in ("q_gamma", "k_gamma"):
        put(n, col(np.concatenate([f["L3_xattn_" + n]] * L_HEADS)))
    put("l3_q", f["L3_xattn_W_q"])
    put("l3_kv", f["L3_xattn_W_kv"])
    put("l3_o", f["L3_xattn_W_out"])
    put("b_fc", f["L3_ffn_w_fc"].T)
    put("b_proj", f["L3_ffn_w_proj"].T.reshape(CHUNKS, P, P).transpose(1, 0, 2).reshape(P, CHUNKS * P))
    put("b_v", f["L3_ffn_v"])
    put("b_ut", f["L3_ffn_u"].T)
    put("b_fb", f["L3_ffn_fast_b"])
    put("b_gate", np.repeat(f["L3_ffn_gate"].reshape(1, 1), P, axis=0))

    context = f["ctx_1024"].reshape(TOKENS, DIM)
    gates = np.stack([f["g_xattn"], f["g_ffn"]], axis=1).reshape(1, 8)
    kpos = np.repeat(f["itok_BxS2_1_8191"][:, None, :], SEQ, axis=1)

    def by_tile(a):
        return np.ascontiguousarray(a.reshape(TILES, P, -1).transpose(1, 0, 2).reshape(P, -1))

    return {
        "x": np.ascontiguousarray(f["x"].reshape(TOKENS, DIM)),
        "ctx": np.ascontiguousarray(context),
        "ctxt": np.ascontiguousarray(context.T),
        "pack": np.concatenate([blocks[n] for n, _ in PACK], axis=1),
        "gates": np.ascontiguousarray(np.repeat(gates, P, axis=0)),
        "qpos": by_tile(f["itok_BxS_8_8191"].astype(np.int32)),
        "kpos": by_tile(kpos.astype(np.int32)),
        "mask": by_tile(f["mask_BxSxS2_if1"].astype(np.int32)),
        "keep": np.ascontiguousarray(f["mask_BxS2_bk0"].astype(np.int32)),
    }


def kernel(**inputs):
    import concourse.bacc as _bacc
    from concourse.bass_utils import run_bass_kernel_spmd as _run

    nc = _bacc.Bacc("TRN2", target_bir_lowering=False, num_devices=1)
    arrays = {f"in_{name}": a for name, a in lay_out(inputs).items()}
    args = [nc.dram_tensor(name, a.shape, mybir.dt.from_np(a.dtype), kind="ExternalInput").ap()
            for name, a in arrays.items()]
    out = nc.dram_tensor("out", (TOKENS, DIM), F32, kind="ExternalOutput").ap()
    build(nc, *args, out)
    r = _run(nc, [arrays], core_ids=[0])
    return r.results[0]["out"].reshape(BATCH, SEQ, DIM)
```

```python
from contextlib import ExitStack

import numpy as np

import concourse.bass as bass
from concourse import mybir

F32 = mybir.dt.float32
I32 = mybir.dt.int32
ACT = mybir.ActivationFunctionType
ALU = mybir.AluOpType
AX = mybir.AxisListType

P = 128
BATCH, SEQ, DIM = 16, 64, 128
TOKENS = BATCH * SEQ
TILES = TOKENS // P
HEADS, HEAD_DIM = 16, 8
HALF = 512
PK_HEADS, PK_KEYS, PK_TOP = 8, 32, 4
PK_EXPERTS = 128
PK_GROUPS = 2 * PK_HEADS
PK_FAR = PK_EXPERTS // PK_KEYS
AE, AE_HID = 8, 64
FE, FE_HID, FE_TOP = 16, 64, 4
PAIRS = FE // 2 + 1
L_HEADS, L_DIM = 2, 64
KEYS = 2 * SEQ
HIDDEN, RANK = 512, 16
CHUNKS = HIDDEN // P
EPS = 1e-5
MASKED = -1e30
SCALE8 = float(HEAD_DIM ** -0.5)
V_COLS = 32
RING_K, RING_Q, RING_V = 4, 8, 5
PAIRS_H = HEADS // 2
POOL_HEADS = 12

PACK = [
    ("ident", P), ("w1t", P), ("w2t", P), ("ones", P),
    ("rows", 5 * P),
    ("pk_wq", 2 * P), ("pk_bq", 2), ("pk_gamma", 1), ("pk_beta", 1), ("pk_keys", 2 * P),
    ("pk_group", 32), ("pk_mean", P), ("pk_down", P), ("pk_up", P),
    ("a1_q", P), ("a1_k", P), ("a1_v", P), ("a1_o", P), ("head_rows", HEADS),
    ("r_w1", AE_HID), ("r_g", 1), ("r_b", 1), ("r_w2", AE),
    ("e_qb", AE), ("e_kb", AE), ("e_vb", AE * AE), ("e_ob", P),
    ("e_q", AE * P), ("e_k", AE * P), ("e_v", AE * P), ("e_o", AE * P),
    ("a2_q", P), ("a2_qp", P), ("a2_k", P), ("a2_kp", P), ("a2_v", P), ("a2_o", P),
    ("cosq", SEQ), ("sinq", SEQ), ("cosk", SEQ), ("sink", SEQ),
    ("f_gate", FE), ("f_w1", PAIRS * P), ("f_w3", PAIRS * P), ("f_w2", PAIRS * P),
    ("x_g", 1), ("x_b", 1), ("l_g", 1), ("l_b", 1), ("q_gamma", 1), ("k_gamma", 1),
    ("l3_q", P), ("l3_kv", 2 * P), ("l3_o", P),
    ("b_fc", HIDDEN), ("b_proj", CHUNKS * P), ("b_v", P), ("b_ut", HIDDEN), ("b_fb", RANK), ("b_gate", 1),
]
OFFSET, _at = {}, 0
for _name, _width in PACK:
    OFFSET[_name] = (_at, _width)
    _at += _width
PACK_COLS = _at
GROUPS = ["rows", "pk_up", "head_rows", "e_ob", "e_o", "sink", "f_w2", "b_gate"]


def group_ends():
    return [OFFSET[name][0] + OFFSET[name][1] for name in GROUPS]


def build(nc, d_x, d_ctx, d_ctxt, d_pack, d_gates, d_qpos, d_kpos, d_mask, d_keep, d_out, layers=8):
    ctx = ExitStack()
    with ctx:
        def sb(name, cols, dt=F32):
            return ctx.enter_context(nc.sbuf_tensor(name, [P, cols], dt))

        def sem(name):
            return ctx.enter_context(nc.semaphore(name))

        bank = [ctx.enter_context(nc.psum_tensor(f"bank{i}", [P, HALF], F32)) for i in range(8)]

        pack = sb("pack", PACK_COLS)

        def W(name, a=0, n=None, rows=P):
            at, width = OFFSET[name]
            return pack[0:rows, at + a:at + a + (width if n is None else n)]

        X = sb("X", TOKENS)
        H = sb("H", TOKENS)
        HT = sb("HT", TOKENS)
        CT = sb("ctxT", TOKENS)
        KBD = sb("KBD", RING_K * 2 * HEADS * SEQ)
        SCR = sb("scratch", 16384)
        VM = sb("VM", RING_V * 2 * PAIRS_H * V_COLS)
        QT = sb("QT", RING_Q * P)
        KT = sb("KT", RING_Q * P)
        PB = sb("probs", 2 * HEADS * SEQ)
        PTB = sb("probsT", 2 * HEADS * SEQ)
        OTB = sb("heads_outT", 2 * P)
        gates_in = sb("gates_in", 8)
        gate = sb("gate", 8)
        stats = sb("stats", TILES * 6)
        mv = sb("mean_var", TILES * 2)
        var_eps = sb("var_eps", TILES)
        rstd = sb("rstd", TILES)
        neghalf = sb("neghalf", 2 * P)
        rowmax = sb("rowmax", HEADS)
        rsum = sb("rsum", 2 * HEADS)
        qpos = sb("qpos", TILES, I32)
        qposf = sb("qposf", TILES)
        kpos = PB[:, 0:TILES * SEQ].bitcast(I32)
        mask = PB[:, TILES * SEQ:2 * TILES * SEQ].bitcast(I32)
        keep = sb("keep", SEQ, I32)
        ND = QT[:, 0:TILES * SEQ]
        MADD = QT[:, TILES * SEQ:2 * TILES * SEQ]
        small = sb("small", 512)
        GATES = sb("expert_gates", TILES * AE)
        GT = H[0:AE, :]
        OB = sb("out_bias", P)

        Xt = X[:, :].rearrange("p (t d) -> p t d", t=TILES)
        Ht = H[:, :].rearrange("p (t d) -> p t d", t=TILES)
        Ct = QT[:, :].rearrange("p (t d) -> p t d", t=TILES)
        KBDu = KBD[:, :].rearrange("p (u b h k) -> p u b h k", u=RING_K, b=2, h=HEADS)
        VMu = VM[:, :].rearrange("p (u b j c) -> p u b j c", u=RING_V, b=2, j=PAIRS_H)
        MV = mv[:, :].rearrange("p (t c) -> p t c", c=2)
        STATS = stats[:, :].rearrange("p (t c) -> p t c", c=6)
        ident = W("ident")
        row_at = {"b0": 0, "b3": P, "rb1": 2 * P, "rb2": 3 * P}

        in_x = sem("in_x")
        in_ctx = sem("in_ctx")
        in_small = sem("in_small")
        in_pack = [sem(f"in_pack_{g}") for g in GROUPS]
        layer_end = sem("layer_end")
        own = {e: sem(f"own_{e}") for e in ("vector", "pool", "scalar")}
        zeroed = sem("zeroed")
        consts = sem("consts")
        gate_ready = sem("gate_ready")
        var_ready = sem("var_ready")
        rstd_ready = sem("rstd_ready")
        normed = sem("normed")
        turned = sem("turned")
        ht_ready = sem("ht_ready")
        l0_out = sem("l0_out")
        ctx_mean = sem("ctx_mean")
        out_stored = sem("out_stored")

        class Order:

            def __init__(self, eng, name):
                self.eng, self.sem, self.n = eng, own[name], 0

            def mark(self, ins):
                ins.then_inc(self.sem, 1)
                self.n += 1

            def settle(self):
                self.eng.wait_ge(self.sem, self.n)

            def link(self, ins):
                self.mark(ins)
                self.settle()

        def end_layer(eng, k):
            eng.drain().then_inc(layer_end, 1)
            eng.wait_ge(layer_end, 5 * (k + 1))

        first_use = {0: (0,), 1: (1,), 2: (2,), 3: (3, 4), 4: (5,), 5: (6,), 6: (7,)}

        def norm_vector(v, order, src, dst, n):
            for t in range(TILES):
                order.mark(v.bn_stats(STATS[:, t, :], src(t)))
            order.settle()
            for t in range(TILES):
                last = v.bn_aggr(MV[:, t, :], STATS[:, t, :])
            last.then_inc(var_ready, 1)
            v.wait_ge(rstd_ready, n + 1)
            for t in range(TILES):
                v.tensor_scalar(dst(t), src(t), MV[:, t, 0:1], rstd[:, t:t + 1], ALU.subtract, ALU.mult)\
                    .then_inc(normed, 1)

        def norm_pool(g, order, n):
            g.wait_ge(var_ready, n + 1)
            order.link(g.tensor_scalar(var_eps[:, :], MV[:, :, 1], EPS, None, ALU.add))
            g.tensor_tensor(rstd[:, :], var_eps[:, :], neghalf[:, 0:TILES], ALU.pow).then_inc(rstd_ready, 1)

        def turn_tensor(pe, src, norm_n, banks=(0, 1)):
            for t in range(TILES):
                pe.wait_ge(normed, TILES * norm_n + t + 1)
                ins = pe.transpose(bank[banks[t // 4]][:, P * (t % 4):P * (t % 4) + P], src(t), ident)
                if t % 4 == 3:
                    ins.then_inc(turned, 1)

        def turn_scalar(a, n, banks=(0, 1)):
            for j in range(2):
                a.wait_ge(turned, 2 * n + j + 1)
                a.copy(HT[:, HALF * j:HALF * j + HALF], bank[banks[j]][:, :]).then_inc(ht_ready, 1)

        def x_tile(t):
            return Xt[:, t, :]

        def h_tile(t):
            return Ht[:, t, :]

        def ht(t, n=1):
            return HT[:, P * t:P * (t + n)]

        def add_to_x(v, k, half, src):
            xs = X[:, HALF * half:HALF * half + HALF]
            return v.scalar_tensor_tensor(xs, src, gate[:, k:k + 1], xs, ALU.mult, ALU.add)

        CS = small[:, 0:BATCH]
        CSB = SCR[:, 0:TOKENS]

        def l0x_vector(v, o):
            v.wait_ge(in_ctx, 16)
            o.link(v.tensor_reduce(CS, CT[:, :].rearrange("p (b s) -> p b s", b=BATCH), AX.X, ALU.add))
            v.tensor_scalar(CSB.rearrange("p (b s) -> p b s", b=BATCH),
                            CS[:, :, None].to_broadcast([P, BATCH, SEQ]), 1.0 / SEQ, None, ALU.mult)\
                .then_inc(ctx_mean, 1)
            v.wait_ge(in_x, 16)
            norm_vector(v, o, x_tile, h_tile, 0)
            v.wait_ge(gate_ready, 1)
            for j in range(2):
                v.wait_ge(l0_out, j + 1)
                add_to_x(v, 0, j, bank[2 + j][:, :])

        def l0x_tensor(pe):
            pe.wait_ge(in_pack[0], 16)
            turn_tensor(pe, h_tile, 0)
            pe.wait_ge(ctx_mean, 1)
            for t in range(TILES):
                pe.wait_ge(ht_ready, t // 4 + 1)
                out = bank[2 + t // 4][:, P * (t % 4):P * (t % 4) + P]
                pe.matmul(out, ht(t), W("w1t"), start=True, stop=False)
                pe.matmul(out, CSB[:, P * t:P * t + P], W("w2t"), start=False, stop=False)
                ins = pe.matmul(out, W("ones", rows=1), W("rows", row_at["b0"], P, rows=1), start=False, stop=True)
                if t % 4 == 3:
                    ins.then_inc(l0_out, 1)

        qa = SCR[:, 0:2048].rearrange("p (a t) -> p a t", a=2)
        qn = SCR[:, 2048:4096].rearrange("p (a t) -> p a t", a=2)
        sq = SCR[:, 4096:6144].rearrange("p (a t) -> p a t", a=2)
        sc = SCR[:, 6144:10240].rearrange("p (t g k) -> p t g k", t=TILES, g=PK_GROUPS)
        mk = SCR[:, 10240:14336].rearrange("p (t g k) -> p t g k", t=TILES, g=PK_GROUPS)
        pw = SCR[:, 14336:16384].rearrange("p (b h i k) -> p b h i k", b=2, h=PK_HEADS, i=PK_FAR)
        gelu_t = SCR[:, 0:1024]
        wg = SCR[:, 2048:3072]
        wexp = SCR[:, 3072:4096].rearrange("p (t e) -> p t e", t=TILES)
        keybd = PTB[:, 576:576 + 2 * P]
        keysq = PTB[:, 832:832 + 2 * P]
        pkst = small[:, 0:64]
        n2 = PTB[:, 1088:1088 + HALF]
        rn = small[:, 192:320]
        top8 = small[:, 320:448]
        totals = small[:, 448:464]
        rtot = small[:, 464:480]
        rem = small[:, 480:488]
        near = small[:, 488:496]
        farw = small[:, 496:504]
        p0n = PTB[:, 0:TILES * PK_HEADS * PK_FAR]
        p0nt = p0n[:, :].rearrange("p (t h i) -> p t h i", t=TILES, h=PK_HEADS)
        knorm = PTB[:, 512:512 + 2 * PK_KEYS]
        pk_q, pk_qa = sem("pk_q"), sem("pk_qa")
        pk_keysq, pk_keysum, pk_keyn2, pk_keyr = sem("pk_keysq"), sem("pk_keysum"), sem("pk_keyn2"), sem("pk_keyr")
        pk_keyready = sem("pk_keyready")
        pk_rowstat, pk_stat, pk_qvar, pk_qrstd = sem("pk_rowstat"), sem("pk_stat"), sem("pk_qvar"), sem("pk_qrstd")
        pk_qn, pk_sq, pk_score, pk_norm2 = sem("pk_qn"), sem("pk_sq"), sem("pk_score"), sem("pk_norm2")
        pk_n2, pk_rn, pk_sc, pk_exp = sem("pk_n2"), sem("pk_rn"), sem("pk_sc"), sem("pk_exp")
        pk_p0, pk_pw, pk_w, pk_wt, pk_wg = sem("pk_p0"), sem("pk_pw"), sem("pk_w"), sem("pk_wt"), sem("pk_wg")
        pk_eh, pk_gelu, pk_out, pk_pwread = sem("pk_eh"), sem("pk_gelu"), sem("pk_out"), sem("pk_pwread")
        pk_n2t = sem("pk_n2t")
        pk_mask, pk_chosen = sem("pk_mask"), sem("pk_chosen")

        def l0f_keys_vector(v, o):
            v.tensor_tensor(keysq, W("pk_keys"), W("pk_keys"), ALU.mult).then_inc(pk_keysq, 1)
            v.wait_ge(pk_keysum, 1)
            v.tensor_scalar(knorm, bank[2][:, 0:2 * PK_KEYS], 1e-24, None, ALU.max).then_inc(pk_keyn2, 1)

        def l0f_spread_keys_vector(v):
            v.wait_ge(pk_keyr, 1)
            shape = [P, 4, 2 * PK_KEYS]
            v.tensor_tensor(keybd.rearrange("p (h k) -> p h k", h=4), W("pk_keys").rearrange("p (h k) -> p h k", h=4),
                            knorm[:, None, :].to_broadcast(shape), ALU.mult).then_inc(pk_keyready, 1)

        def l0f_vector(v, o):
            norm_vector(v, o, x_tile, h_tile, 1)
            l0f_keys_vector(v, o)
            st = pkst[:, 0:24].rearrange("p (a c) -> p a c", a=4)
            agg = pkst[:, 24:28].rearrange("p (a c) -> p a c", a=2)
            for a_ in range(2):
                for j in range(2):
                    v.wait_ge(pk_qa, 2 * a_ + j + 1)
                    o.mark(v.bn_stats(st[:, 2 * a_ + j, :], qa[:, a_, HALF * j:HALF * j + HALF]))
            o.settle()
            for a_ in range(2):
                o.mark(v.bn_aggr(agg[:, a_, :], st[:, 2 * a_:2 * a_ + 2, :].rearrange("p a c -> p (a c)")))
            o.settle()
            msq = pkst[:, 28:30]
            o.link(v.tensor_tensor(msq, agg[:, :, 0], agg[:, :, 0], ALU.mult))
            v.tensor_tensor(agg[:, :, 1], agg[:, :, 1], msq, ALU.add).then_inc(pk_rowstat, 1)
            v.wait_ge(pk_stat, 1)
            stat = pkst[:, 30:32]
            o.link(v.tensor_copy(stat, bank[2][:, 0:2]))
            mean2, qvar = pkst[:, 32:33], pkst[:, 33:34]
            o.link(v.tensor_tensor(mean2, stat[:, 0:1], stat[:, 0:1], ALU.mult))
            o.link(v.tensor_tensor(qvar, stat[:, 1:2], mean2, ALU.subtract))
            v.tensor_scalar(pkst[:, 34:35], qvar, EPS, None, ALU.add).then_inc(pk_qvar, 1)
            v.wait_ge(pk_qrstd, 1)
            scale, shift = pkst[:, 36:37], pkst[:, 37:38]
            o.link(v.reciprocal(pkst[:, 35:36], pkst[:, 35:36]))
            o.link(v.tensor_tensor(scale, pkst[:, 35:36], W("pk_gamma"), ALU.mult))
            o.link(v.tensor_tensor(pkst[:, 38:39], stat[:, 0:1], scale, ALU.mult))
            o.link(v.tensor_tensor(shift, W("pk_beta"), pkst[:, 38:39], ALU.subtract))
            for a_ in range(2):
                v.tensor_scalar(qn[:, a_, :], qa[:, a_, :], scale, shift, ALU.mult, ALU.add).then_inc(pk_qn, 1)
            l0f_spread_keys_vector(v)
            v.wait_ge(pk_norm2, 1)
            v.tensor_scalar(n2, bank[3][:, :], 1e-24, None, ALU.max).then_inc(pk_n2, 1)
            v.wait_ge(pk_rn, 2)
            o.link(v.reciprocal(rn, rn))
            rng = rn.rearrange("p (t g) -> p t g", t=TILES)
            fourth = top8.rearrange("p (g k) -> p g k", g=PK_GROUPS)[:, :, PK_TOP - 1:PK_TOP]
            for step in range(TILES + 2):
                t = step
                if t < TILES:
                    v.wait_ge(pk_score, t + 1)
                    v.tensor_tensor(sc[:, t], bank[4 + t % 4][:, :].rearrange("p (g k) -> p g k", g=PK_GROUPS),
                                    rng[:, t, :, None].to_broadcast([P, PK_GROUPS, PK_KEYS]), ALU.mult)\
                        .then_inc(pk_sc, 1)
                    v.wait_ge(pk_sc, t + 1)
                    for g_ in range(PK_GROUPS):
                        o.mark(v.max(top8[:, 8 * g_:8 * g_ + 8], sc[:, t, g_, :]))
                    o.settle()
                    v.tensor_tensor(mk[:, t], sc[:, t], fourth.to_broadcast([P, PK_GROUPS, PK_KEYS]), ALU.is_ge)\
                        .then_inc(pk_mask, 1)
                t = step - 1
                if 0 <= t < TILES:
                    v.wait_ge(pk_chosen, t + 1)
                    first = mk[:, t].rearrange("p (h c) k -> p h c k", c=2)[:, :, 0, :]
                    o.mark(v.tensor_reduce(totals, mk[:, t], AX.X, ALU.add))
                    o.mark(v.tensor_reduce(rem, first[:, :, PK_FAR:PK_KEYS], AX.X, ALU.add))
                    o.settle()
                    o.link(v.reciprocal(rtot, totals))
                    rt = rtot.rearrange("p (h c) -> p h c", c=2)
                    o.mark(v.tensor_tensor(near, rt[:, :, 0], rt[:, :, 1], ALU.mult))
                    o.mark(v.tensor_tensor(rem, rem, rt[:, :, 0], ALU.mult))
                    o.settle()
                    v.tensor_tensor(p0nt[:, t], first[:, :, 0:PK_FAR],
                                    near[:, :, None].to_broadcast([P, PK_HEADS, PK_FAR]), ALU.mult).then_inc(pk_p0, 1)
                    o.mark(v.tensor_reduce(farw[:, t:t + 1], rem, AX.X, ALU.add))
                t = step - 2
                if 0 <= t < TILES:
                    v.wait_ge(pk_pw, t + 1)
                    v.tensor_reduce(wexp[:, t, :], pw[:, t % 2].rearrange("p h i k -> p (i k) h"), AX.X, ALU.add)\
                        .then_inc(pk_pwread, 1)
                    v.wait_ge(pk_pwread, t + 1)
                    last = wexp[:, t, PK_EXPERTS - 1:PK_EXPERTS]
                    v.tensor_tensor(last, last, farw[:, t:t + 1], ALU.add).then_inc(pk_w, 1)
            for j in range(2):
                v.wait_ge(pk_wt, j + 1)
                v.wait_ge(pk_gelu, j + 1)
                v.tensor_tensor(wg[:, HALF * j:HALF * j + HALF], bank[j][:, :],
                                gelu_t[:, HALF * j:HALF * j + HALF], ALU.mult).then_inc(pk_wg, 1)
            for j in range(2):
                v.wait_ge(pk_out, j + 1)
                add_to_x(v, 1, j, bank[4 + j][:, :])

        def l0f_tensor(pe):
            pe.wait_ge(pk_keysq, 1)
            pe.matmul(bank[2][:, 0:2 * P], W("ones"), keysq, start=True, stop=True).then_inc(pk_keysum, 1)
            for a_ in range(2):
                for j in range(2):
                    pe.wait_ge(ht_ready, 2 * 1 + j + 1)
                    pe.matmul(bank[4 + 2 * a_ + j][:, :], W("pk_wq", P * a_, P), HT[:, HALF * j:HALF * j + HALF],
                              start=True, stop=True).then_inc(pk_q, 1)
            pe.wait_ge(pk_keyn2, 1)
            pe.wait_ge(pk_rowstat, 1)
            agg = pkst[:, 24:28].rearrange("p (a c) -> p a c", a=2)
            for a_ in range(2):
                ins = pe.matmul(bank[2][:, 0:2], W("pk_mean"), agg[:, a_, :], start=(a_ == 0), stop=(a_ == 1))
            ins.then_inc(pk_stat, 1)
            for a_ in range(2):
                pe.wait_ge(pk_sq, a_ + 1)
            for j in range(2):
                for a_ in range(2):
                    at = 64 * j + 32 * a_
                    ins = pe.matmul(bank[3][at:at + 32, :], W("pk_group"), sq[:, a_, HALF * j:HALF * j + HALF],
                                    start=True, stop=True)
            ins.then_inc(pk_norm2, 1)
            pe.wait_ge(pk_qvar, 1)
            pe.wait_ge(pk_n2, 1)
            for c in range(4):
                ins = pe.transpose(bank[2][:, P * c:P * c + P], n2[:, P * c:P * c + P], ident)
            ins.then_inc(pk_n2t, 1)
            pe.wait_ge(pk_qa, 4)
            pe.wait_ge(pk_keyready, 1)
            for t in range(TILES):
                if t >= 4:
                    pe.wait_ge(pk_sc, t - 3)
                for a_ in range(2):
                    ins = pe.matmul(bank[4 + t % 4][:, 2 * P * a_:2 * P * a_ + 2 * P], qn[:, a_, P * t:P * t + P],
                                    keybd, start=True, stop=True)
                ins.then_inc(pk_score, 1)
            pe.wait_ge(pk_stat, 1)
            for j in range(2):
                if j == 0:
                    pe.wait_ge(pk_rn, 2)
                pe.matmul(bank[2 + j][:, :], W("pk_down"), HT[:, HALF * j:HALF * j + HALF],
                          start=True, stop=True).then_inc(pk_eh, 1)
            for t in range(TILES):
                pe.wait_ge(pk_w, t + 1)
                ins = pe.transpose(bank[t // 4][:, P * (t % 4):P * (t % 4) + P], wexp[:, t, :], ident)
                if t % 4 == 3:
                    ins.then_inc(pk_wt, 1)
            pe.wait_ge(pk_sc, TILES)
            for t in range(TILES):
                pe.wait_ge(pk_wg, t // 4 + 1)
                ins = pe.matmul(bank[4 + t // 4][:, P * (t % 4):P * (t % 4) + P], wg[:, P * t:P * t + P], W("pk_up"),
                                start=True, stop=True)
                if t % 4 == 3:
                    ins.then_inc(pk_out, 1)

        def l0f_scalar(a):
            for a_ in range(2):
                for j in range(2):
                    a.wait_ge(pk_q, 2 * a_ + j + 1)
                    a.activation(qa[:, a_, HALF * j:HALF * j + HALF], bank[4 + 2 * a_ + j][:, :], ACT.Identity,
                                 bias=W("pk_bq", a_, 1)).then_inc(pk_qa, 1)
            a.wait_ge(pk_qvar, 1)
            a.activation(pkst[:, 35:36], pkst[:, 34:35], ACT.Sqrt).then_inc(pk_qrstd, 1)
            for a_ in range(2):
                a.wait_ge(pk_qn, a_ + 1)
                a.activation(sq[:, a_, :], qn[:, a_, :], ACT.Square).then_inc(pk_sq, 1)
            a.wait_ge(pk_n2t, 1)
            for j in range(2):
                src = bank[2][:, :].rearrange("p (c j a g) -> p j c a g", c=4, j=2, a=2)[:, j, :, :, 0:8]
                a.activation(rn[:, 64 * j:64 * j + 64].rearrange("p (c a g) -> p c a g", c=4, a=2), src, ACT.Sqrt)\
                    .then_inc(pk_rn, 1)
            position_bias_scalar(a)
            for t in range(TILES):
                a.wait_ge(pk_mask, t + 1)
                a.activation(sc[:, t], sc[:, t], ACT.Exp).then_inc(pk_exp, 1)
            for j in range(2):
                a.wait_ge(pk_eh, j + 1)
                a.activation(gelu_t[:, HALF * j:HALF * j + HALF], bank[2 + j][:, :], ACT.Gelu).then_inc(pk_gelu, 1)

        def l0f_pool(g, o):
            norm_pool(g, o, 1)
            g.wait_ge(pk_keyn2, 1)
            g.tensor_tensor(knorm, knorm, neghalf[:, 0:2 * PK_KEYS], ALU.pow).then_inc(pk_keyr, 1)
            g.wait_ge(a_sloped, 1)
            for step in range(TILES + 1):
                t = step
                if t < TILES:
                    g.wait_ge(pk_exp, t + 1)
                    g.tensor_tensor(mk[:, t], mk[:, t], sc[:, t], ALU.mult).then_inc(pk_chosen, 1)
                t = step - 1
                if 0 <= t < TILES:
                    g.wait_ge(pk_p0, t + 1)
                    if t >= 2:
                        g.wait_ge(pk_pwread, t - 1)
                    second = mk[:, t].rearrange("p (h c) k -> p h c k", c=2)[:, :, 1, :]
                    shape = [P, PK_HEADS, PK_FAR, PK_KEYS]
                    g.tensor_tensor(pw[:, t % 2], p0nt[:, t][:, :, :, None].to_broadcast(shape),
                                    second[:, :, None, :].to_broadcast(shape), ALU.mult).then_inc(pk_pw, 1)
                    position_mask_pool(g, t)

        a_proj, a_q, a_k, a_v = sem("a_proj"), sem("a_q"), sem("a_k"), sem("a_v")
        a_kbd = [sem("a_kbd_pool"), sem("a_kbd_scalar")]
        a_s, a_sub, a_exp = sem("a_s"), sem("a_sub"), sem("a_exp")
        a_t, a_r = sem("a_t"), sem("a_r")
        a_norm = [sem("a_norm_pool"), sem("a_norm_vector")]
        a_sum, a_inv, a_max = sem("a_sum"), sem("a_inv"), sem("a_max")
        a_pt = [sem("a_pt0"), sem("a_pt1")]
        a_pv, a_ots, a_out, a_x = sem("a_pv"), sem("a_ots"), sem("a_out"), sem("a_x")
        a_biased, a_sloped = sem("a_biased"), sem("a_sloped")
        rope_q, rope_k = sem("rope_q"), sem("rope_k")
        lead_s, lead_n, lead_t, lead_pv, lead_out = 2, 3, 4, 5, 6

        class Attention:

            def __init__(self, first, experts, tiles_before, gate_k, wq, wk, wv, wo, self_kv, rope=False, biased=False,
                         keys=None):
                self.first, self.experts, self.n = first, experts, experts * TILES
                self.tiles_before, self.gate_k = tiles_before, gate_k
                self.wq, self.wk, self.wv, self.wo = wq, wk, wv, wo
                self.self_kv, self.rope, self.biased, self.keys = self_kv, rope, biased, keys

        spread_keys = SCR[:, 0:8192].rearrange("p (u b h k) -> p u b h k", u=RING_K, b=2, h=HEADS)
        cross1 = Attention(0, 1, 0, 2, "a1_q", "a1_k", "a1_v", "a1_o", False, biased=True, keys=spread_keys)
        moe = Attention(8, AE, 8, 3, "e_q", "e_k", "e_v", "e_o", True, keys=KBDu)
        cross2 = Attention(8 + 8 * AE, 1, 16, 4, None, None, "a2_v", "a2_o", False, rope=True, keys=KBDu)
        bias1 = KBD[:, :].rearrange("p (t h k) -> p t h k", t=TILES, h=HEADS)
        S_BANK, PT_BANK, O_BANK, PJ_BANK, Y_BANK = (0, 1), (2, 3), 4, (5, 6), 7
        PROJECTED = cross1.n + moe.n
        qb_scaled = sb("qb_scaled", AE)

        def attend_tensor(pe, A):
            for s in range(A.n + lead_out + 1):
                i = s - lead_t
                if 0 <= i < A.n:
                    g = A.first + i
                    for half in range(2):
                        pe.wait_ge(a_norm[half], g + 1)
                        if g > 0:
                            pe.wait_ge(a_pt[half], g)
                        for j in range(4):
                            at = 1024 * (g % 2) + HALF * half + P * j
                            ins = pe.transpose(bank[PT_BANK[half]][:, P * j:P * j + P], PB[:, at:at + P], ident)
                        ins.then_inc(a_t, 1)
                i = s - lead_s
                if 0 <= i < A.n:
                    g = A.first + i
                    if A.rope:
                        pe.wait_ge(rope_q, 2)
                    else:
                        pe.wait_ge(a_q, g + 1)
                    pe.wait_ge(a_kbd[0], g + 1)
                    pe.wait_ge(a_kbd[1], g + 1)
                    q0 = P * (g % RING_Q)
                    for half in range(2):
                        if g > 0:
                            pe.wait_ge(a_sub, 2 * (g - 1) + half + 1)
                        for b in range(2):
                            ins = pe.matmul(bank[S_BANK[half]][SEQ * b:SEQ * b + SEQ, :],
                                            QT[:, q0 + SEQ * b:q0 + SEQ * b + SEQ],
                                            A.keys[:, g % RING_K, b, 8 * half:8 * half + 8, :]
                                            .rearrange("p h k -> p (h k)"), start=True, stop=True)
                        ins.then_inc(a_s, 1)
                i = s - lead_pv
                if 0 <= i < A.n:
                    g = A.first + i
                    pe.wait_ge(a_v, g + 1)
                    for half in range(2):
                        pe.wait_ge(a_pt[half], g + 1)
                    if g > 0:
                        pe.wait_ge(a_ots, g)
                    for b in range(2):
                        for j in (0, 2, 4, 6, 1, 3, 5, 7):
                            at = 1024 * (g % 2) + P * j + SEQ * b
                            ins = pe.matmul(bank[O_BANK][V_COLS * (j // 2):V_COLS * (j // 2 + 1), SEQ * b:SEQ * b + SEQ],
                                            VMu[:, g % RING_V, b, j, :], PTB[:, at:at + SEQ],
                                            start=(j % 2 == 0), stop=(j % 2 == 1))
                    ins.then_inc(a_pv, 1)
                i = s
                if i < A.n:
                    g, t, e = A.first + i, i // A.experts, i % A.experts
                    if g > 1:
                        pe.wait_ge(a_v, g - 1)
                    pe.wait_ge(ht_ready, A.ht_need + 2)
                    kv = HT if A.self_kv else CT
                    pj = bank[PJ_BANK[g % 2]]
                    if not A.rope:
                        pe.matmul(pj[:, 0:P], W(A.wk, P * e, P), kv[:, P * t:P * t + P], start=True, stop=True)
                        pe.matmul(pj[:, P:2 * P], W(A.wq, P * e, P), ht(t), start=True, stop=True)
                    for b in range(2):
                        src = kv[:, P * t + SEQ * b:P * t + SEQ * b + SEQ]
                        for half in range(2):
                            ins = pe.matmul(pj[SEQ * half:SEQ * half + SEQ, P * (2 + b):P * (3 + b)], src,
                                            W(A.wv, P * e, P), start=True, stop=True)
                    ins.then_inc(a_proj, 1)
                i = s - lead_out
                if 0 <= i < A.n:
                    g, t, e = A.first + i, i // A.experts, i % A.experts
                    pe.wait_ge(a_ots, g + 1)
                    y = bank[Y_BANK][:, 0:P]
                    if e == 0:
                        if A.tiles_before + t > 0:
                            pe.wait_ge(a_x, A.tiles_before + t)
                        if A.experts > 1:
                            pe.wait_ge(r_ready, 2)
                            pe.matmul(y, GT[0:AE, P * t:P * t + P], OB[0:AE, :], start=True, stop=False)
                    pe.matmul(y, OTB[:, P * (g % 2):P * (g % 2) + P], W(A.wo, P * e, P),
                              start=(A.experts == 1), stop=(e == A.experts - 1)).then_inc(a_out, 1)

        def attend_scalar(a, A):
            for s in range(A.n + lead_pv + 1):
                i = s - 1
                if 0 <= i < A.n:
                    g, e = A.first + i, i % A.experts
                    a.wait_ge(a_proj, g + 1)
                    pj, q0 = bank[PJ_BANK[g % 2]], P * (g % RING_Q)
                    if not A.rope:
                        if g >= RING_Q:
                            a.wait_ge(a_kbd[0], g - RING_Q + 1)
                            a.wait_ge(a_s, 2 * (g - RING_Q + 1))
                        if A.experts > 1:
                            a.activation(KT[:, q0:q0 + P], pj[:, 0:P], ACT.Identity, bias=W("e_kb", e, 1))\
                                .then_inc(a_k, 1)
                            a.activation(QT[:, q0:q0 + P], pj[:, P:2 * P], ACT.Identity,
                                         bias=qb_scaled[:, e:e + 1], scale=SCALE8).then_inc(a_q, 1)
                        else:
                            a.copy(KT[:, q0:q0 + P], pj[:, 0:P]).then_inc(a_k, 1)
                            a.mul(QT[:, q0:q0 + P], pj[:, P:2 * P], SCALE8).then_inc(a_q, 1)
                    if A.rope:
                        a.wait_ge(rope_k, 2)
                    else:
                        a.wait_ge(a_k, g + 1)
                    if g >= RING_K:
                        a.wait_ge(a_s, 2 * (g - RING_K + 1))
                    keys = KT[:, q0:q0 + P].rearrange("p (b k) -> p b k", b=2)
                    for h in range(POOL_HEADS, HEADS):
                        ins = a.mul(A.keys[:, g % RING_K, :, h, :], keys, W("head_rows", h, 1))
                    ins.then_inc(a_kbd[1], 1)
                    if g >= RING_V:
                        a.wait_ge(a_pv, g - RING_V + 1)
                    for half in range(2):
                        rows = slice(SEQ * half, SEQ * half + SEQ)
                        src = pj[rows, 2 * P:4 * P].rearrange("p (m j c d) -> p m j c d", m=PAIRS_H, j=2, c=2)
                        dst = VMu[rows, g % RING_V].rearrange("p b j c -> p (b j c)")\
                            .rearrange("p (m x c d) -> p m x c d", m=PAIRS_H, x=4, c=2)
                        ins = a.copy(dst[:, :, 0:4:3, half, :], src[:, :, :, half, :])
                    ins.then_inc(a_v, 1)
                i = s - lead_t
                if 0 <= i < A.n:
                    g = A.first + i
                    for half in range(2):
                        a.wait_ge(a_t, 2 * g + half + 1)
                        if g >= 2:
                            a.wait_ge(a_pv, g - 1)
                        at = 1024 * (g % 2) + HALF * half
                        a.copy(PTB[:, at:at + HALF], bank[PT_BANK[half]][:, :]).then_inc(a_pt[half], 1)
                i = s - lead_pv
                if 0 <= i < A.n:
                    g = A.first + i
                    a.wait_ge(a_pv, g + 1)
                    if g >= 2:
                        a.wait_ge(a_out, g - 1)
                    a.copy(OTB[:, P * (g % 2):P * (g % 2) + P], bank[O_BANK][:, 0:P]).then_inc(a_ots, 1)
                i = s - lead_s
                if 0 <= i < A.n:
                    g = A.first + i
                    for half in range(2):
                        a.wait_ge(a_sub, 2 * g + half + 1)
                        at = 1024 * (g % 2) + HALF * half
                        a.activation(PB[:, at:at + HALF], PB[:, at:at + HALF], ACT.Exp).then_inc(a_exp, 1)

        def attend_vector(v, o, A):
            for s in range(lead_s, A.n + lead_out + 2):
                i = s - lead_n
                if 0 <= i < A.n:
                    g, t, e = A.first + i, i // A.experts, i % A.experts
                    probs = PB[:, 1024 * (g % 2):1024 * (g % 2) + 1024].rearrange("p (h k) -> p h k", h=HEADS)
                    r = rsum[:, 8 * (g % 2):8 * (g % 2) + 8]
                    sums = (rsum[:, 16:24], rsum[:, 24:32])
                    gated = GATES[:, AE * t + e:AE * t + e + 1] if A.experts > 1 else W("ones", 0, 1)
                    for half in range(2):
                        v.wait_ge(a_exp, 2 * g + half + 1)
                        v.tensor_reduce(sums[half], probs[:, 8 * half:8 * half + 8], AX.X, ALU.add)\
                            .then_inc(a_sum, 1)
                    for half in range(2):
                        v.wait_ge(a_sum, 2 * g + half + 1)
                        if A.biased:
                            o.link(v.tensor_scalar(sums[half], sums[half], 1.0, None, ALU.add))
                        v.reciprocal(sums[half], sums[half]).then_inc(a_inv, 1)
                    v.wait_ge(a_inv, 2 * g + 1)
                    v.tensor_scalar(r, sums[0], gated, None, ALU.mult).then_inc(a_r, 1)
                    v.wait_ge(a_inv, 2 * g + 2)
                    v.scalar_tensor_tensor(probs[:, 8:16], probs[:, 8:16], gated,
                                           sums[1][:, :, None].to_broadcast([P, 8, SEQ]), ALU.mult, ALU.mult)\
                        .then_inc(a_norm[1], 1)
                i = s - lead_s
                if 0 <= i < A.n:
                    g = A.first + i
                    parts = []
                    for half in range(2):
                        at = 1024 * (g % 2) + HALF * half
                        parts.append((PB[:, at:at + HALF].rearrange("p (h k) -> p h k", h=8),
                                      bank[S_BANK[half]][:, :].rearrange("p (h k) -> p h k", h=8),
                                      rowmax[:, 8 * half:8 * half + 8]))
                    for half, (probs, scores, m) in enumerate(parts):
                        v.wait_ge(a_s, 2 * g + half + 1)
                        if A.biased:
                            if g >= 2 and half == 0:
                                v.wait_ge(a_t, 2 * (g - 1))
                            v.tensor_tensor(probs, scores, bias1[:, i, 8 * half:8 * half + 8, :], ALU.add)\
                                .then_inc(a_biased, 1)
                            v.wait_ge(a_biased, 2 * i + half + 1)
                            scores = probs
                        v.tensor_reduce(m, scores, AX.X, ALU.max).then_inc(a_max, 1)
                    if g >= 2 and not A.biased:
                        v.wait_ge(a_t, 2 * (g - 1))
                    for half, (probs, scores, m) in enumerate(parts):
                        v.wait_ge(a_max, 2 * g + half + 1)
                        v.tensor_tensor(probs, probs if A.biased else scores, m[:, :, None].to_broadcast([P, 8, SEQ]),
                                        ALU.subtract).then_inc(a_sub, 1)
                i = s - lead_out - 1
                if 0 <= i < A.n and i % A.experts == A.experts - 1:
                    g, t = A.first + i, i // A.experts
                    v.wait_ge(a_out, g + 1)
                    v.scalar_tensor_tensor(Xt[:, t, :], bank[Y_BANK][:, 0:P], gate[:, A.gate_k:A.gate_k + 1],
                                           Xt[:, t, :], ALU.mult, ALU.add).then_inc(a_x, 1)

        def attend_pool(gp, A):
            for s in range(A.n + lead_n):
                i = s - 1
                if 0 <= i < A.n:
                    g = A.first + i
                    if A.rope:
                        gp.wait_ge(rope_k, 2)
                    else:
                        gp.wait_ge(a_k, g + 1)
                    if g >= RING_K:
                        gp.wait_ge(a_s, 2 * (g - RING_K + 1))
                    keys = KT[:, P * (g % RING_Q):P * (g % RING_Q) + P].rearrange("p (b k) -> p b k", b=2)
                    shape = [P, 2, POOL_HEADS, SEQ]
                    gp.tensor_tensor(A.keys[:, g % RING_K, :, 0:POOL_HEADS, :], keys[:, :, None, :].to_broadcast(shape),
                                     W("head_rows", 0, POOL_HEADS)[:, None, :, None].to_broadcast(shape), ALU.mult)\
                        .then_inc(a_kbd[0], 1)
                i = s - lead_n
                if 0 <= i < A.n:
                    g = A.first + i
                    gp.wait_ge(a_r, g + 1)
                    at = 1024 * (g % 2)
                    probs = PB[:, at:at + HALF].rearrange("p (h k) -> p h k", h=8)
                    r = rsum[:, 8 * (g % 2):8 * (g % 2) + 8]
                    gp.tensor_tensor(probs, probs, r[:, :, None].to_broadcast([P, 8, SEQ]), ALU.mult)\
                        .then_inc(a_norm[0], 1)

        def l1x_vector(v, o):
            norm_vector(v, o, x_tile, h_tile, 2)
            attend_vector(v, o, cross1)

        def l1x_pool(g, o):
            norm_pool(g, o, 2)
            attend_pool(g, cross1)

        bias_heads = bias1.rearrange("p t h k -> p h t k")

        def position_bias_scalar(a):
            for h in range(HEADS):
                ins = a.mul(bias_heads[:, h], ND.rearrange("p (t k) -> p t k", t=TILES),
                            float(np.float32((2.0 ** (-8.0 / HEADS)) ** (h + 1))))
            ins.then_inc(a_sloped, 1)

        def position_mask_pool(g, t):
            g.tensor_tensor(bias1[:, t], bias1[:, t],
                            MADD[:, SEQ * t:SEQ * t + SEQ][:, None, :].to_broadcast([P, HEADS, SEQ]), ALU.add)

        r_h, r_turned, r_relu, r_logits, r_sub, r_exp = (sem("r_h"), sem("r_turned"), sem("r_relu"), sem("r_logits"),
                                                         sem("r_sub"), sem("r_exp"))
        r_gates, r_gt, r_ob, r_ready = sem("r_gates"), sem("r_gt"), sem("r_ob"), sem("r_ready")
        r1 = SCR[:, 0:512]
        r1t = SCR[0:AE_HID, 512:1536]
        lg = SCR[:, 1536:1600]
        lge = SCR[:, 1600:1664]
        msk = SCR[:, 1664:1728]
        m8 = SCR[:, 1728:1792]

        def pick(v, o, logits, n, top, sub_sem, exp_sem, out, buf):
            lt, et, mt = (x.rearrange("p (t e) -> p t e", t=TILES) for x in buf[0:3])
            m8t = buf[3].rearrange("p (t e) -> p t e", t=TILES)
            o.link(v.tensor_copy(lt, logits))
            for t in range(TILES):
                o.mark(v.max(m8t[:, t, :], lt[:, t, :]))
            o.settle()
            o.mark(v.tensor_tensor(mt, lt, m8t[:, :, top - 1:top].to_broadcast([P, TILES, n]), ALU.is_ge))
            v.tensor_tensor(et, lt, m8t[:, :, 0:1].to_broadcast([P, TILES, n]), ALU.subtract).then_inc(sub_sem, 1)
            v.wait_ge(exp_sem, 1)
            o.settle()
            o.link(v.tensor_tensor(mt, mt, et, ALU.mult))
            o.link(v.tensor_reduce(rsum[:, 0:TILES], mt, AX.X, ALU.add))
            o.link(v.reciprocal(rsum[:, TILES:2 * TILES], rsum[:, 0:TILES]))
            return v.tensor_tensor(out, mt, rsum[:, TILES:2 * TILES, None].to_broadcast([P, TILES, n]), ALU.mult)

        def l1f_vector(v, o):
            norm_vector(v, o, x_tile, h_tile, 3)
            v.tensor_scalar(qb_scaled[:, :], W("e_qb"), SCALE8, None, ALU.mult).then_inc(r_ob, 1)
            v.wait_ge(r_h, 1)
            norm_vector(v, o, lambda t: bank[2][:, AE_HID * t:AE_HID * (t + 1)],
                        lambda t: r1[:, AE_HID * t:AE_HID * (t + 1)], 4)
            v.wait_ge(r_logits, 1)
            gt = GATES[:, :].rearrange("p (t e) -> p t e", t=TILES)
            pick(v, o, bank[3][:, 0:TILES * AE].rearrange("p (t e) -> p t e", t=TILES), AE, 2, r_sub, r_exp, gt,
                 (lg, lge, msk, m8)).then_inc(r_gates, 1)
            v.wait_ge(r_gates, 1)
            attend_vector(v, o, moe)

        def l1f_tensor(pe):
            turn_tensor(pe, h_tile, 3)
            pe.wait_ge(ht_ready, 8)
            for t in range(TILES):
                out = bank[2][:, AE_HID * t:AE_HID * (t + 1)]
                pe.matmul(out, ht(t), W("r_w1"), start=True, stop=False)
                ins = pe.matmul(out, W("ones", rows=1), W("rows", row_at["rb1"], AE_HID, rows=1), start=False, stop=True)
            ins.then_inc(r_h, 1)
            for e in range(AE):
                pe.matmul(bank[6][0:AE, 0:P], W("e_vb", AE * e, AE), W("e_o", P * e, P), start=(e == 0), stop=False)
            pe.matmul(bank[6][0:AE, 0:P], W("ident", 0, AE, rows=AE), W("e_ob", rows=AE), start=False, stop=True)\
                .then_inc(r_turned, 1)
            for t in range(TILES):
                pe.wait_ge(normed, TILES * 4 + t + 1)
                ins = pe.transpose(bank[4 + t // 4][0:AE_HID, P * (t % 4):P * (t % 4) + P],
                                   r1[:, AE_HID * t:AE_HID * (t + 1)], ident)
                if t % 4 == 3:
                    ins.then_inc(r_turned, 1)
            for t in range(TILES):
                pe.wait_ge(r_relu, t // 4 + 1)
                out = bank[3][:, AE * t:AE * (t + 1)]
                pe.matmul(out, r1t[:, P * t:P * t + P], W("r_w2", rows=AE_HID), start=True, stop=False)
                ins = pe.matmul(out, W("ones", rows=1), W("rows", row_at["rb2"], AE, rows=1), start=False, stop=True)
            ins.then_inc(r_logits, 1)
            pe.wait_ge(r_gates, 1)
            for t in range(TILES):
                ins = pe.transpose(bank[4 + t // 4][0:AE, P * (t % 4):P * (t % 4) + P],
                                   GATES[:, AE * t:AE * (t + 1)], ident)
                if t % 4 == 3:
                    ins.then_inc(r_gt, 1)
            pe.wait_ge(r_ready, 3)
            attend_tensor(pe, moe)

        def l1f_scalar(a):
            turn_scalar(a, 3)
            a.wait_ge(r_turned, 1)
            a.copy(OB[0:AE, :], bank[6][0:AE, 0:P]).then_inc(r_ready, 1)
            for j in range(2):
                a.wait_ge(r_turned, j + 2)
                a.activation(r1t[:, HALF * j:HALF * j + HALF], bank[4 + j][0:AE_HID, :], ACT.Relu,
                             bias=W("r_b", rows=AE_HID), scale=W("r_g", rows=AE_HID)).then_inc(r_relu, 1)
            a.wait_ge(r_sub, 1)
            a.activation(lge, lge, ACT.Exp).then_inc(r_exp, 1)
            for j in range(2):
                a.wait_ge(r_gt, j + 1)
                a.copy(GT[0:AE, HALF * j:HALF * j + HALF], bank[4 + j][0:AE, :]).then_inc(r_ready, 1)
            a.wait_ge(r_ob, 1)
            attend_scalar(a, moe)

        rp, rp_a, rp_b = sem("rp"), sem("rp_a"), sem("rp_b")
        t_cos = SCR[:, 0:1024]
        t_sin = SCR[:, 1024:2048]

        def l2x_tensor(pe):
            for r in range(4):
                src, half = ("k", r) if r < 2 else ("q", r - 2)
                if r == 2:
                    turn_tensor(pe, h_tile, 5)
                    pe.wait_ge(ht_ready, 10)
                if r >= 2:
                    pe.wait_ge(rp_b, r - 1)
                rhs = (CT if src == "k" else HT)[:, HALF * half:HALF * half + HALF]
                pe.matmul(bank[2 + 2 * (r % 2)][:, :], W(f"a2_{src}"), rhs, start=True, stop=True)
                pe.matmul(bank[3 + 2 * (r % 2)][:, :], W(f"a2_{src}p"), rhs, start=True, stop=True).then_inc(rp, 1)
            pe.wait_ge(rp_b, 4)
            attend_tensor(pe, cross2)

        def l2x_vector(v, o):
            norm_vector(v, o, x_tile, h_tile, 5)
            for r in range(4):
                src = "k" if r < 2 else "q"
                v.wait_ge(rp, r + 1)
                if r >= 2:
                    v.wait_ge(rope_k, r - 1)
                at = HALF * (r % 2)
                shape = [P, 8, SEQ]

                def by_batch(x):
                    return x.rearrange("p (b s) -> p b s", b=8)

                o.mark(v.tensor_tensor(by_batch(t_cos[:, at:at + HALF]), by_batch(bank[2 + 2 * (r % 2)][:, :]),
                                       W(f"cos{src}")[:, None, :].to_broadcast(shape), ALU.mult))
                o.settle()
                v.tensor_tensor(by_batch(t_sin[:, at:at + HALF]), by_batch(bank[3 + 2 * (r % 2)][:, :]),
                                W(f"sin{src}")[:, None, :].to_broadcast(shape), ALU.mult).then_inc(rp_b, 1)
            attend_vector(v, o, cross2)

        def l2x_pool(g, o):
            norm_pool(g, o, 5)
            for r in range(4):
                g.wait_ge(rp_b, r + 1)
                at = HALF * (r % 2)
                dst, ready = (KT, rope_k) if r < 2 else (QT, rope_q)
                g.tensor_tensor(dst[:, at:at + HALF], t_cos[:, at:at + HALF], t_sin[:, at:at + HALF], ALU.add)\
                    .then_inc(ready, 1)
            attend_pool(g, cross2)

        f_logits, f_sub, f_exp, f_comb, f_ct, f_ctr = (sem("f_logits"), sem("f_sub"), sem("f_exp"), sem("f_comb"),
                                                       sem("f_ct"), sem("f_ctr"))
        f_h, f_silu, f_gated, f_act, f_out = sem("f_h"), sem("f_silu"), sem("f_gated"), sem("f_act"), sem("f_out")
        act_t = SCR[:, 0:PAIRS * 1024].rearrange("p (e t) -> p e t", e=PAIRS)
        silu = SCR[:, 9216:10240]
        gated = SCR[:, 10240:11264]
        comb_t = SCR[:, 11264:12288]
        comb = SCR[:, 12288:13312].rearrange("p (t e) -> p t e", t=TILES)
        flg, fle, fmk, fm8 = SCR[:, 13312:13440], SCR[:, 13440:13568], SCR[:, 13568:13696], SCR[:, 13696:13760]

        pick_row = KT

        def l2f_vector(v, o):
            o.mark(v.memset(SCR[:, 12288:13312], 0.0))
            o.mark(v.tensor_copy(KT[:, :].rearrange("p (r c) -> p r c", c=SEQ),
                                 ident[:, 0:BATCH, None].to_broadcast([P, BATCH, SEQ])))
            o.settle()
            norm_vector(v, o, x_tile, h_tile, 6)
            v.wait_ge(f_logits, 1)
            pick(v, o, bank[2][:, 0:TILES * FE].rearrange("p (t e) -> p t e", t=TILES), FE, FE_TOP, f_sub, f_exp,
                 comb[:, :, 0:FE], (flg, fle, fmk, fm8)).then_inc(f_comb, 1)
            for r in range(2 * PAIRS):
                e, half = r // 2, r % 2
                at = HALF * (r % 2)
                dst = act_t[:, e, HALF * half:HALF * half + HALF]
                shared = e == PAIRS - 1
                v.wait_ge(f_silu, r + 1)
                g_ = dst if shared else gated[:, at:at + HALF]
                ins = v.tensor_tensor(g_, bank[2 + r % 2][:, :], silu[:, at:at + HALF], ALU.mult)
                ins.then_inc(f_gated, 1)
                if not shared:
                    v.wait_ge(f_gated, r + 1)
                    v.tensor_tensor(dst, bank[4 + r % 2][:, :], g_, ALU.mult).then_inc(f_act, 1)
            for j in range(2):
                v.wait_ge(f_out, j + 1)
                add_to_x(v, 5, j, bank[6 + j][:, :])

        def l2f_tensor(pe):
            turn_tensor(pe, h_tile, 6)
            pe.wait_ge(ht_ready, 12)
            for t in range(TILES):
                ins = pe.matmul(bank[2][:, FE * t:FE * (t + 1)], ht(t), W("f_gate"), start=True, stop=True)
            ins.then_inc(f_logits, 1)
            pe.wait_ge(f_comb, 1)
            for t in range(TILES):
                ins = pe.transpose(bank[6 + t // 4][:, P * (t % 4):P * (t % 4) + P], comb[:, t, :], ident)
                if t % 4 == 3:
                    ins.then_inc(f_ct, 1)
            pe.wait_ge(f_ctr, 2)
            for r in range(2 * PAIRS):
                e, half = r // 2, r % 2
                rhs = HT[:, HALF * half:HALF * half + HALF]
                if r >= 2:
                    pe.wait_ge(f_gated, r - 1)
                pe.matmul(bank[r % 2][:, :], W("f_w1", P * e, P), rhs, start=True, stop=True)
                pe.matmul(bank[2 + r % 2][:, :], W("f_w3", P * e, P), rhs, start=True, stop=True).then_inc(f_h, 1)
                if e < PAIRS - 1:
                    if r >= 2:
                        pe.wait_ge(f_act, r - 1)
                    pe.matmul(bank[4 + r % 2][:, :], pick_row[:, P * e:P * e + P], comb_t[:, HALF * half:HALF * half + HALF],
                              start=True, stop=True).then_inc(f_crep, 1)
            pe.wait_ge(f_gated, 2 * PAIRS)
            pe.wait_ge(f_act, 2 * (PAIRS - 1))
            for t in range(TILES):
                for e in range(PAIRS):
                    ins = pe.matmul(bank[6 + t // 4][:, P * (t % 4):P * (t % 4) + P], act_t[:, e, P * t:P * t + P],
                                    W("f_w2", P * e, P), start=(e == 0), stop=(e == PAIRS - 1))
                if t % 4 == 3:
                    ins.then_inc(f_out, 1)

        f_crep = sem("f_crep")

        def l2f_scalar(a):
            turn_scalar(a, 5)
            a.wait_ge(f_sub, 1)
            a.activation(fle, fle, ACT.Exp).then_inc(f_exp, 1)
            for j in range(2):
                a.wait_ge(f_ct, j + 1)
                a.copy(comb_t[:, HALF * j:HALF * j + HALF], bank[6 + j][:, :]).then_inc(f_ctr, 1)
            for r in range(2 * PAIRS):
                at = HALF * (r % 2)
                a.wait_ge(f_h, r + 1)
                if r < 2 * (PAIRS - 1):
                    a.wait_ge(f_crep, r + 1)
                if r >= 2:
                    a.wait_ge(f_gated, r - 1)
                a.activation(silu[:, at:at + HALF], bank[r % 2][:, :], ACT.Silu).then_inc(f_silu, 1)

        cat_t = SCR[:, 0:2048].rearrange("p (b j) -> p b j", b=BATCH)
        qq = SCR[:, 2048:3072]
        kk = SCR[:, 3072:5120]
        vv = SCR[:, 5120:7200].rearrange("p (b h c) -> p b h c", b=BATCH, h=L_HEADS)
        kt3 = SCR[:, 7200:9248].rearrange("p (b j) -> p b j", b=BATCH)
        pp = SCR[:, 9248:11296]
        ptt = SCR[:, 11296:13344].rearrange("p (h t q) -> p h t q", h=L_HEADS, t=TILES)
        h2 = SCR[:, 13344:14368].rearrange("p (t d) -> p t d", t=TILES)
        h3 = SCR[:, 14368:15392].rearrange("p (t d) -> p t d", t=TILES)
        sq3 = KBD[:, 0:3072]
        ss = KBD[:, 3072:3120]
        ssc = KBD[:, 3120:3168]
        rr = KBD[:, 3168:3216]
        madd3 = KBD[:, 3216:3472]
        qt3 = KBD[:, 3584:4608]
        on3 = KBD[:, 4608:5632]
        ot3 = KBD[:, 5632:6656]
        max3 = KBD[:, 6656:6672]
        inv3 = KBD[:, 6672:6688]
        l_cat, l_q, l_kv, l_qq, l_kk, l_sq, l_rn = (sem("l_cat"), sem("l_q"), sem("l_kv"), sem("l_qq"), sem("l_kk"),
                                                     sem("l_sq"), sem("l_rn"))
        l_qkn, l_turn, l_qkt, l_s, l_sub, l_exp = (sem("l_qkn"), sem("l_turn"), sem("l_qkt"), sem("l_s"), sem("l_sub"),
                                                   sem("l_exp"))
        l_pt, l_ptt, l_o, l_on, l_ot, l_ots, l_y, l_mask = (sem("l_pt"), sem("l_ptt"), sem("l_o"), sem("l_on"),
                                                            sem("l_ot"), sem("l_ots"), sem("l_y"), sem("l_mask"))

        def l3x_vector(v, o):
            norm_vector(v, o, x_tile, h_tile, 7)
            v.wait_ge(normed, 8 * TILES)
            norm_vector(v, o, h_tile, lambda t: h2[:, t, :], 8)
            v.wait_ge(in_ctx, 32)
            norm_vector(v, o, lambda t: Ct[:, t, :], lambda t: h3[:, t, :], 9)
            m3 = madd3.rearrange("p (h j) -> p h j", h=L_HEADS)
            o.link(v.memset(madd3, 0.0))
            for h in range(L_HEADS):
                ins = v.tensor_scalar(m3[0:BATCH, h, 0:SEQ], keep[0:BATCH, :], 0.0, MASKED, ALU.is_equal, ALU.mult)
            ins.then_inc(l_mask, 1)
            o.mark(v.memset(vv[:, :, :, L_DIM:L_DIM + 1], 1.0))
            v.wait_ge(l_qq, 2)
            o.mark(v.tensor_tensor(sq3[:, 0:1024], qq, qq, ALU.mult))
            v.wait_ge(l_kk, 8)
            o.mark(v.tensor_tensor(sq3[:, 1024:3072], kk, kk, ALU.mult))
            o.settle()
            o.link(v.tensor_reduce(ss, sq3.rearrange("p (g d) -> p g d", d=L_DIM), AX.X, ALU.add))
            v.tensor_scalar(ssc, ss, 1.0 / L_DIM, 1e-16, ALU.mult, ALU.max).then_inc(l_sq, 1)
            v.wait_ge(l_rn, 1)
            o.link(v.tensor_scalar(rr[:, 0:16], rr[:, 0:16], float(L_DIM ** -0.5), None, ALU.mult))
            for src, at, n in ((qq, 0, 16), (kk, 16, 32)):
                x = src.rearrange("p (g d) -> p g d", d=L_DIM)
                v.tensor_tensor(x, x, rr[:, at:at + n, None].to_broadcast([P, n, L_DIM]), ALU.mult).then_inc(l_qkn, 1)
            p3 = pp.rearrange("p (h t j) -> p h t j", h=L_HEADS, t=TILES)
            for r in range(4):
                h, part = r % 2, r // 2
                v.wait_ge(l_s, part + 1)
                s3 = bank[r][:, :].rearrange("p (t j) -> p t j", t=4)
                m = max3[:, 4 * r:4 * r + 4]
                o.link(v.tensor_reduce(m, s3, AX.X, ALU.max))
                v.tensor_tensor(p3[:, h, 4 * part:4 * part + 4, :], s3, m[:, :, None].to_broadcast([P, 4, KEYS]),
                                ALU.subtract).then_inc(l_sub, 1)
            for t in range(TILES):
                v.wait_ge(l_o, t // 2 + 1)
                o3 = bank[t // 2][:, 130 * (t % 2):130 * (t % 2) + 130].rearrange("p (h c) -> p h c", h=L_HEADS)
                r_ = inv3[:, 2 * t:2 * t + 2]
                o.link(v.reciprocal(r_, o3[:, :, L_DIM]))
                v.tensor_tensor(on3[:, P * t:P * t + P].rearrange("p (h d) -> p h d", h=L_HEADS), o3[:, :, 0:L_DIM],
                                r_[:, :, None].to_broadcast([P, L_HEADS, L_DIM]), ALU.mult).then_inc(l_on, 1)
            for j in range(2):
                v.wait_ge(l_y, j + 1)
                add_to_x(v, 6, j, bank[6 + j][:, :])

        def l3x_pool(g, o):
            norm_pool(g, o, 7)
            norm_pool(g, o, 8)
            norm_pool(g, o, 9)
            g.wait_ge(l_sq, 1)
            g.tensor_tensor(rr, ssc, neghalf[:, 0:48], ALU.pow).then_inc(l_rn, 1)

        def l3x_tensor(pe):
            for n, src in ((8, h2), (9, h3)):
                turn_tensor(pe, lambda t, s_=src: s_[:, t, :], n, banks=(0, 1) if n == 8 else (2, 3))
            pe.wait_ge(l_cat, 4)
            for t in range(TILES):
                for b in range(2):
                    ins = pe.matmul(bank[t // 4][SEQ * b:SEQ * b + SEQ, P * (t % 4):P * (t % 4) + P],
                                    cat_t[:, 2 * t + b, SEQ:KEYS], W("l3_q"), start=True, stop=True)
                if t % 4 == 3:
                    ins.then_inc(l_q, 1)
            for b in range(BATCH):
                r = b // 2
                if b % 2 == 0 and r >= 4:
                    pe.wait_ge(l_kk, r - 3)
                ins = pe.matmul(bank[4 + r % 4][:, 2 * P * (b % 2):2 * P * (b % 2) + 2 * P], cat_t[:, b, :],
                                W("l3_kv"), start=True, stop=True)
                if b % 2 == 1:
                    ins.then_inc(l_kv, 1)
            for r in range(6):
                if r == 0:
                    pe.wait_ge(l_qkn, 1)
                if r == 2:
                    pe.wait_ge(l_qkn, 2)
                src = qq if r < 2 else kk
                for j in range(4):
                    at = P * (4 * (r if r < 2 else r - 2) + j)
                    ins = pe.transpose(bank[r][:, P * j:P * j + P], src[:, at:at + P], ident)
                ins.then_inc(l_turn, 1)
            pe.wait_ge(l_qkt, 6)
            pe.wait_ge(l_mask, 1)
            for part in range(2):
                for t in range(4 * part, 4 * part + 4):
                    for h in range(L_HEADS):
                        out = bank[2 * part + h][:, KEYS * (t % 4):KEYS * (t % 4) + KEYS]
                        pe.matmul(out, pick_row[0:BATCH, P * t:P * t + P], madd3[0:BATCH, KEYS * h:KEYS * h + KEYS],
                                  start=True, stop=False)
                        for b in range(2):
                            rows = slice(L_DIM * h, L_DIM * h + L_DIM)
                            ins = pe.matmul(out[SEQ * b:SEQ * b + SEQ, :],
                                            qt3[rows, P * t + SEQ * b:P * t + SEQ * b + SEQ],
                                            kt3[rows, 2 * t + b, :], start=False, stop=True)
                ins.then_inc(l_s, 1)
            for r in range(4):
                h, part = r % 2, r // 2
                pe.wait_ge(l_exp, r + 1)
                for j in range(4):
                    at = 1024 * h + HALF * part + P * j
                    ins = pe.transpose(bank[4 + r][:, P * j:P * j + P], pp[:, at:at + P], ident)
                ins.then_inc(l_pt, 1)
            pe.wait_ge(l_ptt, 4)
            for t in range(TILES):
                for h in range(L_HEADS):
                    for b in range(2):
                        at = 130 * (t % 2) + 65 * h
                        ins = pe.matmul(bank[t // 2][SEQ * b:SEQ * b + SEQ, at:at + 65],
                                        ptt[:, h, t, SEQ * b:SEQ * b + SEQ], vv[:, 2 * t + b, h, :],
                                        start=True, stop=True)
                if t % 2 == 1:
                    ins.then_inc(l_o, 1)
            for t in range(TILES):
                pe.wait_ge(l_on, t + 1)
                ins = pe.transpose(bank[4 + t // 4][:, P * (t % 4):P * (t % 4) + P], on3[:, P * t:P * t + P], ident)
                if t % 4 == 3:
                    ins.then_inc(l_ot, 1)
            for t in range(TILES):
                pe.wait_ge(l_ots, t // 4 + 1)
                out = bank[6 + t // 4][:, P * (t % 4):P * (t % 4) + P]
                pe.matmul(out, ot3[:, P * t:P * t + P], W("l3_o"), start=True, stop=False)
                ins = pe.matmul(out, W("ones", rows=1), W("rows", row_at["b3"], P, rows=1), start=False, stop=True)
                if t % 4 == 3:
                    ins.then_inc(l_y, 1)

        def l3x_scalar(a):
            for n in range(2):
                for j in range(2):
                    a.wait_ge(turned, 2 * (6 + n) + j + 1)
                    g_, b_ = (W("l_g"), W("l_b")) if n == 0 else (W("x_g"), W("x_b"))
                    dst = cat_t[:, 8 * j:8 * j + 8, SEQ * (1 - n):SEQ * (2 - n)]
                    a.activation(dst, bank[2 * n + j][:, :].rearrange("p (b s) -> p b s", b=8), ACT.Identity,
                                 bias=b_, scale=g_).then_inc(l_cat, 1)
            for j in range(2):
                a.wait_ge(l_q, j + 1)
                a.copy(qq[:, HALF * j:HALF * j + HALF], bank[j][:, :]).then_inc(l_qq, 1)
            for r in range(8):
                a.wait_ge(l_kv, r + 1)
                src = bank[4 + r % 4][:, :].rearrange("p (b c) -> p b c", b=2)
                a.copy(vv[:, 2 * r:2 * r + 2, :, 0:L_DIM],
                       src[:, :, P:2 * P].rearrange("p b (h d) -> p b h d", h=L_HEADS))
                a.copy(kk[:, 2 * P * r:2 * P * r + 2 * P].rearrange("p (b c) -> p b c", b=2), src[:, :, 0:P])\
                    .then_inc(l_kk, 1)
            for r in range(6):
                a.wait_ge(l_turn, r + 1)
                dst = qt3[:, HALF * r:HALF * r + HALF] if r < 2 else \
                    SCR[:, 7200 + HALF * (r - 2):7200 + HALF * (r - 1)]
                a.mul(dst, bank[r][:, :], W("q_gamma") if r < 2 else W("k_gamma")).then_inc(l_qkt, 1)
            for r in range(4):
                h, part = r % 2, r // 2
                at = 1024 * h + HALF * part
                a.wait_ge(l_sub, r + 1)
                a.activation(pp[:, at:at + HALF], pp[:, at:at + HALF], ACT.Exp).then_inc(l_exp, 1)
            for r in range(4):
                h, part = r % 2, r // 2
                a.wait_ge(l_pt, r + 1)
                a.copy(ptt[:, h, 4 * part:4 * part + 4, :].rearrange("p t q -> p (t q)"), bank[4 + r][:, :])\
                    .then_inc(l_ptt, 1)
            for j in range(2):
                a.wait_ge(l_ot, j + 1)
                a.copy(ot3[:, HALF * j:HALF * j + HALF], bank[4 + j][:, :]).then_inc(l_ots, 1)

        b_abs, b_sum, b_scale, b_tern = sem("b_abs"), sem("b_sum"), sem("b_scale"), sem("b_tern")
        b_t1, b_t1s, b_m, b_w, b_h, b_relu, b_r2, b_y = (sem("b_t1"), sem("b_t1s"), sem("b_m"), sem("b_w"), sem("b_h"),
                                                         sem("b_relu"), sem("b_r2"), sem("b_y"))
        b_abs2, b_sum2, b_wp = sem("b_abs2"), sem("b_sum2"), sem("b_wp")
        wabs = SCR[:, 0:512]
        wscale = SCR[:, 512:1024]
        whalf = SCR[:, 1024:1536]
        wneg = SCR[:, 1536:2048]
        weff = SCR[:, 2048:2560]
        pabs = SCR[:, 2560:3072]
        pscale = SCR[:, 3072:3200]
        phalf = SCR[:, 3200:3328]
        pneg = SCR[:, 3328:3840]
        peff = SCR[:, 3840:4352]
        t1 = SCR[0:RANK, 4352:4864]
        rl = SCR[:, 5120:6144]
        r2 = SCR[:, 6144:10240].rearrange("p (c t) -> p c t", c=CHUNKS)

        def l3f_vector(v, o):
            norm_vector(v, o, x_tile, h_tile, 10)

            def ternary(w, total, n, scale, half, neg, out, shape=None):
                def s(x):
                    return x if shape is None else x[:, None, :].to_broadcast(shape)
                o.link(v.tensor_scalar(scale, total, 1.0 / n, 1e-5, ALU.mult, ALU.max))
                o.link(v.tensor_scalar(half, scale, -0.5, None, ALU.mult))
                o.link(v.tensor_tensor(neg, w, s(half), ALU.is_lt))
                o.link(v.tensor_scalar(half, scale, 0.5, None, ALU.mult))
                o.link(v.tensor_tensor(out, w, s(half), ALU.is_gt))
                o.link(v.tensor_tensor(out, out, neg, ALU.subtract))
                return v.tensor_tensor(out, out, s(scale), ALU.mult)

            v.wait_ge(b_sum, 1)
            o.link(ternary(W("b_fc"), bank[2][:, :], P, wscale, whalf, wneg, weff))
            v.wait_ge(b_m, 1)
            v.scalar_tensor_tensor(weff, bank[3][:, :], W("b_gate"), weff, ALU.mult, ALU.add).then_inc(b_w, 1)
            v.wait_ge(b_sum2, 1)
            shape = [P, CHUNKS, P]

            def by_chunk(x):
                return x.rearrange("p (c d) -> p c d", c=CHUNKS)

            ternary(by_chunk(W("b_proj")), bank[4][:, 0:P], HIDDEN, pscale, phalf, by_chunk(pneg), by_chunk(peff), shape)\
                .then_inc(b_wp, 1)
            for r in range(2 * CHUNKS):
                c, half = r // 2, r % 2
                at = HALF * (r % 2)
                v.wait_ge(b_relu, r + 1)
                v.tensor_tensor(r2[:, c, HALF * half:HALF * half + HALF], rl[:, at:at + HALF], rl[:, at:at + HALF],
                                ALU.mult).then_inc(b_r2, 1)
            for j in range(2):
                v.wait_ge(b_y, j + 1)
                add_to_x(v, 7, j, bank[6 + j][:, :]).then_inc(final_x, 1)

        final_x = sem("final_x")

        def l3f_tensor(pe):
            pe.wait_ge(b_abs, 1)
            pe.matmul(bank[2][:, :], W("ones"), wabs, start=True, stop=True).then_inc(b_sum, 1)
            pe.matmul(bank[3][0:RANK, :], W("b_fb", rows=RANK), W("b_ut", rows=RANK), start=True, stop=True)\
                .then_inc(b_t1, 1)
            pe.wait_ge(b_abs, 2)
            for c in range(CHUNKS):
                ins = pe.matmul(bank[4][:, 0:P], W("ones"), pabs[:, P * c:P * c + P], start=(c == 0), stop=(c == 3))
            ins.then_inc(b_sum2, 1)
            pe.wait_ge(b_t1s, 1)
            pe.matmul(bank[3][:, :], W("b_v", rows=RANK), t1, start=True, stop=True).then_inc(b_m, 1)
            turn_tensor(pe, h_tile, 10)
            pe.wait_ge(b_w, 1)
            for r in range(2 * CHUNKS):
                c, half = r // 2, r % 2
                pe.wait_ge(ht_ready, 12 + half + 1)
                if r >= 2:
                    pe.wait_ge(b_relu, r - 1)
                out = bank[(2, 3)[r % 2]]
                pe.matmul(out[:, :], weff[:, P * c:P * c + P], HT[:, HALF * half:HALF * half + HALF],
                          start=True, stop=True).then_inc(b_h, 1)
            pe.wait_ge(b_wp, 1)
            pe.wait_ge(b_r2, 2 * CHUNKS)
            for t in range(TILES):
                for c in range(CHUNKS):
                    ins = pe.matmul(bank[6 + t // 4][:, P * (t % 4):P * (t % 4) + P], r2[:, c, P * t:P * t + P],
                                    peff[:, P * c:P * c + P], start=(c == 0), stop=(c == CHUNKS - 1))
                if t % 4 == 3:
                    ins.then_inc(b_y, 1)

        def l3f_scalar(a):
            a.activation(wabs, W("b_fc"), ACT.Abs).then_inc(b_abs, 1)
            a.activation(pabs, W("b_proj"), ACT.Abs).then_inc(b_abs, 1)
            a.wait_ge(b_t1, 1)
            a.copy(t1, bank[3][0:RANK, :]).then_inc(b_t1s, 1)
            turn_scalar(a, 8)
            for r in range(2 * CHUNKS):
                at = HALF * (r % 2)
                a.wait_ge(b_h, r + 1)
                if r >= 2:
                    a.wait_ge(b_r2, r - 1)
                a.activation(rl[:, at:at + HALF], bank[(2, 3)[r % 2]][:, :], ACT.Relu).then_inc(b_relu, 1)

        cross1.ht_need, moe.ht_need, cross2.ht_need = 4, 6, 8

        block = ctx.enter_context(nc.Block())

        @block.sync
        def _(sp):
            ends = [0] + group_ends()

            def load_pack(g):
                sp.dma_start(pack[:, ends[g]:ends[g + 1]], d_pack[:, ends[g]:ends[g + 1]]).then_inc(in_pack[g], 16)

            sp.dma_start(Xt, d_x.rearrange("(t p) d -> p t d", p=P)).then_inc(in_x, 16)
            load_pack(0)
            sp.dma_start(CT[:, :], d_ctxt).then_inc(in_ctx, 16)
            sp.dma_start(gates_in[:, :], d_gates).then_inc(in_small, 16)
            load_pack(1)
            sp.dma_start(qpos[:, :], d_qpos).then_inc(in_small, 16)
            sp.dma_start(kpos[:, :], d_kpos).then_inc(in_small, 16)
            sp.dma_start(mask[:, :], d_mask).then_inc(in_small, 16)
            sp.dma_start(keep[0:BATCH, :], d_keep).then_inc(in_small, 16)
            for g in range(2, len(GROUPS)):
                load_pack(g)
            for k in range(8):
                if k < layers:
                    if k == 6:
                        sp.dma_start(Ct, d_ctx.rearrange("(t p) d -> p t d", p=P)).then_inc(in_ctx, 16)
                for g in first_use.get(k + 1, ()):
                    sp.wait_ge(in_pack[g], 16)
                end_layer(sp, k)
            sp.dma_start(d_out.rearrange("(t p) d -> p t d", p=P), Xt).then_inc(out_stored, 16)
            sp.wait_ge(out_stored, 16)

        @block.gpsimd
        def _(g):
            o = Order(g, "pool")
            g.memset(neghalf[:, :], -0.5).then_inc(consts, 1)
            g.wait_ge(consts, 1)
            for k in range(8):
                if k < layers:
                    if k == 0:
                        norm_pool(g, o, 0)
                        g.memset(VM[:, :], 0.0).then_inc(zeroed, 1)
                    elif k == 1:
                        l0f_pool(g, o)
                    elif k == 2:
                        l1x_pool(g, o)
                    elif k == 3:
                        norm_pool(g, o, 3)
                        norm_pool(g, o, 4)
                        attend_pool(g, moe)
                    elif k == 4:
                        l2x_pool(g, o)
                    elif k == 5:
                        norm_pool(g, o, 6)
                    elif k == 6:
                        l3x_pool(g, o)
                    elif k == 7:
                        norm_pool(g, o, 10)
                end_layer(g, k)

        @block.scalar
        def _(a):
            a.wait_ge(in_small, 16 * 5)
            a.activation(gate[:, :], gates_in[:, :], ACT.Tanh).then_inc(gate_ready, 1)
            for k in range(8):
                if k < layers:
                    if k == 0:
                        turn_scalar(a, 0)
                    elif k == 1:
                        turn_scalar(a, 1)
                        l0f_scalar(a)
                    elif k == 2:
                        turn_scalar(a, 2)
                        attend_scalar(a, cross1)
                    elif k == 3:
                        l1f_scalar(a)
                    elif k == 4:
                        turn_scalar(a, 4)
                        attend_scalar(a, cross2)
                    elif k == 5:
                        l2f_scalar(a)
                    elif k == 6:
                        l3x_scalar(a)
                    elif k == 7:
                        l3f_scalar(a)
                end_layer(a, k)

        @block.tensor
        def _(pe):
            for k in range(8):
                if k < layers:
                    if k == 0:
                        l0x_tensor(pe)
                    elif k == 1:
                        turn_tensor(pe, h_tile, 1)
                        l0f_tensor(pe)
                    elif k == 2:
                        turn_tensor(pe, h_tile, 2)
                        attend_tensor(pe, cross1)
                    elif k == 3:
                        l1f_tensor(pe)
                    elif k == 4:
                        l2x_tensor(pe)
                    elif k == 5:
                        l2f_tensor(pe)
                    elif k == 6:
                        l3x_tensor(pe)
                    elif k == 7:
                        l3f_tensor(pe)
                end_layer(pe, k)

        @block.vector
        def _(v):
            o = Order(v, "vector")
            for k in range(8):
                if k < layers:
                    if k == 0:
                        l0x_vector(v, o)
                        v.wait_ge(in_small, 16 * 5)
                        o.link(v.tensor_copy(qposf[:, :], qpos[:, :]))
                        for t in range(TILES):
                            o.mark(v.tensor_scalar(ND[:, SEQ * t:SEQ * t + SEQ], kpos[:, SEQ * t:SEQ * t + SEQ],
                                                   qposf[:, t:t + 1], None, ALU.subtract))
                        o.mark(v.tensor_scalar(MADD[:, :], mask, 0.0, MASKED, ALU.is_equal, ALU.mult))
                    elif k == 1:
                        l0f_vector(v, o)
                    elif k == 2:
                        l1x_vector(v, o)
                    elif k == 3:
                        l1f_vector(v, o)
                    elif k == 4:
                        l2x_vector(v, o)
                    elif k == 5:
                        l2f_vector(v, o)
                    elif k == 6:
                        l3x_vector(v, o)
                    elif k == 7:
                        l3f_vector(v, o)
                end_layer(v, k)


def lay_out(i):
    f = {k: np.asarray(v) for k, v in i.items()}
    blocks = {}

    def put(name, a, rows=P):
        a = np.asarray(a, np.float32) if a.dtype == np.float32 else a
        full = np.zeros((P, OFFSET[name][1]), np.float32)
        full[0:a.shape[0], 0:a.shape[1]] = a
        blocks[name] = full

    def col(a):
        return a.reshape(-1, 1)

    put("ident", np.eye(P, dtype=np.float32))
    put("w1t", f["L0_xattn_W"][:, :DIM].T)
    put("w2t", f["L0_xattn_W"][:, DIM:].T)
    put("ones", np.ones((P, P), np.float32))
    rows = np.zeros((1, 5 * P), np.float32)
    rows[0, 0:P] = f["L0_xattn_b"]
    rows[0, P:2 * P] = f["L3_xattn_b_out"]
    rows[0, 2 * P:2 * P + AE_HID] = f["L1_ffn_rb1"]
    rows[0, 3 * P:3 * P + AE] = f["L1_ffn_rb2"]
    put("rows", rows)
    put("pk_wq", f["L0_ffn_Wq"])
    put("pk_bq", f["L0_ffn_bq"].reshape(2, P).T)
    put("pk_gamma", col(np.concatenate([f["L0_ffn_bn_gamma"]] * 4)))
    put("pk_beta", col(np.concatenate([f["L0_ffn_bn_beta"]] * 4)))
    keys = np.zeros((4, 2, 16, 4, 2, PK_KEYS), np.float32)
    group = np.zeros((4, 2, 16, 4, 2), np.float32)
    for h in range(4):
        for c, k in enumerate((f["L0_ffn_sub_key0"], f["L0_ffn_sub_key1"])):
            keys[h, c, :, h, c, :] = k.T
            group[h, c, :, h, c] = 1.0
    put("pk_keys", keys.reshape(P, 2 * P))
    put("pk_group", group.reshape(P, 8))
    same = np.equal.outer(np.arange(P) % 32, np.arange(P) % 32)
    put("pk_mean", np.where(same, np.float32(1.0 / PK_HEADS), np.float32(0.0)))
    put("pk_down", f["L0_ffn_expert_down"].T)
    put("pk_up", f["L0_ffn_expert_up"])
    for n, k in (("a1_q", "W_q"), ("a1_k", "W_k"), ("a1_v", "W_v"), ("a1_o", "W_o")):
        put(n, f["L1_xattn_" + k].T)
    put("head_rows", np.equal.outer(np.arange(P) // HEAD_DIM, np.arange(HEADS)).astype(np.float32))
    put("r_w1", f["L1_ffn_rW1"].T)
    put("r_g", col(f["L1_ffn_ln_g"]))
    put("r_b", col(f["L1_ffn_ln_b"]))
    put("r_w2", f["L1_ffn_rW2"].T)
    put("e_qb", f["L1_ffn_qb"].T)
    put("e_kb", f["L1_ffn_kb"].T)
    vb = np.zeros((P, AE, AE), np.float32)
    for e in range(AE):
        vb[:, e, e] = f["L1_ffn_vb"][e]
    put("e_vb", vb.reshape(P, AE * AE))
    put("e_ob", f["L1_ffn_ob"])
    for n, k in (("e_q", "qW"), ("e_k", "kW"), ("e_v", "vW"), ("e_o", "oW")):
        put(n, f["L1_ffn_" + k].transpose(2, 0, 1).reshape(P, AE * P))
    turn = np.arange(P).reshape(HEADS, 2, HEAD_DIM // 2)[:, ::-1].reshape(P)
    for n, k in (("q", "Wq"), ("k", "Wk")):
        w = f["L2_xattn_" + k]
        put("a2_" + n, w.T)
        put("a2_" + n + "p", w[turn].T)
    put("a2_v", f["L2_xattn_Wv"].T)
    put("a2_o", f["L2_xattn_Wo"].T)
    freq = 1.0 / 10000.0 ** (np.arange(0, HEAD_DIM, 2, dtype=np.float32) / np.float32(HEAD_DIM))
    angle = np.outer(np.arange(SEQ, dtype=np.float32), freq.astype(np.float32)).astype(np.float32)
    cos = np.tile(np.cos(angle).T, (2 * HEADS, 1))
    sin = np.sin(angle).T
    sin = np.tile(np.concatenate([-sin, sin]), (HEADS, 1))
    put("cosq", (cos * SCALE8).astype(np.float32))
    put("sinq", (sin * SCALE8).astype(np.float32))
    put("cosk", cos.astype(np.float32))
    put("sink", sin.astype(np.float32))
    put("f_gate", f["L2_ffn_gate_w"].T)
    for n, k in (("f_w1", "w1"), ("f_w3", "w3")):
        full = np.zeros((P, 2 * PAIRS, FE_HID), np.float32)
        full[:, 0:FE] = f["L2_ffn_" + k].transpose(2, 0, 1)
        full[:, FE] = f["L2_ffn_s" + k].T
        put(n, full.reshape(P, PAIRS * P))
    full = np.zeros((2, FE_HID, PAIRS, P), np.float32)
    full[:, :, 0:FE // 2] = f["L2_ffn_w2"].transpose(0, 2, 1).reshape(FE // 2, 2, FE_HID, P).transpose(1, 2, 0, 3)
    full[0, :, FE // 2] = f["L2_ffn_sw2"].T
    put("f_w2", full.reshape(P, PAIRS * P))
    for n, k in (("x_g", "ln_x_g"), ("x_b", "ln_x_b"), ("l_g", "ln_l_g"), ("l_b", "ln_l_b")):
        put(n, col(f["L3_xattn_" + k]))
    for n in ("q_gamma", "k_gamma"):
        put(n, col(np.concatenate([f["L3_xattn_" + n]] * L_HEADS)))
    put("l3_q", f["L3_xattn_W_q"])
    put("l3_kv", f["L3_xattn_W_kv"])
    put("l3_o", f["L3_xattn_W_out"])
    put("b_fc", f["L3_ffn_w_fc"].T)
    put("b_proj", f["L3_ffn_w_proj"].T.reshape(CHUNKS, P, P).transpose(1, 0, 2).reshape(P, CHUNKS * P))
    put("b_v", f["L3_ffn_v"])
    put("b_ut", f["L3_ffn_u"].T)
    put("b_fb", f["L3_ffn_fast_b"])
    put("b_gate", np.repeat(f["L3_ffn_gate"].reshape(1, 1), P, axis=0))

    context = f["ctx_1024"].reshape(TOKENS, DIM)
    gates = np.stack([f["g_xattn"], f["g_ffn"]], axis=1).reshape(1, 8)
    kpos = np.repeat(f["itok_BxS2_1_8191"][:, None, :], SEQ, axis=1)

    def by_tile(a):
        return np.ascontiguousarray(a.reshape(TILES, P, -1).transpose(1, 0, 2).reshape(P, -1))

    return {
        "x": np.ascontiguousarray(f["x"].reshape(TOKENS, DIM)),
        "ctx": np.ascontiguousarray(context),
        "ctxt": np.ascontiguousarray(context.T),
        "pack": np.concatenate([blocks[n] for n, _ in PACK], axis=1),
        "gates": np.ascontiguousarray(np.repeat(gates, P, axis=0)),
        "qpos": by_tile(f["itok_BxS_8_8191"].astype(np.int32)),
        "kpos": by_tile(kpos.astype(np.int32)),
        "mask": by_tile(f["mask_BxSxS2_if1"].astype(np.int32)),
        "keep": np.ascontiguousarray(f["mask_BxS2_bk0"].astype(np.int32)),
    }


def kernel(**inputs):
    import concourse.bacc as _bacc
    from concourse.bass_utils import run_bass_kernel_spmd as _run

    nc = _bacc.Bacc("TRN2", target_bir_lowering=False, num_devices=1)
    arrays = {f"in_{name}": a for name, a in lay_out(inputs).items()}
    args = [nc.dram_tensor(name, a.shape, mybir.dt.from_np(a.dtype), kind="ExternalInput").ap()
            for name, a in arrays.items()]
    out = nc.dram_tensor("out", (TOKENS, DIM), F32, kind="ExternalOutput").ap()
    build(nc, *args, out)
    r = _run(nc, [arrays], core_ids=[0])
    return r.results[0]["out"].reshape(BATCH, SEQ, DIM)
```

```python
from contextlib import ExitStack

import numpy as np

import concourse.bass as bass
from concourse import mybir

F32 = mybir.dt.float32
I32 = mybir.dt.int32
BF16 = mybir.dt.bfloat16
ACT = mybir.ActivationFunctionType
ALU = mybir.AluOpType
AX = mybir.AxisListType

P = 128
BATCH, SEQ, DIM = 16, 64, 128
TOKENS = BATCH * SEQ
TILES = TOKENS // P
HEADS, HEAD_DIM = 16, 8
HALF = 512
PK_HEADS, PK_KEYS, PK_TOP = 8, 32, 4
PK_EXPERTS = 128
PK_GROUPS = 2 * PK_HEADS
PK_FAR = PK_EXPERTS // PK_KEYS
AE, AE_HID = 8, 64
FE, FE_HID, FE_TOP = 16, 64, 4
PAIRS = FE // 2 + 1
L_HEADS, L_DIM = 2, 64
KEYS = 2 * SEQ
HIDDEN, RANK = 512, 16
CHUNKS = HIDDEN // P
EPS = 1e-5
MASKED = -1e30
SCALE8 = float(HEAD_DIM ** -0.5)
V_COLS = 32
RING_K, RING_Q, RING_V = 4, 8, 5
PAIRS_H = HEADS // 2
POOL_HEADS = 12

PACK = [
    ("ident", P), ("w1t", P), ("w2t", P), ("ones", P), ("eps", 1),
    ("rows", 5 * P),
    ("pk_wq", 2 * P), ("pk_bq", 2), ("pk_gamma", 1), ("pk_beta", 1), ("pk_keys", 2 * P),
    ("pk_group", 32), ("pk_mean", P), ("pk_down", P), ("pk_up", P),
    ("a1_q", P), ("a1_k", P), ("a1_v", P), ("a1_o", P), ("head_rows", HEADS),
    ("r_w1", AE_HID), ("r_g", 1), ("r_b", 1), ("r_w2", AE),
    ("e_qb", AE), ("e_kb", AE), ("e_vb", AE * AE), ("e_ob", P),
    ("e_q", AE * P), ("e_k", AE * P), ("e_v", AE * P), ("e_o", AE * P),
    ("a2_q", P), ("a2_qp", P), ("a2_k", P), ("a2_kp", P), ("a2_v", P), ("a2_o", P),
    ("cosq", SEQ), ("sinq", SEQ), ("cosk", SEQ), ("sink", SEQ),
    ("f_gate", FE), ("f_w1", PAIRS * P), ("f_w3", PAIRS * P), ("f_w2", PAIRS * P),
    ("x_g", 1), ("x_b", 1), ("l_g", 1), ("l_b", 1), ("q_gamma", 1), ("k_gamma", 1), ("own_rows", P),
    ("l3_q", P), ("l3_kv", 2 * P), ("l3_o", P),
    ("b_fc", HIDDEN), ("b_proj", CHUNKS * P), ("b_v", P), ("b_ut", HIDDEN), ("b_fb", RANK), ("b_gate", 1),
]
OFFSET, _at = {}, 0
for _name, _width in PACK:
    OFFSET[_name] = (_at, _width)
    _at += _width
PACK_COLS = _at
GROUPS = ["rows", "pk_up", "head_rows", "e_ob", "e_o", "sink", "f_w2", "b_gate"]


def group_ends():
    return [OFFSET[name][0] + OFFSET[name][1] for name in GROUPS]


def build(nc, d_x, d_ctx, d_ctxt, d_pack, d_gates, d_qpos, d_kpos, d_mask, d_keep, d_out):
    ctx = ExitStack()
    with ctx:
        def sb(name, cols, dt=F32):
            return ctx.enter_context(nc.sbuf_tensor(name, [P, cols], dt))

        def sem(name):
            return ctx.enter_context(nc.semaphore(name))

        bank = [ctx.enter_context(nc.psum_tensor(f"bank{i}", [P, HALF], F32)) for i in range(8)]

        pack = sb("pack", PACK_COLS)

        def W(name, a=0, n=None, rows=P):
            at, width = OFFSET[name]
            return pack[0:rows, at + a:at + a + (width if n is None else n)]

        X = sb("X", TOKENS)
        H = sb("H", TOKENS)
        HT = sb("HT", TOKENS)
        CT = sb("ctxT", TOKENS)
        KBD = sb("KBD", RING_K * 2 * HEADS * SEQ)
        SCR = sb("scratch", 16384)
        VM = sb("VM", RING_V * 2 * PAIRS_H * V_COLS)
        QT = sb("QT", RING_Q * P)
        KT = sb("KT", RING_Q * P)
        PB = sb("probs", 2 * HEADS * SEQ)
        PTB = sb("probsT", 2 * HEADS * SEQ)
        OTB = sb("heads_outT", 2 * P)
        gates_in = sb("gates_in", 8)
        gate = sb("gate", 8)
        stats = sb("stats", TILES * 6)
        mv = sb("mean_var", TILES * 2)
        rstd = sb("rstd", TILES)
        rowmax = sb("rowmax", HEADS)
        rsum = sb("rsum", 2 * HEADS)
        qpos = sb("qpos", TILES, I32)
        qposf = sb("qposf", TILES)
        kpos = PB[:, 0:TILES * SEQ].bitcast(I32)
        mask = PB[:, TILES * SEQ:2 * TILES * SEQ].bitcast(I32)
        ND = QT[:, 0:TILES * SEQ]
        MADD = QT[:, TILES * SEQ:2 * TILES * SEQ]
        small = sb("small", 512)
        GATES = sb("expert_gates", TILES * AE)
        GT = H[0:AE, :]
        OB = sb("out_bias", P)

        Xt = X[:, :].rearrange("p (t d) -> p t d", t=TILES)
        Ht = H[:, :].rearrange("p (t d) -> p t d", t=TILES)
        Ct = QT[:, :].rearrange("p (t d) -> p t d", t=TILES)
        KBDu = KBD[:, :].rearrange("p (u b h k) -> p u b h k", u=RING_K, b=2, h=HEADS)
        VMu = VM[:, :].rearrange("p (u b j c) -> p u b j c", u=RING_V, b=2, j=PAIRS_H)
        MV = mv[:, :].rearrange("p (t c) -> p t c", c=2)
        STATS = stats[:, :].rearrange("p (t c) -> p t c", c=6)
        ident = W("ident")
        row_at = {"b0": 0, "b3": P, "rb1": 2 * P, "rb2": 3 * P}

        in_x = sem("in_x")
        in_ctx = sem("in_ctx")
        in_gates = sem("in_gates")
        in_small, in_keep = sem("in_small"), sem("in_keep")
        in_pack = [sem(f"in_pack_{g}") for g in GROUPS]
        layer_end = sem("layer_end")
        own = {e: sem(f"own_{e}") for e in ("vector", "pool", "scalar")}
        zeroed = sem("zeroed")
        gate_ready = sem("gate_ready")
        var_ready = sem("var_ready")
        std_ready = sem("std_ready")
        normed = sem("normed")
        turned = sem("turned")
        ht_ready = sem("ht_ready")
        l0_out = sem("l0_out")
        ctx_mean = sem("ctx_mean")
        out_stored = sem("out_stored")

        class Order:

            def __init__(self, eng, name):
                self.eng, self.sem, self.n = eng, own[name], 0

            def mark(self, ins):
                ins.then_inc(self.sem, 1)
                self.n += 1

            def settle(self):
                self.eng.wait_ge(self.sem, self.n)

            def link(self, ins):
                self.mark(ins)
                self.settle()

        def end_layer(eng, k):
            eng.drain().then_inc(layer_end, 1)
            eng.wait_ge(layer_end, 5 * (k + 1))

        first_use = {0: (0,), 1: (1,), 2: (2,), 3: (3, 4), 4: (5,), 5: (6, 7)}

        def norm_vector(v, order, src, dst, n, meanwhile=None):
            for t in range(TILES):
                order.mark(v.bn_stats(STATS[:, t, :], src(t)))
            order.settle()
            for t in range(TILES):
                ins = v.bn_aggr(MV[:, t, :], STATS[:, t, :])
                if t % 4 == 3:
                    ins.then_inc(var_ready, 1)
            if meanwhile is not None:
                meanwhile()
            for j in range(2):
                v.wait_ge(std_ready, 2 * n + j + 1)
                order.link(v.reciprocal(rstd[:, 4 * j:4 * j + 4], rstd[:, 4 * j:4 * j + 4]))
                for t in range(4 * j, 4 * j + 4):
                    v.tensor_scalar(dst(t), src(t), MV[:, t, 0:1], rstd[:, t:t + 1], ALU.subtract, ALU.mult)\
                        .then_inc(normed, 1)

        def norm_scalar(a, n):
            for j in range(2):
                a.wait_ge(var_ready, 2 * n + j + 1)
                a.activation(rstd[:, 4 * j:4 * j + 4], MV[:, 4 * j:4 * j + 4, 1], ACT.Sqrt, bias=W("eps"))\
                    .then_inc(std_ready, 1)

        def turn_tensor(pe, src, norm_n, banks=(0, 1)):
            for t in range(TILES):
                pe.wait_ge(normed, TILES * norm_n + t + 1)
                ins = pe.transpose(bank[banks[t // 4]][:, P * (t % 4):P * (t % 4) + P], src(t), ident)
                if t % 4 == 3:
                    ins.then_inc(turned, 1)

        def turn_scalar(a, n, banks=(0, 1)):
            for j in range(2):
                a.wait_ge(turned, 2 * n + j + 1)
                a.copy(HT[:, HALF * j:HALF * j + HALF], bank[banks[j]][:, :]).then_inc(ht_ready, 1)

        def x_tile(t):
            return Xt[:, t, :]

        def h_tile(t):
            return Ht[:, t, :]

        def ht(t, n=1):
            return HT[:, P * t:P * (t + n)]

        def add_to_x(v, k, half, src):
            xs = X[:, HALF * half:HALF * half + HALF]
            return v.scalar_tensor_tensor(xs, src, gate[:, k:k + 1], xs, ALU.mult, ALU.add)

        CS = small[:, 0:BATCH]
        CSB = SCR[:, 0:TOKENS]

        def l0x_vector(v, o):
            v.wait_ge(in_x, 16)
            norm_vector(v, o, x_tile, h_tile, 0, meanwhile=lambda: context_mean_vector(v, o))
            v.wait_ge(gate_ready, 1)
            for j in range(2):
                v.wait_ge(l0_out, j + 1)
                add_to_x(v, 0, j, bank[2 + j][:, :])

        def context_mean_vector(v, o):
            v.wait_ge(in_ctx, 16)
            o.link(v.tensor_reduce(CS, CT[:, :].rearrange("p (b s) -> p b s", b=BATCH), AX.X, ALU.add))
            v.tensor_scalar(CSB.rearrange("p (b s) -> p b s", b=BATCH),
                            CS[:, :, None].to_broadcast([P, BATCH, SEQ]), 1.0 / SEQ, None, ALU.mult)\
                .then_inc(ctx_mean, 1)

        def four_rows(pe, k, name, width=P, n=4):
            row = W("rows", row_at[name], width, rows=1)[:, None, :].to_broadcast([1, n, width])
            pe.matmul(bank[k][:, 0:n * width].rearrange("p (n w) -> p n w", n=n), W("ones", rows=1), row,
                      start=True, stop=False)

        def l0x_tensor(pe):
            pe.wait_ge(in_pack[0], 16)
            four_rows(pe, 2, "b0")
            four_rows(pe, 3, "b0")
            turn_tensor(pe, h_tile, 0)
            pe.wait_ge(ctx_mean, 1)
            for t in range(TILES):
                pe.matmul(bank[2 + t // 4][:, P * (t % 4):P * (t % 4) + P], CSB[:, P * t:P * t + P], W("w2t"),
                          start=False, stop=False)
            for t in range(TILES):
                pe.wait_ge(ht_ready, t // 4 + 1)
                ins = pe.matmul(bank[2 + t // 4][:, P * (t % 4):P * (t % 4) + P], ht(t), W("w1t"),
                                start=False, stop=(t % 4 == 3))
                if t % 4 == 3:
                    ins.then_inc(l0_out, 1)

        qa = SCR[:, 0:2048].rearrange("p (a t) -> p a t", a=2)
        qn = SCR[:, 2048:4096].rearrange("p (a t) -> p a t", a=2)
        sq = SCR[:, 4096:6144].rearrange("p (a t) -> p a t", a=2)
        sc = SCR[:, 6144:10240].rearrange("p (t g k) -> p t g k", t=TILES, g=PK_GROUPS)
        mk = SCR[:, 10240:14336].rearrange("p (t g k) -> p t g k", t=TILES, g=PK_GROUPS)
        pw = SCR[:, 14336:16384].rearrange("p (b h i k) -> p b h i k", b=2, h=PK_HEADS, i=PK_FAR)
        gelu_t = SCR[:, 0:1024]
        wg = SCR[:, 2048:3072]
        wexp = SCR[:, 3072:4096].rearrange("p (t e) -> p t e", t=TILES)
        keybd = PTB[:, 576:576 + 2 * P]
        keysq = PTB[:, 832:832 + 2 * P]
        pkst = small[:, 0:64]
        n2 = PTB[:, 1088:1088 + HALF]
        rn = small[:, 192:320]
        top8 = small[:, 320:448]
        totals = small[:, 448:464]
        rtot = small[:, 464:480]
        rem = small[:, 480:488]
        near = small[:, 488:496]
        farw = small[:, 496:504]
        p0n = PTB[:, 0:TILES * PK_HEADS * PK_FAR]
        p0nt = p0n[:, :].rearrange("p (t h i) -> p t h i", t=TILES, h=PK_HEADS)
        knorm = PTB[:, 512:512 + 2 * PK_KEYS]
        pk_q, pk_qa = sem("pk_q"), sem("pk_qa")
        pk_keysq, pk_keysum, pk_keyn2, pk_keyr = sem("pk_keysq"), sem("pk_keysum"), sem("pk_keyn2"), sem("pk_keyr")
        pk_keyready = sem("pk_keyready")
        pk_rowstat, pk_stat, pk_qvar, pk_qrstd = sem("pk_rowstat"), sem("pk_stat"), sem("pk_qvar"), sem("pk_qrstd")
        pk_qn, pk_sq, pk_score, pk_norm2 = sem("pk_qn"), sem("pk_sq"), sem("pk_score"), sem("pk_norm2")
        pk_n2, pk_rn, pk_sc, pk_exp = sem("pk_n2"), sem("pk_rn"), sem("pk_sc"), sem("pk_exp")
        pk_p0, pk_pw, pk_w, pk_wt, pk_wg = sem("pk_p0"), sem("pk_pw"), sem("pk_w"), sem("pk_wt"), sem("pk_wg")
        pk_eh, pk_gelu, pk_out, pk_pwread = sem("pk_eh"), sem("pk_gelu"), sem("pk_out"), sem("pk_pwread")
        pk_n2t = sem("pk_n2t")
        pk_mask, pk_chosen = sem("pk_mask"), sem("pk_chosen")

        def l0f_ahead_vector(v, o):
            v.tensor_tensor(keysq, W("pk_keys"), W("pk_keys"), ALU.mult).then_inc(pk_keysq, 1)
            v.wait_ge(in_small, 16 * 3)
            o.link(v.tensor_copy(qposf[:, :], qpos[:, :]))
            for t in range(TILES):
                o.mark(v.tensor_scalar(ND[:, SEQ * t:SEQ * t + SEQ], kpos[:, SEQ * t:SEQ * t + SEQ],
                                       qposf[:, t:t + 1], None, ALU.subtract))
            o.mark(v.tensor_scalar(MADD[:, :], mask, 0.0, MASKED, ALU.is_equal, ALU.mult))

        def l0f_keys_vector(v, o):
            v.wait_ge(pk_keysum, 1)
            v.tensor_scalar(knorm, bank[2][:, 0:2 * PK_KEYS], 1e-24, None, ALU.max).then_inc(pk_keyn2, 1)

        def l0f_spread_keys_vector(v, o):
            v.wait_ge(pk_keyr, 1)
            o.link(v.reciprocal(knorm, knorm))
            shape = [P, 4, 2 * PK_KEYS]
            v.tensor_tensor(keybd.rearrange("p (h k) -> p h k", h=4), W("pk_keys").rearrange("p (h k) -> p h k", h=4),
                            knorm[:, None, :].to_broadcast(shape), ALU.mult).then_inc(pk_keyready, 1)

        def l0f_vector(v, o):
            norm_vector(v, o, x_tile, h_tile, 1, meanwhile=lambda: l0f_ahead_vector(v, o))
            l0f_keys_vector(v, o)
            st = pkst[:, 0:24].rearrange("p (a c) -> p a c", a=4)
            agg = pkst[:, 24:28].rearrange("p (a c) -> p a c", a=2)
            for a_ in range(2):
                for j in range(2):
                    v.wait_ge(pk_qa, 2 * a_ + j + 1)
                    o.mark(v.bn_stats(st[:, 2 * a_ + j, :], qa[:, a_, HALF * j:HALF * j + HALF]))
            o.settle()
            for a_ in range(2):
                o.mark(v.bn_aggr(agg[:, a_, :], st[:, 2 * a_:2 * a_ + 2, :].rearrange("p a c -> p (a c)")))
            o.settle()
            msq = pkst[:, 28:30]
            o.link(v.tensor_tensor(msq, agg[:, :, 0], agg[:, :, 0], ALU.mult))
            v.tensor_tensor(agg[:, :, 1], agg[:, :, 1], msq, ALU.add).then_inc(pk_rowstat, 1)
            v.wait_ge(pk_stat, 1)
            stat = pkst[:, 30:32]
            o.link(v.tensor_copy(stat, bank[2][:, 0:2]))
            mean2, qvar = pkst[:, 32:33], pkst[:, 33:34]
            o.link(v.tensor_tensor(mean2, stat[:, 0:1], stat[:, 0:1], ALU.mult))
            o.link(v.tensor_tensor(qvar, stat[:, 1:2], mean2, ALU.subtract))
            v.tensor_scalar(pkst[:, 34:35], qvar, EPS, None, ALU.add).then_inc(pk_qvar, 1)
            v.wait_ge(pk_qrstd, 1)
            scale, shift = pkst[:, 36:37], pkst[:, 37:38]
            o.link(v.reciprocal(pkst[:, 35:36], pkst[:, 35:36]))
            o.link(v.tensor_tensor(scale, pkst[:, 35:36], W("pk_gamma"), ALU.mult))
            o.link(v.tensor_tensor(pkst[:, 38:39], stat[:, 0:1], scale, ALU.mult))
            o.link(v.tensor_tensor(shift, W("pk_beta"), pkst[:, 38:39], ALU.subtract))
            for a_ in range(2):
                v.tensor_scalar(qn[:, a_, :], qa[:, a_, :], scale, shift, ALU.mult, ALU.add).then_inc(pk_qn, 1)
            l0f_spread_keys_vector(v, o)
            v.wait_ge(pk_norm2, 1)
            v.tensor_scalar(n2, bank[3][:, :], 1e-24, None, ALU.max).then_inc(pk_n2, 1)
            v.wait_ge(pk_rn, 2)
            o.link(v.reciprocal(rn, rn))
            rng = rn.rearrange("p (t g) -> p t g", t=TILES)
            fourth = top8.rearrange("p (g k) -> p g k", g=PK_GROUPS)[:, :, PK_TOP - 1:PK_TOP]
            for step in range(TILES + 2):
                t = step
                if t < TILES:
                    v.wait_ge(pk_score, t + 1)
                    v.tensor_tensor(sc[:, t], bank[4 + t % 4][:, :].rearrange("p (g k) -> p g k", g=PK_GROUPS),
                                    rng[:, t, :, None].to_broadcast([P, PK_GROUPS, PK_KEYS]), ALU.mult)\
                        .then_inc(pk_sc, 1)
                    v.wait_ge(pk_sc, t + 1)
                    for g_ in range(PK_GROUPS):
                        o.mark(v.max(top8[:, 8 * g_:8 * g_ + 8], sc[:, t, g_, :]))
                    o.settle()
                    v.tensor_tensor(mk[:, t], sc[:, t], fourth.to_broadcast([P, PK_GROUPS, PK_KEYS]), ALU.is_ge)\
                        .then_inc(pk_mask, 1)
                t = step - 1
                if 0 <= t < TILES:
                    v.wait_ge(pk_chosen, t + 1)
                    first = mk[:, t].rearrange("p (h c) k -> p h c k", c=2)[:, :, 0, :]
                    o.mark(v.tensor_reduce(totals, mk[:, t], AX.X, ALU.add))
                    o.mark(v.tensor_reduce(rem, first[:, :, PK_FAR:PK_KEYS], AX.X, ALU.add))
                    o.settle()
                    o.link(v.reciprocal(rtot, totals))
                    rt = rtot.rearrange("p (h c) -> p h c", c=2)
                    o.mark(v.tensor_tensor(near, rt[:, :, 0], rt[:, :, 1], ALU.mult))
                    o.mark(v.tensor_tensor(rem, rem, rt[:, :, 0], ALU.mult))
                    o.settle()
                    v.tensor_tensor(p0nt[:, t], first[:, :, 0:PK_FAR],
                                    near[:, :, None].to_broadcast([P, PK_HEADS, PK_FAR]), ALU.mult).then_inc(pk_p0, 1)
                    o.mark(v.tensor_reduce(farw[:, t:t + 1], rem, AX.X, ALU.add))
                t = step - 2
                if 0 <= t < TILES:
                    v.wait_ge(pk_pw, t + 1)
                    v.tensor_reduce(wexp[:, t, :], pw[:, t % 2].rearrange("p h i k -> p (i k) h"), AX.X, ALU.add)\
                        .then_inc(pk_pwread, 1)
                    v.wait_ge(pk_pwread, t + 1)
                    last = wexp[:, t, PK_EXPERTS - 1:PK_EXPERTS]
                    v.tensor_tensor(last, last, farw[:, t:t + 1], ALU.add).then_inc(pk_w, 1)
            for j in range(2):
                v.wait_ge(pk_wt, j + 1)
                v.wait_ge(pk_gelu, j + 1)
                v.tensor_tensor(wg[:, HALF * j:HALF * j + HALF], bank[j][:, :],
                                gelu_t[:, HALF * j:HALF * j + HALF], ALU.mult).then_inc(pk_wg, 1)
            for j in range(2):
                v.wait_ge(pk_out, j + 1)
                add_to_x(v, 1, j, bank[4 + j][:, :])

        def l0f_tensor(pe):
            pe.wait_ge(pk_keysq, 1)
            pe.matmul(bank[2][:, 0:2 * P], W("ones"), keysq, start=True, stop=True).then_inc(pk_keysum, 1)
            for a_ in range(2):
                for j in range(2):
                    pe.wait_ge(ht_ready, 2 * 1 + j + 1)
                    pe.matmul(bank[4 + 2 * a_ + j][:, :], W("pk_wq", P * a_, P), HT[:, HALF * j:HALF * j + HALF],
                              start=True, stop=True).then_inc(pk_q, 1)
            pe.wait_ge(pk_keyn2, 1)
            pe.wait_ge(pk_rowstat, 1)
            agg = pkst[:, 24:28].rearrange("p (a c) -> p a c", a=2)
            for a_ in range(2):
                ins = pe.matmul(bank[2][:, 0:2], W("pk_mean"), agg[:, a_, :], start=(a_ == 0), stop=(a_ == 1))
            ins.then_inc(pk_stat, 1)
            for a_ in range(2):
                pe.wait_ge(pk_sq, a_ + 1)
            for j in range(2):
                for a_ in range(2):
                    at = 64 * j + 32 * a_
                    ins = pe.matmul(bank[3][at:at + 32, :], W("pk_group"), sq[:, a_, HALF * j:HALF * j + HALF],
                                    start=True, stop=True)
            ins.then_inc(pk_norm2, 1)
            pe.wait_ge(pk_qvar, 1)
            pe.wait_ge(pk_n2, 1)
            for c in range(4):
                ins = pe.transpose(bank[2][:, P * c:P * c + P], n2[:, P * c:P * c + P], ident)
            ins.then_inc(pk_n2t, 1)
            pe.wait_ge(pk_qa, 4)
            pe.wait_ge(pk_keyready, 1)
            for t in range(TILES):
                if t >= 4:
                    pe.wait_ge(pk_sc, t - 3)
                for a_ in range(2):
                    ins = pe.matmul(bank[4 + t % 4][:, 2 * P * a_:2 * P * a_ + 2 * P], qn[:, a_, P * t:P * t + P],
                                    keybd, start=True, stop=True)
                ins.then_inc(pk_score, 1)
            pe.wait_ge(pk_stat, 1)
            for j in range(2):
                if j == 0:
                    pe.wait_ge(pk_rn, 2)
                pe.matmul(bank[2 + j][:, :], W("pk_down"), HT[:, HALF * j:HALF * j + HALF],
                          start=True, stop=True).then_inc(pk_eh, 1)
            for t in range(TILES):
                pe.wait_ge(pk_w, t + 1)
                ins = pe.transpose(bank[t // 4][:, P * (t % 4):P * (t % 4) + P], wexp[:, t, :], ident)
                if t % 4 == 3:
                    ins.then_inc(pk_wt, 1)
            pe.wait_ge(pk_sc, TILES)
            for t in range(TILES):
                pe.wait_ge(pk_wg, t // 4 + 1)
                ins = pe.matmul(bank[4 + t // 4][:, P * (t % 4):P * (t % 4) + P], wg[:, P * t:P * t + P], W("pk_up"),
                                start=True, stop=True)
                if t % 4 == 3:
                    ins.then_inc(pk_out, 1)

        def l0f_scalar(a):
            a.wait_ge(pk_keyn2, 1)
            a.activation(knorm, knorm, ACT.Sqrt).then_inc(pk_keyr, 1)
            for a_ in range(2):
                for j in range(2):
                    a.wait_ge(pk_q, 2 * a_ + j + 1)
                    a.activation(qa[:, a_, HALF * j:HALF * j + HALF], bank[4 + 2 * a_ + j][:, :], ACT.Identity,
                                 bias=W("pk_bq", a_, 1)).then_inc(pk_qa, 1)
            position_bias_scalar(a, range(0, 5))
            a.wait_ge(pk_qvar, 1)
            a.activation(pkst[:, 35:36], pkst[:, 34:35], ACT.Sqrt).then_inc(pk_qrstd, 1)
            for a_ in range(2):
                a.wait_ge(pk_qn, a_ + 1)
                a.activation(sq[:, a_, :], qn[:, a_, :], ACT.Square).then_inc(pk_sq, 1)
            position_bias_scalar(a, range(5, 13))
            a.wait_ge(pk_n2t, 1)
            for j in range(2):
                src = bank[2][:, :].rearrange("p (c j a g) -> p j c a g", c=4, j=2, a=2)[:, j, :, :, 0:8]
                a.activation(rn[:, 64 * j:64 * j + 64].rearrange("p (c a g) -> p c a g", c=4, a=2), src, ACT.Sqrt)\
                    .then_inc(pk_rn, 1)
            position_bias_scalar(a, range(13, HEADS))
            for t in range(TILES):
                a.wait_ge(pk_mask, t + 1)
                a.activation(sc[:, t], sc[:, t], ACT.Exp).then_inc(pk_exp, 1)
            for j in range(2):
                a.wait_ge(pk_eh, j + 1)
                a.activation(gelu_t[:, HALF * j:HALF * j + HALF], bank[2 + j][:, :], ACT.Gelu).then_inc(pk_gelu, 1)

        def l0f_pool(g, o):
            g.wait_ge(a_sloped, 1)
            for step in range(TILES + 1):
                t = step
                if t < TILES:
                    g.wait_ge(pk_exp, t + 1)
                    g.tensor_tensor(mk[:, t], mk[:, t], sc[:, t], ALU.mult).then_inc(pk_chosen, 1)
                t = step - 1
                if 0 <= t < TILES:
                    g.wait_ge(pk_p0, t + 1)
                    if t >= 2:
                        g.wait_ge(pk_pwread, t - 1)
                    second = mk[:, t].rearrange("p (h c) k -> p h c k", c=2)[:, :, 1, :]
                    shape = [P, PK_HEADS, PK_FAR, PK_KEYS]
                    g.tensor_tensor(pw[:, t % 2], p0nt[:, t][:, :, :, None].to_broadcast(shape),
                                    second[:, :, None, :].to_broadcast(shape), ALU.mult).then_inc(pk_pw, 1)
                    position_mask_pool(g, t)

        a_proj, a_q, a_k, a_v = sem("a_proj"), sem("a_q"), sem("a_k"), sem("a_v")
        a_kbd = [sem("a_kbd_pool"), sem("a_kbd_scalar")]
        a_s, a_sub, a_exp = sem("a_s"), sem("a_sub"), sem("a_exp")
        a_t, a_r = sem("a_t"), sem("a_r")
        a_norm = [sem("a_norm_pool"), sem("a_norm_vector")]
        a_sum, a_inv, a_max = sem("a_sum"), sem("a_inv"), sem("a_max")
        a_pt = [sem("a_pt0"), sem("a_pt1")]
        a_pv, a_ots, a_out, a_x = sem("a_pv"), sem("a_ots"), sem("a_out"), sem("a_x")
        a_sloped = sem("a_sloped")
        rope_q, rope_k = sem("rope_q"), sem("rope_k")
        lead_s, lead_n, lead_t, lead_pv, lead_out = 2, 3, 4, 5, 6

        class Attention:

            def __init__(self, first, experts, tiles_before, gate_k, wq, wk, wv, wo, self_kv, rope=False, biased=False,
                         keys=None):
                self.first, self.experts, self.n = first, experts, experts * TILES
                self.tiles_before, self.gate_k = tiles_before, gate_k
                self.wq, self.wk, self.wv, self.wo = wq, wk, wv, wo
                self.self_kv, self.rope, self.biased, self.keys = self_kv, rope, biased, keys

        spread_keys = SCR[:, 0:8192].rearrange("p (u b h k) -> p u b h k", u=RING_K, b=2, h=HEADS)
        cross1 = Attention(0, 1, 0, 2, "a1_q", "a1_k", "a1_v", "a1_o", False, biased=True, keys=spread_keys)
        moe = Attention(8, AE, 8, 3, "e_q", "e_k", "e_v", "e_o", True, keys=KBDu)
        cross2 = Attention(8 + 8 * AE, 1, 16, 4, None, None, "a2_v", "a2_o", False, rope=True, keys=KBDu)
        bias1 = KBD[:, :].rearrange("p (t h k) -> p t h k", t=TILES, h=HEADS)
        S_BANK, PT_BANK, O_BANK, PJ_BANK, Y_BANK = (0, 1), (2, 3), 4, (5, 6), 7
        PROJECTED = cross1.n + moe.n
        qb_scaled = sb("qb_scaled", AE)

        def attend_tensor(pe, A, steps=None):
            for s in steps or range(A.n + lead_out + 1):
                i = s - lead_t
                if 0 <= i < A.n:
                    g = A.first + i
                    for half in range(2):
                        pe.wait_ge(a_norm[half], g + 1)
                        if g > 0:
                            pe.wait_ge(a_pt[half], g)
                        for j in range(4):
                            at = 1024 * (g % 2) + HALF * half + P * j
                            ins = pe.transpose(bank[PT_BANK[half]][:, P * j:P * j + P], PB[:, at:at + P], ident)
                        ins.then_inc(a_t, 1)
                i = s - lead_s
                if 0 <= i < A.n:
                    g = A.first + i
                    if A.rope:
                        pe.wait_ge(rope_q, 2)
                    else:
                        pe.wait_ge(a_q, g + 1)
                    pe.wait_ge(a_kbd[0], g + 1)
                    pe.wait_ge(a_kbd[1], g + 1)
                    q0 = P * (g % RING_Q)
                    for half in range(2):
                        if g > 0:
                            pe.wait_ge(a_sub, 2 * (g - 1) + half + 1)
                        if A.biased:
                            pe.matmul(bank[S_BANK[half]][:, :], ident,
                                      bias1[:, i, 8 * half:8 * half + 8, :].rearrange("p h k -> p (h k)"),
                                      start=True, stop=False)
                        for b in range(2):
                            ins = pe.matmul(bank[S_BANK[half]][SEQ * b:SEQ * b + SEQ, :],
                                            QT[:, q0 + SEQ * b:q0 + SEQ * b + SEQ],
                                            A.keys[:, g % RING_K, b, 8 * half:8 * half + 8, :]
                                            .rearrange("p h k -> p (h k)"), start=not A.biased, stop=True)
                        ins.then_inc(a_s, 1)
                i = s - lead_pv
                if 0 <= i < A.n:
                    g = A.first + i
                    pe.wait_ge(a_v, g + 1)
                    for half in range(2):
                        pe.wait_ge(a_pt[half], g + 1)
                    if g > 0:
                        pe.wait_ge(a_ots, g)
                    for b in range(2):
                        for j in (0, 2, 4, 6, 1, 3, 5, 7):
                            at = 1024 * (g % 2) + P * j + SEQ * b
                            ins = pe.matmul(bank[O_BANK][V_COLS * (j // 2):V_COLS * (j // 2 + 1), SEQ * b:SEQ * b + SEQ],
                                            VMu[:, g % RING_V, b, j, :], PTB[:, at:at + SEQ],
                                            start=(j % 2 == 0), stop=(j % 2 == 1))
                    ins.then_inc(a_pv, 1)
                i = s
                if i < A.n:
                    g, t, e = A.first + i, i // A.experts, i % A.experts
                    if g > 1:
                        pe.wait_ge(a_v, g - 1)
                    pe.wait_ge(ht_ready, A.ht_need + 2)
                    kv = HT if A.self_kv else CT
                    pj = bank[PJ_BANK[g % 2]]
                    if not A.rope:
                        pe.matmul(pj[:, 0:P], W(A.wk, P * e, P), kv[:, P * t:P * t + P], start=True, stop=True)
                        pe.matmul(pj[:, P:2 * P], W(A.wq, P * e, P), ht(t), start=True, stop=True)
                    for b in range(2):
                        src = kv[:, P * t + SEQ * b:P * t + SEQ * b + SEQ]
                        for half in range(2):
                            ins = pe.matmul(pj[SEQ * half:SEQ * half + SEQ, P * (2 + b):P * (3 + b)], src,
                                            W(A.wv, P * e, P), start=True, stop=True)
                    ins.then_inc(a_proj, 1)
                i = s - lead_out
                if 0 <= i < A.n:
                    g, t, e = A.first + i, i // A.experts, i % A.experts
                    pe.wait_ge(a_ots, g + 1)
                    y = bank[Y_BANK][:, 0:P]
                    if e == 0:
                        if A.tiles_before + t > 0:
                            pe.wait_ge(a_x, A.tiles_before + t)
                        if A.experts > 1:
                            pe.wait_ge(r_ready, 3)
                            pe.matmul(y, GT[0:AE, P * t:P * t + P], OB[0:AE, :], start=True, stop=False)
                    pe.matmul(y, OTB[:, P * (g % 2):P * (g % 2) + P], W(A.wo, P * e, P),
                              start=(A.experts == 1), stop=(e == A.experts - 1)).then_inc(a_out, 1)

        def attend_scalar(a, A, steps=None):
            for s in steps or range(A.n + lead_pv + 1):
                i = s - 1
                if 0 <= i < A.n:
                    g, e = A.first + i, i % A.experts
                    a.wait_ge(a_proj, g + 1)
                    pj, q0 = bank[PJ_BANK[g % 2]], P * (g % RING_Q)
                    if not A.rope:
                        if g >= RING_Q:
                            a.wait_ge(a_kbd[0], g - RING_Q + 1)
                            a.wait_ge(a_s, 2 * (g - RING_Q + 1))
                        if A.experts > 1:
                            a.activation(KT[:, q0:q0 + P], pj[:, 0:P], ACT.Identity, bias=W("e_kb", e, 1))\
                                .then_inc(a_k, 1)
                            a.activation(QT[:, q0:q0 + P], pj[:, P:2 * P], ACT.Identity,
                                         bias=qb_scaled[:, e:e + 1], scale=SCALE8).then_inc(a_q, 1)
                        else:
                            a.copy(KT[:, q0:q0 + P], pj[:, 0:P]).then_inc(a_k, 1)
                            a.mul(QT[:, q0:q0 + P], pj[:, P:2 * P], SCALE8).then_inc(a_q, 1)
                    if A.rope:
                        a.wait_ge(rope_k, 2)
                    else:
                        a.wait_ge(a_k, g + 1)
                    if g >= RING_K:
                        a.wait_ge(a_s, 2 * (g - RING_K + 1))
                    keys = KT[:, q0:q0 + P].rearrange("p (b k) -> p b k", b=2)
                    for h in range(POOL_HEADS, HEADS):
                        ins = a.mul(A.keys[:, g % RING_K, :, h, :], keys, W("head_rows", h, 1))
                    ins.then_inc(a_kbd[1], 1)
                    if g >= RING_V:
                        a.wait_ge(a_pv, g - RING_V + 1)
                    for half in range(2):
                        rows = slice(SEQ * half, SEQ * half + SEQ)
                        src = pj[rows, 2 * P:4 * P].rearrange("p (m j c d) -> p m j c d", m=PAIRS_H, j=2, c=2)
                        dst = VMu[rows, g % RING_V].rearrange("p b j c -> p (b j c)")\
                            .rearrange("p (m x c d) -> p m x c d", m=PAIRS_H, x=4, c=2)
                        ins = a.copy(dst[:, :, 0:4:3, half, :], src[:, :, :, half, :])
                    ins.then_inc(a_v, 1)
                i = s - lead_t
                if 0 <= i < A.n:
                    g = A.first + i
                    for half in range(2):
                        a.wait_ge(a_t, 2 * g + half + 1)
                        if g >= 2:
                            a.wait_ge(a_pv, g - 1)
                        at = 1024 * (g % 2) + HALF * half
                        a.copy(PTB[:, at:at + HALF], bank[PT_BANK[half]][:, :]).then_inc(a_pt[half], 1)
                i = s - lead_pv
                if 0 <= i < A.n:
                    g = A.first + i
                    a.wait_ge(a_pv, g + 1)
                    if g >= 2:
                        a.wait_ge(a_out, g - 1)
                    a.copy(OTB[:, P * (g % 2):P * (g % 2) + P], bank[O_BANK][:, 0:P]).then_inc(a_ots, 1)
                i = s - lead_s
                if 0 <= i < A.n:
                    g = A.first + i
                    for half in range(2):
                        a.wait_ge(a_sub, 2 * g + half + 1)
                        at = 1024 * (g % 2) + HALF * half
                        a.activation(PB[:, at:at + HALF], PB[:, at:at + HALF], ACT.Exp).then_inc(a_exp, 1)

        def attend_vector(v, o, A):
            for s in range(lead_s, A.n + lead_out + 2):
                i = s - lead_n
                if 0 <= i < A.n:
                    g, t, e = A.first + i, i // A.experts, i % A.experts
                    probs = PB[:, 1024 * (g % 2):1024 * (g % 2) + 1024].rearrange("p (h k) -> p h k", h=HEADS)
                    r = rsum[:, 8 * (g % 2):8 * (g % 2) + 8]
                    sums = (rsum[:, 16:24], rsum[:, 24:32])
                    gated = GATES[:, AE * t + e:AE * t + e + 1] if A.experts > 1 else W("ones", 0, 1)
                    for half in range(2):
                        v.wait_ge(a_exp, 2 * g + half + 1)
                        v.tensor_reduce(sums[half], probs[:, 8 * half:8 * half + 8], AX.X, ALU.add)\
                            .then_inc(a_sum, 1)
                    for half in range(2):
                        v.wait_ge(a_sum, 2 * g + half + 1)
                        if A.biased:
                            o.link(v.tensor_scalar(sums[half], sums[half], 1.0, None, ALU.add))
                        v.reciprocal(sums[half], sums[half]).then_inc(a_inv, 1)
                    v.wait_ge(a_inv, 2 * g + 1)
                    v.tensor_scalar(r, sums[0], gated, None, ALU.mult).then_inc(a_r, 1)
                    v.wait_ge(a_inv, 2 * g + 2)
                    v.scalar_tensor_tensor(probs[:, 8:16], probs[:, 8:16], gated,
                                           sums[1][:, :, None].to_broadcast([P, 8, SEQ]), ALU.mult, ALU.mult)\
                        .then_inc(a_norm[1], 1)
                i = s - lead_out - 1
                if 0 <= i < A.n and i % A.experts == A.experts - 1:
                    g, t = A.first + i, i // A.experts
                    v.wait_ge(a_out, g + 1)
                    v.scalar_tensor_tensor(Xt[:, t, :], bank[Y_BANK][:, 0:P], gate[:, A.gate_k:A.gate_k + 1],
                                           Xt[:, t, :], ALU.mult, ALU.add).then_inc(a_x, 1)
                i = s - lead_s
                if 0 <= i < A.n:
                    g = A.first + i
                    parts = []
                    for half in range(2):
                        at = 1024 * (g % 2) + HALF * half
                        parts.append((PB[:, at:at + HALF].rearrange("p (h k) -> p h k", h=8),
                                      bank[S_BANK[half]][:, :].rearrange("p (h k) -> p h k", h=8),
                                      rowmax[:, 8 * half:8 * half + 8]))
                    for half, (probs, scores, m) in enumerate(parts):
                        v.wait_ge(a_s, 2 * g + half + 1)
                        v.tensor_reduce(m, scores, AX.X, ALU.max).then_inc(a_max, 1)
                    if g >= 2:
                        v.wait_ge(a_t, 2 * (g - 1))
                    for half, (probs, scores, m) in enumerate(parts):
                        v.wait_ge(a_max, 2 * g + half + 1)
                        v.tensor_tensor(probs, scores, m[:, :, None].to_broadcast([P, 8, SEQ]),
                                        ALU.subtract).then_inc(a_sub, 1)

        def attend_pool(gp, A):
            for s in range(A.n + lead_n):
                i = s - 1
                if 0 <= i < A.n:
                    g = A.first + i
                    if A.rope:
                        gp.wait_ge(rope_k, 2)
                    else:
                        gp.wait_ge(a_k, g + 1)
                    if g >= RING_K:
                        gp.wait_ge(a_s, 2 * (g - RING_K + 1))
                    keys = KT[:, P * (g % RING_Q):P * (g % RING_Q) + P].rearrange("p (b k) -> p b k", b=2)
                    shape = [P, 2, POOL_HEADS, SEQ]
                    gp.tensor_tensor(A.keys[:, g % RING_K, :, 0:POOL_HEADS, :], keys[:, :, None, :].to_broadcast(shape),
                                     W("head_rows", 0, POOL_HEADS)[:, None, :, None].to_broadcast(shape), ALU.mult)\
                        .then_inc(a_kbd[0], 1)
                i = s - lead_n
                if 0 <= i < A.n:
                    g = A.first + i
                    gp.wait_ge(a_r, g + 1)
                    at = 1024 * (g % 2)
                    probs = PB[:, at:at + HALF].rearrange("p (h k) -> p h k", h=8)
                    r = rsum[:, 8 * (g % 2):8 * (g % 2) + 8]
                    gp.tensor_tensor(probs, probs, r[:, :, None].to_broadcast([P, 8, SEQ]), ALU.mult)\
                        .then_inc(a_norm[0], 1)

        def l1x_vector(v, o):
            norm_vector(v, o, x_tile, h_tile, 2)
            attend_vector(v, o, cross1)

        def l1x_pool(g, o):
            attend_pool(g, cross1)

        bias_heads = bias1.rearrange("p t h k -> p h t k")

        def position_bias_scalar(a, heads):
            for h in heads:
                ins = a.mul(bias_heads[:, h], ND.rearrange("p (t k) -> p t k", t=TILES),
                            float(np.float32((2.0 ** (-8.0 / HEADS)) ** (h + 1))))
            if HEADS - 1 in heads:
                ins.then_inc(a_sloped, 1)

        def position_mask_pool(g, t):
            g.tensor_tensor(bias1[:, t], bias1[:, t],
                            MADD[:, SEQ * t:SEQ * t + SEQ][:, None, :].to_broadcast([P, HEADS, SEQ]), ALU.add)

        r_h, r_turned, r_relu, r_logits, r_sub, r_exp = (sem("r_h"), sem("r_turned"), sem("r_relu"), sem("r_logits"),
                                                         sem("r_sub"), sem("r_exp"))
        r_gates, r_gt, r_ob, r_ready = sem("r_gates"), sem("r_gt"), sem("r_ob"), sem("r_ready")
        r1 = SCR[:, 0:512]
        r1t = SCR[0:AE_HID, 512:1536]
        lg = SCR[:, 1536:1600]
        lge = SCR[:, 1600:1664]
        msk = SCR[:, 1664:1728]
        m8 = SCR[:, 1728:1792]

        def pick(v, o, logits, n, top, sub_sem, exp_sem, out, buf):
            lt, et, mt = (x.rearrange("p (t e) -> p t e", t=TILES) for x in buf[0:3])
            m8t = buf[3].rearrange("p (t e) -> p t e", t=TILES)
            o.link(v.tensor_copy(lt, logits))
            for t in range(TILES):
                o.mark(v.max(m8t[:, t, :], lt[:, t, :]))
            o.settle()
            o.mark(v.tensor_tensor(mt, lt, m8t[:, :, top - 1:top].to_broadcast([P, TILES, n]), ALU.is_ge))
            v.tensor_tensor(et, lt, m8t[:, :, 0:1].to_broadcast([P, TILES, n]), ALU.subtract).then_inc(sub_sem, 1)
            v.wait_ge(exp_sem, 1)
            o.settle()
            o.link(v.tensor_tensor(mt, mt, et, ALU.mult))
            o.link(v.tensor_reduce(rsum[:, 0:TILES], mt, AX.X, ALU.add))
            o.link(v.reciprocal(rsum[:, TILES:2 * TILES], rsum[:, 0:TILES]))
            return v.tensor_tensor(out, mt, rsum[:, TILES:2 * TILES, None].to_broadcast([P, TILES, n]), ALU.mult)

        def l1f_vector(v, o):
            norm_vector(v, o, x_tile, h_tile, 3, meanwhile=lambda: v.tensor_scalar(
                qb_scaled[:, :], W("e_qb"), SCALE8, None, ALU.mult).then_inc(r_ob, 1))
            v.wait_ge(r_h, 1)
            norm_vector(v, o, lambda t: bank[2][:, AE_HID * t:AE_HID * (t + 1)],
                        lambda t: r1[:, AE_HID * t:AE_HID * (t + 1)], 4)
            v.wait_ge(r_logits, 1)
            gt = GATES[:, :].rearrange("p (t e) -> p t e", t=TILES)
            pick(v, o, bank[3][:, 0:TILES * AE].rearrange("p (t e) -> p t e", t=TILES), AE, 2, r_sub, r_exp, gt,
                 (lg, lge, msk, m8)).then_inc(r_gates, 1)
            v.wait_ge(r_gates, 1)
            attend_vector(v, o, moe)

        def l1f_tensor(pe):
            turn_tensor(pe, h_tile, 3)
            pe.wait_ge(ht_ready, 8)
            four_rows(pe, 2, "rb1", AE_HID, TILES)
            for t in range(TILES):
                ins = pe.matmul(bank[2][:, AE_HID * t:AE_HID * (t + 1)], ht(t), W("r_w1"), start=False,
                                stop=(t == TILES - 1))
            ins.then_inc(r_h, 1)
            for e in range(AE):
                pe.matmul(bank[7][0:AE, 0:P], W("e_vb", AE * e, AE), W("e_o", P * e, P), start=(e == 0), stop=False)
            pe.matmul(bank[7][0:AE, 0:P], W("ident", 0, AE, rows=AE), W("e_ob", rows=AE), start=False, stop=True)\
                .then_inc(r_turned, 1)
            attend_tensor(pe, moe, range(0, 2))
            for t in range(TILES):
                pe.wait_ge(normed, TILES * 4 + t + 1)
                ins = pe.transpose(bank[t // 4][0:AE_HID, P * (t % 4):P * (t % 4) + P],
                                   r1[:, AE_HID * t:AE_HID * (t + 1)], ident)
                if t % 4 == 3:
                    ins.then_inc(r_turned, 1)
            four_rows(pe, 3, "rb2", AE, TILES)
            for t in range(TILES):
                pe.wait_ge(r_relu, t // 4 + 1)
                ins = pe.matmul(bank[3][:, AE * t:AE * (t + 1)], r1t[:, P * t:P * t + P], W("r_w2", rows=AE_HID),
                                start=False, stop=(t == TILES - 1))
            ins.then_inc(r_logits, 1)
            attend_tensor(pe, moe, range(2, 3))
            pe.wait_ge(r_gates, 1)
            pe.wait_ge(r_ready, 1)
            for t in range(TILES):
                ins = pe.transpose(bank[(4, 7)[t // 4]][0:AE, P * (t % 4):P * (t % 4) + P],
                                   GATES[:, AE * t:AE * (t + 1)], ident)
                if t % 4 == 3:
                    ins.then_inc(r_gt, 1)
            attend_tensor(pe, moe, range(3, moe.n + lead_out + 1))

        def l1f_scalar(a):
            norm_scalar(a, 3)
            turn_scalar(a, 3)
            a.wait_ge(r_turned, 1)
            a.copy(OB[0:AE, :], bank[7][0:AE, 0:P]).then_inc(r_ready, 1)
            norm_scalar(a, 4)
            a.wait_ge(r_ob, 1)
            attend_scalar(a, moe, range(0, 2))
            for j in range(2):
                a.wait_ge(r_turned, j + 2)
                a.activation(r1t[:, HALF * j:HALF * j + HALF], bank[j][0:AE_HID, :], ACT.Relu,
                             bias=W("r_b", rows=AE_HID), scale=W("r_g", rows=AE_HID)).then_inc(r_relu, 1)
            a.wait_ge(r_sub, 1)
            a.activation(lge, lge, ACT.Exp).then_inc(r_exp, 1)
            for j in range(2):
                a.wait_ge(r_gt, j + 1)
                a.copy(GT[0:AE, HALF * j:HALF * j + HALF], bank[(4, 7)[j]][0:AE, :]).then_inc(r_ready, 1)
            attend_scalar(a, moe, range(2, moe.n + lead_pv + 1))

        rp, rp_a, rp_b = sem("rp"), sem("rp_a"), sem("rp_b")
        t_cos = SCR[:, 0:1024]
        t_sin = SCR[:, 1024:2048]

        def l2x_tensor(pe):
            for r in range(4):
                src, half = ("k", r) if r < 2 else ("q", r - 2)
                if r == 2:
                    turn_tensor(pe, h_tile, 5)
                    pe.wait_ge(ht_ready, 10)
                if r >= 2:
                    pe.wait_ge(rp_b, r - 1)
                rhs = (CT if src == "k" else HT)[:, HALF * half:HALF * half + HALF]
                pe.matmul(bank[2 + 2 * (r % 2)][:, :], W(f"a2_{src}"), rhs, start=True, stop=True)
                pe.matmul(bank[3 + 2 * (r % 2)][:, :], W(f"a2_{src}p"), rhs, start=True, stop=True).then_inc(rp, 1)
            pe.wait_ge(rp_b, 4)
            attend_tensor(pe, cross2)

        def l2x_vector(v, o):
            norm_vector(v, o, x_tile, h_tile, 5)
            for r in range(4):
                src = "k" if r < 2 else "q"
                v.wait_ge(rp, r + 1)
                if r >= 2:
                    v.wait_ge(rope_k, r - 1)
                at = HALF * (r % 2)
                shape = [P, 8, SEQ]

                def by_batch(x):
                    return x.rearrange("p (b s) -> p b s", b=8)

                o.mark(v.tensor_tensor(by_batch(t_cos[:, at:at + HALF]), by_batch(bank[2 + 2 * (r % 2)][:, :]),
                                       W(f"cos{src}")[:, None, :].to_broadcast(shape), ALU.mult))
                o.settle()
                v.tensor_tensor(by_batch(t_sin[:, at:at + HALF]), by_batch(bank[3 + 2 * (r % 2)][:, :]),
                                W(f"sin{src}")[:, None, :].to_broadcast(shape), ALU.mult).then_inc(rp_b, 1)
            attend_vector(v, o, cross2)

        def l2x_pool(g, o):
            for r in range(4):
                g.wait_ge(rp_b, r + 1)
                at = HALF * (r % 2)
                dst, ready = (KT, rope_k) if r < 2 else (QT, rope_q)
                g.tensor_tensor(dst[:, at:at + HALF], t_cos[:, at:at + HALF], t_sin[:, at:at + HALF], ALU.add)\
                    .then_inc(ready, 1)
            attend_pool(g, cross2)

        f_logits, f_sub, f_exp, f_comb, f_ct, f_ctr = (sem("f_logits"), sem("f_sub"), sem("f_exp"), sem("f_comb"),
                                                       sem("f_ct"), sem("f_ctr"))
        f_h, f_silu, f_gated, f_act, f_out = sem("f_h"), sem("f_silu"), sem("f_gated"), sem("f_act"), sem("f_out")
        act_t = SCR[:, 0:PAIRS * 1024].rearrange("p (e t) -> p e t", e=PAIRS)
        silu = SCR[:, 9216:10240]
        gated = SCR[:, 10240:11264]
        comb = SCR[:, 12288:13312].rearrange("p (t e) -> p t e", t=TILES)
        flg, fle, fmk, fm8 = SCR[:, 13312:13440], SCR[:, 13440:13568], SCR[:, 13568:13696], SCR[:, 13696:13760]

        flg3 = flg.rearrange("p (t e) -> p t e", t=TILES)
        f_part = SCR[:, 13760:13824].bitcast(BF16).rearrange("p (t e) -> p t e", t=TILES)
        comb_b = SCR[:, 11264:11776].bitcast(BF16)
        pick_three = PB[:, 0:HALF].bitcast(BF16)
        f_pick, f_w = sem("f_pick"), sem("f_w")
        def expert_rows_vector(v, o):
            o.mark(v.memset(SCR[:, 12288:13312], 0.0))
            o.settle()
            three = ident[:, 0:3 * 32].rearrange("p (k r) -> p r k", k=3)[:, 0:FE, :]
            o.link(v.tensor_reduce(flg[:, 0:FE], three, AX.X, ALU.add))
            v.tensor_copy(pick_three.rearrange("p (r c) -> p r c", c=SEQ),
                          flg[:, 0:FE, None].to_broadcast([P, FE, SEQ])).then_inc(f_pick, 1)

        def l2f_vector(v, o):
            norm_vector(v, o, x_tile, h_tile, 6, meanwhile=lambda: expert_rows_vector(v, o))
            v.wait_ge(f_pick, 1)
            v.wait_ge(f_logits, 1)
            pick(v, o, bank[2][:, 0:TILES * FE].rearrange("p (t e) -> p t e", t=TILES), FE, FE_TOP, f_sub, f_exp,
                 flg3, (flg, fle, fmk, fm8)).then_inc(f_w, 1)
            v.wait_ge(f_w, 1)
            for k_ in range(2):
                o.link(v.tensor_copy(f_part, flg3))
                o.mark(v.tensor_copy(comb[:, :, 32 * k_:32 * k_ + FE], f_part))
                o.link(v.tensor_tensor(flg3, flg3, f_part, ALU.subtract))
            v.tensor_copy(comb[:, :, 64:64 + FE], flg3).then_inc(f_comb, 1)
            for r in range(2 * PAIRS):
                e, half = r // 2, r % 2
                at = HALF * (r % 2)
                dst = act_t[:, e, HALF * half:HALF * half + HALF]
                shared = e == PAIRS - 1
                v.wait_ge(f_silu, r + 1)
                g_ = dst if shared else gated[:, at:at + HALF]
                ins = v.tensor_tensor(g_, bank[2 + r % 2][:, :], silu[:, at:at + HALF], ALU.mult)
                ins.then_inc(f_gated, 1)
                if not shared:
                    v.wait_ge(f_gated, r + 1)
                    v.tensor_tensor(dst, bank[4 + r % 2][:, :], g_, ALU.mult).then_inc(f_act, 1)
            v.wait_ge(in_ctx, 32)
            norm_vector(v, o, lambda t: Ct[:, t, :], lambda t: h3[:, t, :], 7)
            for j in range(2):
                v.wait_ge(f_out, j + 1)
                add_to_x(v, 5, j, bank[6 + j][:, :])

        def l2f_tensor(pe):
            turn_tensor(pe, h_tile, 6)
            pe.wait_ge(ht_ready, 12)
            for t in range(TILES):
                ins = pe.matmul(bank[2][:, FE * t:FE * (t + 1)], ht(t), W("f_gate"), start=True, stop=True)
            ins.then_inc(f_logits, 1)
            for r in range(2 * PAIRS):
                e, half = r // 2, r % 2
                rhs = HT[:, HALF * half:HALF * half + HALF]
                if r >= 2:
                    pe.wait_ge(f_gated, r - 1)
                pe.matmul(bank[r % 2][:, :], W("f_w1", P * e, P), rhs, start=True, stop=True)
                if r == 0:
                    pe.wait_ge(f_sub, 1)
                pe.matmul(bank[2 + r % 2][:, :], W("f_w3", P * e, P), rhs, start=True, stop=True).then_inc(f_h, 1)
                if r == 1:
                    pe.wait_ge(f_comb, 1)
                    for t in range(TILES):
                        ins = pe.transpose(bank[6 + t // 4][:, P * (t % 4):P * (t % 4) + P], comb[:, t, :], ident)
                        if t % 4 == 3:
                            ins.then_inc(f_ct, 1)
                    pe.wait_ge(f_ctr, 2)
                for r_ in ((0, 1) if r == 1 else (r,) if r > 1 else ()):
                    if r_ // 2 < PAIRS - 1:
                        if r_ >= 2:
                            pe.wait_ge(f_act, r_ - 1)
                        pe.matmul(bank[4 + r_ % 2][:, :], pick_three[:, P * (r_ // 2):P * (r_ // 2) + P],
                                  comb_b[:, HALF * (r_ % 2):HALF * (r_ % 2) + HALF],
                                  start=True, stop=True).then_inc(f_crep, 1)
            pe.wait_ge(f_gated, 2 * PAIRS)
            pe.wait_ge(f_act, 2 * (PAIRS - 1))
            for t in range(TILES):
                for e in range(PAIRS):
                    ins = pe.matmul(bank[6 + t // 4][:, P * (t % 4):P * (t % 4) + P], act_t[:, e, P * t:P * t + P],
                                    W("f_w2", P * e, P), start=(e == 0), stop=(e == PAIRS - 1))
                if t % 4 == 3:
                    ins.then_inc(f_out, 1)

        f_crep = sem("f_crep")

        def l2f_scalar(a):
            norm_scalar(a, 6)
            turn_scalar(a, 5)
            a.wait_ge(f_sub, 1)
            a.activation(fle, fle, ACT.Exp).then_inc(f_exp, 1)
            for j in range(2):
                a.wait_ge(f_ct, j + 1)
                a.copy(comb_b[:, HALF * j:HALF * j + HALF], bank[6 + j][:, :]).then_inc(f_ctr, 1)
            for r in range(2 * PAIRS):
                at = HALF * (r % 2)
                a.wait_ge(f_h, r + 1)
                if r < 2 * (PAIRS - 1):
                    a.wait_ge(f_crep, r + 1)
                if r >= 2:
                    a.wait_ge(f_gated, r - 1)
                a.activation(silu[:, at:at + HALF], bank[r % 2][:, :], ACT.Silu).then_inc(f_silu, 1)
            norm_scalar(a, 7)

        cat_t = SCR[:, 0:2048].rearrange("p (b j) -> p b j", b=BATCH)
        qq = SCR[:, 2048:3072]
        kk = SCR[:, 3072:5120]
        vv = SCR[:, 5120:7200].rearrange("p (b h c) -> p b h c", b=BATCH, h=L_HEADS)
        kt3 = SCR[:, 7200:9248].rearrange("p (b j) -> p b j", b=BATCH)
        pp = SCR[:, 9248:11296]
        ptt = SCR[:, 11296:13344].rearrange("p (h t q) -> p h t q", h=L_HEADS, t=TILES)
        h2 = SCR[:, 13344:14368].rearrange("p (t d) -> p t d", t=TILES)
        h3 = SCR[:, 14368:15392].rearrange("p (t d) -> p t d", t=TILES)
        sq3 = KBD[:, 0:3072]
        ss = KBD[:, 3072:3120]
        ssc = KBD[:, 3120:3168]
        rr = KBD[:, 3168:3216]
        keep = KT[0:2, 0:HALF].bitcast(I32)
        own_rows = VM[0:2, 0:P // 2].bitcast(BF16)
        mask3 = KT[0:2, HALF:2 * HALF].bitcast(BF16).rearrange("p (t j) -> p t j", t=TILES)
        qt3 = (KBD[:, 3584:4608], KBD[:, 7168:8192])
        on3 = KBD[:, 4608:5632]
        ot3 = KBD[:, 5632:6656]
        max3 = KBD[:, 6656:6672]
        inv3 = KBD[:, 6672:6688]
        l_cat, l_q, l_kv, l_qq, l_kk, l_sq, l_rn = (sem("l_cat"), sem("l_q"), sem("l_kv"), sem("l_qq"), sem("l_kk"),
                                                     sem("l_sq"), sem("l_rn"))
        l_inv, l_kn, l_zero = sem("l_inv"), sem("l_kn"), sem("l_zero")
        l_qkn, l_turn, l_qkt, l_s, l_sub, l_exp = (sem("l_qkn"), sem("l_turn"), sem("l_qkt"), sem("l_s"), sem("l_sub"),
                                                   sem("l_exp"))
        l_pt, l_ptt, l_o, l_on, l_ot, l_ots, l_y, l_mask = (sem("l_pt"), sem("l_ptt"), sem("l_o"), sem("l_on"),
                                                            sem("l_ot"), sem("l_ots"), sem("l_y"), sem("l_mask"))

        def latent_mask_vector(v, o):
            o.link(v.memset(mask3, 0.0))
            v.tensor_copy(own_rows, W("own_rows", rows=2)).then_inc(l_mask, 1)
            v.wait_ge(in_keep, 16)
            v.tensor_scalar(mask3[:, :, 0:SEQ], keep.rearrange("p (t k) -> p t k", t=TILES), 0.0, MASKED,
                            ALU.is_equal, ALU.mult).then_inc(l_mask, 1)
            o.mark(v.memset(vv[:, :, :, L_DIM:L_DIM + 1], 1.0))

        def l3x_vector(v, o):
            norm_vector(v, o, x_tile, h_tile, 8, meanwhile=lambda: latent_mask_vector(v, o))
            v.wait_ge(normed, 9 * TILES)
            norm_vector(v, o, h_tile, lambda t: h2[:, t, :], 9)
            v.wait_ge(l_qq, 2)
            o.link(v.tensor_tensor(sq3[:, 0:1024], qq, qq, ALU.mult))
            o.mark(v.tensor_reduce(ss[:, 0:16], sq3[:, 0:1024].rearrange("p (g d) -> p g d", d=L_DIM), AX.X, ALU.add))
            for r in range(8):
                at = 2 * P * r
                v.wait_ge(l_kk, r + 1)
                sq = sq3[:, 1024 + at:1024 + at + 2 * P]
                o.link(v.tensor_tensor(sq, kk[:, at:at + 2 * P], kk[:, at:at + 2 * P], ALU.mult))
                o.mark(v.tensor_reduce(ss[:, 16 + 4 * r:20 + 4 * r], sq.rearrange("p (g d) -> p g d", d=L_DIM), AX.X,
                                       ALU.add))
            o.settle()
            v.tensor_scalar(ssc, ss, 1.0 / L_DIM, 1e-16, ALU.mult, ALU.max).then_inc(l_sq, 1)
            v.wait_ge(l_rn, 2)
            v.reciprocal(rr, rr).then_inc(l_inv, 1)
            v.wait_ge(l_inv, 1)
            for r in range(4):
                x = kk[:, HALF * r:HALF * r + HALF].rearrange("p (g d) -> p g d", d=L_DIM)
                v.tensor_tensor(x, x, rr[:, 16 + 8 * r:24 + 8 * r, None].to_broadcast([P, 8, L_DIM]), ALU.mult)\
                    .then_inc(l_kn, 1)
            l3f_weights_vector(v, o)
            p3 = pp.rearrange("p (h t j) -> p h t j", h=L_HEADS, t=TILES)
            for r in range(4):
                h, part = r % 2, r // 2
                v.wait_ge(l_s, part + 1)
                s3 = bank[r][:, :].rearrange("p (t j) -> p t j", t=4)
                m = max3[:, 4 * r:4 * r + 4]
                o.link(v.tensor_reduce(m, s3, AX.X, ALU.max))
                v.tensor_tensor(p3[:, h, 4 * part:4 * part + 4, :], s3, m[:, :, None].to_broadcast([P, 4, KEYS]),
                                ALU.subtract).then_inc(l_sub, 1)
            for t in range(TILES):
                v.wait_ge(l_o, t // 2 + 1)
                o3 = bank[t // 2][:, 130 * (t % 2):130 * (t % 2) + 130].rearrange("p (h c) -> p h c", h=L_HEADS)
                r_ = inv3[:, 2 * t:2 * t + 2]
                o.link(v.reciprocal(r_, o3[:, :, L_DIM]))
                v.tensor_tensor(on3[:, P * t:P * t + P].rearrange("p (h d) -> p h d", h=L_HEADS), o3[:, :, 0:L_DIM],
                                r_[:, :, None].to_broadcast([P, L_HEADS, L_DIM]), ALU.mult).then_inc(l_on, 1)
            for j in range(2):
                v.wait_ge(l_y, j + 1)
                add_to_x(v, 6, j, bank[6 + j][:, :])

        def l3x_pool(g, o):
            g.memset(qt3[0][L_DIM:P, :], 0.0).then_inc(l_zero, 1)
            g.wait_ge(l_zero, 1)
            g.memset(qt3[1][0:L_DIM, :], 0.0).then_inc(l_zero, 1)
            g.wait_ge(l_zero, 2)
            g.wait_ge(l_inv, 1)
            x = qq.rearrange("p (g d) -> p g d", d=L_DIM)
            g.tensor_tensor(x, x, rr[:, 0:16, None].to_broadcast([P, 16, L_DIM]), ALU.mult).then_inc(l_qkn, 1)

        def l3x_tensor(pe):
            for n, src in ((7, h3), (9, h2)):
                turn_tensor(pe, lambda t, s_=src: s_[:, t, :], n, banks=(0, 1) if n == 9 else (2, 3))
                if n == 7:
                    l3f_weights_tensor(pe)
            pe.wait_ge(l_cat, 4)
            pe.wait_ge(b_kept, 3)
            for t in range(TILES):
                for b in range(2):
                    ins = pe.matmul(bank[t // 4][SEQ * b:SEQ * b + SEQ, P * (t % 4):P * (t % 4) + P],
                                    cat_t[:, 2 * t + b, SEQ:KEYS], W("l3_q"), start=True, stop=True)
                if t % 4 == 3:
                    ins.then_inc(l_q, 1)
            for b in range(BATCH):
                r = b // 2
                if b % 2 == 0 and r >= 4:
                    pe.wait_ge(l_kk, r - 3)
                ins = pe.matmul(bank[4 + r % 4][:, 2 * P * (b % 2):2 * P * (b % 2) + 2 * P], cat_t[:, b, :],
                                W("l3_kv"), start=True, stop=True)
                if b % 2 == 1:
                    ins.then_inc(l_kv, 1)
            for r in range(6):
                if r == 0:
                    pe.wait_ge(l_qkn, 1)
                if r >= 2:
                    pe.wait_ge(l_kn, r - 1)
                src = qq if r < 2 else kk
                for j in range(4):
                    at = P * (4 * (r if r < 2 else r - 2) + j)
                    ins = pe.transpose(bank[r][:, P * j:P * j + P], src[:, at:at + P], ident)
                ins.then_inc(l_turn, 1)
            pe.wait_ge(l_qkt, 6)
            pe.wait_ge(l_mask, 2)
            pe.wait_ge(l_zero, 2)
            for part in range(2):
                for h in range(L_HEADS):
                    out = bank[2 * part + h]
                    pe.matmul(out[:, :], own_rows, mask3[:, 4 * part:4 * part + 4, :].rearrange("p t j -> p (t j)"),
                              start=True, stop=False)
                    for t in range(4 * part, 4 * part + 4):
                        for b in range(2):
                            ins = pe.matmul(out[SEQ * b:SEQ * b + SEQ, KEYS * (t % 4):KEYS * (t % 4) + KEYS],
                                            qt3[h][:, P * t + SEQ * b:P * t + SEQ * b + SEQ],
                                            kt3[:, 2 * t + b, :], start=False, stop=(t % 4 == 3))
                ins.then_inc(l_s, 1)
            for r in range(4):
                h, part = r % 2, r // 2
                pe.wait_ge(l_exp, r + 1)
                for j in range(4):
                    at = 1024 * h + HALF * part + P * j
                    ins = pe.transpose(bank[4 + r][:, P * j:P * j + P], pp[:, at:at + P], ident)
                ins.then_inc(l_pt, 1)
            pe.wait_ge(l_ptt, 4)
            for t in range(TILES):
                for h in range(L_HEADS):
                    for b in range(2):
                        at = 130 * (t % 2) + 65 * h
                        ins = pe.matmul(bank[t // 2][SEQ * b:SEQ * b + SEQ, at:at + 65],
                                        ptt[:, h, t, SEQ * b:SEQ * b + SEQ], vv[:, 2 * t + b, h, :],
                                        start=True, stop=True)
                if t % 2 == 1:
                    ins.then_inc(l_o, 1)
            for t in range(TILES):
                pe.wait_ge(l_on, t + 1)
                ins = pe.transpose(bank[4 + t // 4][:, P * (t % 4):P * (t % 4) + P], on3[:, P * t:P * t + P], ident)
                if t % 4 == 3:
                    ins.then_inc(l_ot, 1)
            four_rows(pe, 6, "b3")
            four_rows(pe, 7, "b3")
            for t in range(TILES):
                pe.wait_ge(l_ots, t // 4 + 1)
                ins = pe.matmul(bank[6 + t // 4][:, P * (t % 4):P * (t % 4) + P], ot3[:, P * t:P * t + P], W("l3_o"),
                                start=False, stop=(t % 4 == 3))
                if t % 4 == 3:
                    ins.then_inc(l_y, 1)

        def l3x_scalar(a):
            a.activation(wabs, W("b_fc"), ACT.Abs).then_inc(b_abs, 1)
            a.activation(pabs, W("b_proj"), ACT.Abs).then_inc(b_abs, 1)
            norm_scalar(a, 8)
            for n in (1, 0):
                for j in range(2):
                    a.wait_ge(turned, 2 * (7 - n) + j + 1)
                    g_, b_ = (W("l_g"), W("l_b")) if n == 0 else (W("x_g"), W("x_b"))
                    dst = cat_t[:, 8 * j:8 * j + 8, SEQ * (1 - n):SEQ * (2 - n)]
                    a.activation(dst, bank[2 * n + j][:, :].rearrange("p (b s) -> p b s", b=8), ACT.Identity,
                                 bias=b_, scale=g_).then_inc(l_cat, 1)
                if n == 1:
                    l3f_weights_scalar(a)
            for j in range(2):
                a.wait_ge(l_q, j + 1)
                a.copy(qq[:, HALF * j:HALF * j + HALF], bank[j][:, :]).then_inc(l_qq, 1)
            for r in range(8):
                a.wait_ge(l_kv, r + 1)
                src = bank[4 + r % 4][:, :].rearrange("p (b c) -> p b c", b=2)
                a.copy(vv[:, 2 * r:2 * r + 2, :, 0:L_DIM],
                       src[:, :, P:2 * P].rearrange("p b (h d) -> p b h d", h=L_HEADS))
                a.copy(kk[:, 2 * P * r:2 * P * r + 2 * P].rearrange("p (b c) -> p b c", b=2), src[:, :, 0:P])\
                    .then_inc(l_kk, 1)
            a.wait_ge(l_sq, 1)
            a.activation(rr[:, 0:16], ssc[:, 0:16], ACT.Sqrt, scale=float(L_DIM)).then_inc(l_rn, 1)
            a.activation(rr[:, 16:48], ssc[:, 16:48], ACT.Sqrt).then_inc(l_rn, 1)
            for r in range(6):
                a.wait_ge(l_turn, r + 1)
                if r < 2:
                    for h in range(L_HEADS):
                        rows = slice(L_DIM * h, L_DIM * h + L_DIM)
                        ins = a.mul(qt3[h][rows, HALF * r:HALF * r + HALF], bank[r][rows, :],
                                    W("q_gamma")[rows])
                    ins.then_inc(l_qkt, 1)
                else:
                    a.mul(SCR[:, 7200 + HALF * (r - 2):7200 + HALF * (r - 1)], bank[r][:, :], W("k_gamma"))\
                        .then_inc(l_qkt, 1)
            for r in range(4):
                h, part = r % 2, r // 2
                at = 1024 * h + HALF * part
                a.wait_ge(l_sub, r + 1)
                a.activation(pp[:, at:at + HALF], pp[:, at:at + HALF], ACT.Exp).then_inc(l_exp, 1)
            for r in range(4):
                h, part = r % 2, r // 2
                a.wait_ge(l_pt, r + 1)
                a.copy(ptt[:, h, 4 * part:4 * part + 4, :].rearrange("p t q -> p (t q)"), bank[4 + r][:, :])\
                    .then_inc(l_ptt, 1)
            for j in range(2):
                a.wait_ge(l_ot, j + 1)
                a.copy(ot3[:, HALF * j:HALF * j + HALF], bank[4 + j][:, :]).then_inc(l_ots, 1)

        b_abs, b_sum = sem("b_abs"), sem("b_sum")
        b_t1, b_t1s, b_m, b_w, b_h, b_relu, b_r2, b_y = (sem("b_t1"), sem("b_t1s"), sem("b_m"), sem("b_w"), sem("b_h"),
                                                         sem("b_relu"), sem("b_r2"), sem("b_y"))
        b_sum2, b_kept = sem("b_sum2"), sem("b_kept")
        weff, peff = W("b_fc"), W("b_proj")
        wabs, pabs = PTB[:, 0:512], PTB[:, 512:1024]
        t1 = PTB[0:RANK, 1024:1536]
        fast = PTB[:, 1536:2048]
        wsum = PB[:, 0:512]
        whalf = PB[:, 512:1024]
        wneg = PB[:, 1024:1536]
        psum = PB[:, 1536:1664]
        phalf = PB[:, 1664:1792]
        pneg = H[:, 0:512]
        rl = SCR[:, 5120:6144]
        r2 = SCR[:, 6144:10240].rearrange("p (c t) -> p c t", c=CHUNKS)

        def l3f_weights_vector(v, o):
            def ternary(w, total, n, scale, half, neg, out, shape=None):
                def s(x):
                    return x if shape is None else x[:, None, :].to_broadcast(shape)
                o.link(v.tensor_scalar(scale, total, 1.0 / n, 1e-5, ALU.mult, ALU.max))
                o.link(v.tensor_scalar(half, scale, -0.5, None, ALU.mult))
                o.link(v.tensor_tensor(neg, w, s(half), ALU.is_lt))
                o.link(v.tensor_scalar(half, scale, 0.5, None, ALU.mult))
                o.link(v.tensor_tensor(out, w, s(half), ALU.is_gt))
                o.link(v.tensor_tensor(out, out, neg, ALU.subtract))
                return v.tensor_tensor(out, out, s(scale), ALU.mult)

            shape = [P, CHUNKS, P]

            def by_chunk(x):
                return x.rearrange("p (c d) -> p c d", c=CHUNKS)

            v.wait_ge(b_kept, 2)
            o.link(ternary(W("b_fc"), wsum, P, wsum, whalf, wneg, weff))
            ternary(by_chunk(W("b_proj")), psum, HIDDEN, psum, phalf, by_chunk(pneg), by_chunk(peff), shape)\
                .then_inc(b_w, 1)
            v.wait_ge(b_kept, 3)
            v.scalar_tensor_tensor(weff, fast, W("b_gate"), weff, ALU.mult, ALU.add).then_inc(b_w, 1)

        def l3f_vector(v, o):
            norm_vector(v, o, x_tile, h_tile, 10)
            for r in range(2 * CHUNKS):
                c, half = r // 2, r % 2
                at = HALF * (r % 2)
                v.wait_ge(b_relu, r + 1)
                v.tensor_tensor(r2[:, c, HALF * half:HALF * half + HALF], rl[:, at:at + HALF], rl[:, at:at + HALF],
                                ALU.mult).then_inc(b_r2, 1)
            for j in range(2):
                v.wait_ge(b_y, j + 1)
                add_to_x(v, 7, j, bank[6 + j][:, :]).then_inc(final_x, 1)

        final_x = sem("final_x")

        def l3f_weights_tensor(pe):
            pe.wait_ge(b_abs, 1)
            pe.matmul(bank[4][:, :], W("ones"), wabs, start=True, stop=True).then_inc(b_sum, 1)
            pe.matmul(bank[6][0:RANK, :], W("b_fb", rows=RANK), W("b_ut", rows=RANK), start=True, stop=True)\
                .then_inc(b_t1, 1)
            pe.wait_ge(b_abs, 2)
            for c in range(CHUNKS):
                ins = pe.matmul(bank[5][:, 0:P], W("ones"), pabs[:, P * c:P * c + P], start=(c == 0), stop=(c == 3))
            ins.then_inc(b_sum2, 1)
            pe.wait_ge(b_t1s, 1)
            pe.matmul(bank[7][:, :], W("b_v", rows=RANK), t1, start=True, stop=True).then_inc(b_m, 1)

        def l3f_tensor(pe):
            turn_tensor(pe, h_tile, 10)
            for r in range(2 * CHUNKS):
                c, half = r // 2, r % 2
                pe.wait_ge(ht_ready, 12 + half + 1)
                if r >= 2:
                    pe.wait_ge(b_relu, r - 1)
                out = bank[(2, 3)[r % 2]]
                pe.matmul(out[:, :], weff[:, P * c:P * c + P], HT[:, HALF * half:HALF * half + HALF],
                          start=True, stop=True).then_inc(b_h, 1)
            pe.wait_ge(b_r2, 2 * CHUNKS)
            for t in range(TILES):
                for c in range(CHUNKS):
                    ins = pe.matmul(bank[6 + t // 4][:, P * (t % 4):P * (t % 4) + P], r2[:, c, P * t:P * t + P],
                                    peff[:, P * c:P * c + P], start=(c == 0), stop=(c == CHUNKS - 1))
                if t % 4 == 3:
                    ins.then_inc(b_y, 1)

        def l3f_weights_scalar(a):
            a.wait_ge(b_t1, 1)
            a.copy(t1, bank[6][0:RANK, :]).then_inc(b_t1s, 1)
            a.wait_ge(b_sum, 1)
            a.copy(wsum, bank[4][:, :]).then_inc(b_kept, 1)
            a.wait_ge(b_sum2, 1)
            a.copy(psum, bank[5][:, 0:P]).then_inc(b_kept, 1)
            norm_scalar(a, 9)
            a.wait_ge(b_m, 1)
            a.copy(fast, bank[7][:, :]).then_inc(b_kept, 1)

        def l3f_scalar(a):
            norm_scalar(a, 10)
            turn_scalar(a, 8)
            for r in range(2 * CHUNKS):
                at = HALF * (r % 2)
                a.wait_ge(b_h, r + 1)
                if r >= 2:
                    a.wait_ge(b_r2, r - 1)
                a.activation(rl[:, at:at + HALF], bank[(2, 3)[r % 2]][:, :], ACT.Relu).then_inc(b_relu, 1)

        cross1.ht_need, moe.ht_need, cross2.ht_need = 4, 6, 8

        block = ctx.enter_context(nc.Block())

        @block.sync
        def _(sp):
            ends = [0] + group_ends()

            def load_pack(g):
                sp.dma_start(pack[:, ends[g]:ends[g + 1]], d_pack[:, ends[g]:ends[g + 1]]).then_inc(in_pack[g], 16)

            sp.dma_start(Xt, d_x.rearrange("(t p) d -> p t d", p=P)).then_inc(in_x, 16)
            load_pack(0)
            sp.dma_start(CT[:, :], d_ctxt).then_inc(in_ctx, 16)
            sp.dma_start(gates_in[:, :], d_gates).then_inc(in_gates, 16)
            load_pack(1)
            sp.dma_start(qpos[:, :], d_qpos).then_inc(in_small, 16)
            sp.dma_start(kpos[:, :], d_kpos).then_inc(in_small, 16)
            sp.dma_start(mask[:, :], d_mask).then_inc(in_small, 16)
            for g in range(2, len(GROUPS)):
                load_pack(g)
            for k in range(8):
                if k == 5:
                    sp.dma_start(keep, d_keep).then_inc(in_keep, 16)
                    sp.dma_start(Ct, d_ctx.rearrange("(t p) d -> p t d", p=P)).then_inc(in_ctx, 16)
                if k == 7:
                    for j in range(2):
                        sp.wait_ge(final_x, j + 1)
                        sp.dma_start(d_out.rearrange("(t p) d -> p t d", p=P)[:, 4 * j:4 * j + 4],
                                     Xt[:, 4 * j:4 * j + 4]).then_inc(out_stored, 16)
                for g in first_use.get(k + 1, ()):
                    sp.wait_ge(in_pack[g], 16)
                end_layer(sp, k)
            sp.wait_ge(out_stored, 32)

        @block.gpsimd
        def _(g):
            o = Order(g, "pool")
            for k in range(8):
                if k == 0:
                    g.memset(VM[:, :], 0.0).then_inc(zeroed, 1)
                elif k == 1:
                    l0f_pool(g, o)
                elif k == 2:
                    l1x_pool(g, o)
                elif k == 3:
                    attend_pool(g, moe)
                elif k == 4:
                    l2x_pool(g, o)
                elif k == 6:
                    l3x_pool(g, o)
                end_layer(g, k)

        @block.scalar
        def _(a):
            for k in range(8):
                if k == 0:
                    a.wait_ge(in_pack[0], 16)
                    norm_scalar(a, 0)
                    turn_scalar(a, 0)
                    a.wait_ge(in_gates, 16)
                    a.activation(gate[:, :], gates_in[:, :], ACT.Tanh).then_inc(gate_ready, 1)
                elif k == 1:
                    norm_scalar(a, 1)
                    turn_scalar(a, 1)
                    l0f_scalar(a)
                elif k == 2:
                    norm_scalar(a, 2)
                    turn_scalar(a, 2)
                    attend_scalar(a, cross1)
                elif k == 3:
                    l1f_scalar(a)
                elif k == 4:
                    norm_scalar(a, 5)
                    turn_scalar(a, 4)
                    attend_scalar(a, cross2)
                elif k == 5:
                    l2f_scalar(a)
                elif k == 6:
                    l3x_scalar(a)
                elif k == 7:
                    l3f_scalar(a)
                end_layer(a, k)

        @block.tensor
        def _(pe):
            for k in range(8):
                if k == 0:
                    l0x_tensor(pe)
                elif k == 1:
                    turn_tensor(pe, h_tile, 1)
                    l0f_tensor(pe)
                elif k == 2:
                    turn_tensor(pe, h_tile, 2)
                    attend_tensor(pe, cross1)
                elif k == 3:
                    l1f_tensor(pe)
                elif k == 4:
                    l2x_tensor(pe)
                elif k == 5:
                    l2f_tensor(pe)
                elif k == 6:
                    l3x_tensor(pe)
                elif k == 7:
                    l3f_tensor(pe)
                end_layer(pe, k)

        @block.vector
        def _(v):
            o = Order(v, "vector")
            for k in range(8):
                if k == 0:
                    l0x_vector(v, o)
                elif k == 1:
                    l0f_vector(v, o)
                elif k == 2:
                    l1x_vector(v, o)
                elif k == 3:
                    l1f_vector(v, o)
                elif k == 4:
                    l2x_vector(v, o)
                elif k == 5:
                    l2f_vector(v, o)
                elif k == 6:
                    l3x_vector(v, o)
                elif k == 7:
                    l3f_vector(v, o)
                end_layer(v, k)


def lay_out(i):
    f = {k: np.asarray(v) for k, v in i.items()}
    blocks = {}

    def put(name, a, rows=P):
        a = np.asarray(a, np.float32) if a.dtype == np.float32 else a
        full = np.zeros((P, OFFSET[name][1]), np.float32)
        full[0:a.shape[0], 0:a.shape[1]] = a
        blocks[name] = full

    def col(a):
        return a.reshape(-1, 1)

    put("ident", np.eye(P, dtype=np.float32))
    put("w1t", f["L0_xattn_W"][:, :DIM].T)
    put("w2t", f["L0_xattn_W"][:, DIM:].T)
    put("eps", np.full((P, 1), EPS, np.float32))
    put("ones", np.ones((P, P), np.float32))
    rows = np.zeros((1, 5 * P), np.float32)
    rows[0, 0:P] = f["L0_xattn_b"]
    rows[0, P:2 * P] = f["L3_xattn_b_out"]
    rows[0, 2 * P:2 * P + AE_HID] = f["L1_ffn_rb1"]
    rows[0, 3 * P:3 * P + AE] = f["L1_ffn_rb2"]
    put("rows", rows)
    put("pk_wq", f["L0_ffn_Wq"])
    put("pk_bq", f["L0_ffn_bq"].reshape(2, P).T)
    put("pk_gamma", col(np.concatenate([f["L0_ffn_bn_gamma"]] * 4)))
    put("pk_beta", col(np.concatenate([f["L0_ffn_bn_beta"]] * 4)))
    keys = np.zeros((4, 2, 16, 4, 2, PK_KEYS), np.float32)
    group = np.zeros((4, 2, 16, 4, 2), np.float32)
    for h in range(4):
        for c, k in enumerate((f["L0_ffn_sub_key0"], f["L0_ffn_sub_key1"])):
            keys[h, c, :, h, c, :] = k.T
            group[h, c, :, h, c] = 1.0
    put("pk_keys", keys.reshape(P, 2 * P))
    put("pk_group", group.reshape(P, 8))
    same = np.equal.outer(np.arange(P) % 32, np.arange(P) % 32)
    put("pk_mean", np.where(same, np.float32(1.0 / PK_HEADS), np.float32(0.0)))
    put("pk_down", f["L0_ffn_expert_down"].T)
    put("pk_up", f["L0_ffn_expert_up"])
    for n, k in (("a1_q", "W_q"), ("a1_k", "W_k"), ("a1_v", "W_v"), ("a1_o", "W_o")):
        put(n, f["L1_xattn_" + k].T)
    put("head_rows", np.equal.outer(np.arange(P) // HEAD_DIM, np.arange(HEADS)).astype(np.float32))
    put("r_w1", f["L1_ffn_rW1"].T)
    put("r_g", col(f["L1_ffn_ln_g"]))
    put("r_b", col(f["L1_ffn_ln_b"]))
    put("r_w2", f["L1_ffn_rW2"].T)
    put("e_qb", f["L1_ffn_qb"].T)
    put("e_kb", f["L1_ffn_kb"].T)
    vb = np.zeros((P, AE, AE), np.float32)
    for e in range(AE):
        vb[:, e, e] = f["L1_ffn_vb"][e]
    put("e_vb", vb.reshape(P, AE * AE))
    put("e_ob", f["L1_ffn_ob"])
    for n, k in (("e_q", "qW"), ("e_k", "kW"), ("e_v", "vW"), ("e_o", "oW")):
        put(n, f["L1_ffn_" + k].transpose(2, 0, 1).reshape(P, AE * P))
    turn = np.arange(P).reshape(HEADS, 2, HEAD_DIM // 2)[:, ::-1].reshape(P)
    for n, k in (("q", "Wq"), ("k", "Wk")):
        w = f["L2_xattn_" + k]
        put("a2_" + n, w.T)
        put("a2_" + n + "p", w[turn].T)
    put("a2_v", f["L2_xattn_Wv"].T)
    put("a2_o", f["L2_xattn_Wo"].T)
    freq = 1.0 / 10000.0 ** (np.arange(0, HEAD_DIM, 2, dtype=np.float32) / np.float32(HEAD_DIM))
    angle = np.outer(np.arange(SEQ, dtype=np.float32), freq.astype(np.float32)).astype(np.float32)
    cos = np.tile(np.cos(angle).T, (2 * HEADS, 1))
    sin = np.sin(angle).T
    sin = np.tile(np.concatenate([-sin, sin]), (HEADS, 1))
    put("cosq", (cos * SCALE8).astype(np.float32))
    put("sinq", (sin * SCALE8).astype(np.float32))
    put("cosk", cos.astype(np.float32))
    put("sink", sin.astype(np.float32))
    put("f_gate", f["L2_ffn_gate_w"].T)
    for n, k in (("f_w1", "w1"), ("f_w3", "w3")):
        full = np.zeros((P, 2 * PAIRS, FE_HID), np.float32)
        full[:, 0:FE] = f["L2_ffn_" + k].transpose(2, 0, 1)
        full[:, FE] = f["L2_ffn_s" + k].T
        put(n, full.reshape(P, PAIRS * P))
    full = np.zeros((2, FE_HID, PAIRS, P), np.float32)
    full[:, :, 0:FE // 2] = f["L2_ffn_w2"].transpose(0, 2, 1).reshape(FE // 2, 2, FE_HID, P).transpose(1, 2, 0, 3)
    full[0, :, FE // 2] = f["L2_ffn_sw2"].T
    put("f_w2", full.reshape(P, PAIRS * P))
    for n, k in (("x_g", "ln_x_g"), ("x_b", "ln_x_b"), ("l_g", "ln_l_g"), ("l_b", "ln_l_b")):
        put(n, col(f["L3_xattn_" + k]))
    for n in ("q_gamma", "k_gamma"):
        put(n, col(np.concatenate([f["L3_xattn_" + n]] * L_HEADS)))
    put("own_rows", np.equal.outer(np.arange(2), np.arange(P) // SEQ).astype(np.float32))
    put("l3_q", f["L3_xattn_W_q"])
    put("l3_kv", f["L3_xattn_W_kv"])
    put("l3_o", f["L3_xattn_W_out"])
    put("b_fc", f["L3_ffn_w_fc"].T)
    put("b_proj", f["L3_ffn_w_proj"].T.reshape(CHUNKS, P, P).transpose(1, 0, 2).reshape(P, CHUNKS * P))
    put("b_v", f["L3_ffn_v"])
    put("b_ut", f["L3_ffn_u"].T)
    put("b_fb", f["L3_ffn_fast_b"])
    put("b_gate", np.repeat(f["L3_ffn_gate"].reshape(1, 1), P, axis=0))

    context = f["ctx_1024"].reshape(TOKENS, DIM)
    gates = np.stack([f["g_xattn"], f["g_ffn"]], axis=1).reshape(1, 8)
    kpos = np.repeat(f["itok_BxS2_1_8191"][:, None, :], SEQ, axis=1)

    def by_tile(a):
        return np.ascontiguousarray(a.reshape(TILES, P, -1).transpose(1, 0, 2).reshape(P, -1))

    return {
        "x": np.ascontiguousarray(f["x"].reshape(TOKENS, DIM)),
        "ctx": np.ascontiguousarray(context),
        "ctxt": np.ascontiguousarray(context.T),
        "pack": np.concatenate([blocks[n] for n, _ in PACK], axis=1),
        "gates": np.ascontiguousarray(np.repeat(gates, P, axis=0)),
        "qpos": by_tile(f["itok_BxS_8_8191"].astype(np.int32)),
        "kpos": by_tile(kpos.astype(np.int32)),
        "mask": by_tile(f["mask_BxSxS2_if1"].astype(np.int32)),
        "keep": np.ascontiguousarray(f["mask_BxS2_bk0"].astype(np.int32).reshape(TILES, 2, SEQ).transpose(1, 0, 2)
                                     .reshape(2, TILES * SEQ)),
    }


def kernel(**inputs):
    import concourse.bacc as _bacc
    from concourse.bass_utils import run_bass_kernel_spmd as _run

    nc = _bacc.Bacc("TRN2", target_bir_lowering=False, num_devices=1)
    arrays = {f"in_{name}": a for name, a in lay_out(inputs).items()}
    args = [nc.dram_tensor(name, a.shape, mybir.dt.from_np(a.dtype), kind="ExternalInput").ap()
            for name, a in arrays.items()]
    out = nc.dram_tensor("out", (TOKENS, DIM), F32, kind="ExternalOutput").ap()
    build(nc, *args, out)
    r = _run(nc, [arrays], core_ids=[0])
    return r.results[0]["out"].reshape(BATCH, SEQ, DIM)
```
